# Optimizing a Trainium2 kernel written in Bass

```python
import numpy as np
import jax
import jax.numpy as jnp

def _softmax(x, axis=-1):
    return jax.nn.softmax(x, axis=axis)

def _gelu(x):
    return jax.nn.gelu(x, approximate=True)

def _silu(x):
    return jax.nn.silu(x)

def _sigmoid(x):
    return jax.nn.sigmoid(x)

def _layernorm(x, axis=-1, eps=1e-05):
    m = jnp.mean(x, axis=axis, keepdims=True)
    v = jnp.var(x, axis=axis, keepdims=True)
    return (x - m) / jnp.sqrt(v + eps)

def _scatter_add(tgt, idx, src, axis=0):
    return tgt.at[idx].add(src)

def _segment_sum(src, seg, n):
    return jax.ops.segment_sum(src, seg, n)
kernel_name = 'mk_conv_preact_d2_conv_nchw8_r2_1a1ac5'

def setup_inputs(seed: int=0):
    np.random.seed(seed)
    _w = jnp.asarray

    def _rec_inputs():
        import jax
        import jax.numpy as jnp
        _gk = jax.random.key(seed)
        x = 7.22e-05 + 1 * jax.random.normal(jax.random.fold_in(_gk, 1), (2, 8, 256, 512), jnp.float32)
        return x
    x = _rec_inputs()

    def _L0_conv_setup():
        import jax, jax.numpy as jnp
        import numpy as np
        import math
        B, C, F, W = (2, 8, 256, 512)
        HEADS = 8

        def _mcl(x, Wm, b):
            return jnp.einsum('bcgw,cfg->bcfw', x, Wm) + b[None, :, :, None]

        def _conv(x, w, b, pad):
            y = jax.lax.conv_general_dilated(x, w, window_strides=(1, 1), padding=[(0, 0), (pad, pad)], dimension_numbers=('NCHW', 'OIHW', 'NCHW'))
            return y + b[None, :, None, None]

        def _rope(t):
            d = t.shape[-1]
            seq = t.shape[-2]
            inv_freq = 1.0 / 10000.0 ** (jnp.arange(0, d, 2, dtype=jnp.float32) / d)
            freqs = jnp.arange(seq, dtype=jnp.float32)[:, None] * inv_freq[None, :]
            emb = jnp.repeat(freqs, 2, axis=-1)
            cos, sin = (jnp.cos(emb), jnp.sin(emb))
            tp = t.reshape(t.shape[:-1] + (d // 2, 2))
            rot = jnp.stack([-tp[..., 1], tp[..., 0]], axis=-1).reshape(t.shape)
            return t * cos.astype(t.dtype) + rot * sin.astype(t.dtype)
        key = jax.random.key(seed)
        ks = jax.random.split(key, 18)
        s = 0.02
        d = {'x': jax.random.normal(ks[0], (B, C, F, W), dtype=jnp.float32)}
        names = ['q', 'k', 'v', 'o']
        for i, n in enumerate(names):
            d['W' + n] = jax.random.normal(ks[1 + 4 * i], (C, F, F), dtype=jnp.float32) * s
            d['b' + n] = jnp.zeros((C, F), dtype=jnp.float32)
            kw = 7 if n != 'o' else 1
            d[n + '_conv_w'] = jax.random.normal(ks[2 + 4 * i], (C, C, 1, kw), dtype=jnp.float32) * s
            d[n + '_conv_b'] = jnp.zeros((C,), dtype=jnp.float32)
        return d
    _L0_conv_all = _L0_conv_setup()
    _L0_conv_in = {k: v for k, v in _L0_conv_all.items() if k in ('Wq', 'bq', 'q_conv_w', 'q_conv_b', 'Wk', 'bk', 'k_conv_w', 'k_conv_b', 'Wv', 'bv', 'v_conv_w', 'v_conv_b', 'Wo', 'bo', 'o_conv_w', 'o_conv_b')}
    del _L0_conv_all

    def _L1_conv_setup():
        import jax, jax.numpy as jnp
        import numpy as np
        PI = np.float32(np.pi)

        def compute_maps(height, width, ky, kx, stride=1, dilation=1):
            az = jnp.linspace(-1.0 + 1.0 / width, 1.0 - 1.0 / width, width, dtype=jnp.float32) * PI
            po = jnp.linspace(1.0 / (2 * height), 1.0 - 1.0 / (2 * height), height, dtype=jnp.float32) * PI
            azimuth, polar = jnp.meshgrid(az[::stride], po[::stride], indexing='xy')
            h, w = azimuth.shape
            sin_a, cos_a = (jnp.sin(azimuth), jnp.cos(azimuth))
            sin_p, cos_p = (jnp.sin(polar), jnp.cos(polar))
            axis_z = jnp.stack([sin_p * sin_a, -cos_p, sin_p * cos_a], axis=-1)
            axis_x = jnp.stack([cos_a, jnp.zeros_like(azimuth), -sin_a], axis=-1)
            axis_y = jnp.stack([cos_p * sin_a, sin_p, cos_p * cos_a], axis=-1)
            xv = jnp.arange(kx, dtype=jnp.float32) - kx // 2
            yv = jnp.arange(ky, dtype=jnp.float32) - ky // 2
            xx, yy = jnp.meshgrid(xv, yv, indexing='xy')
            scale = jnp.float32(dilation) * PI / height
            xyz = axis_z[:, :, None, None, :] + axis_x[:, :, None, None, :] * (xx * scale)[None, None, :, :, None] + axis_y[:, :, None, None, :] * (yy * scale)[None, None, :, :, None]
            xyz = xyz.reshape(h, w, ky * kx, 3)
            polar_s = jnp.arctan2(jnp.sqrt(xyz[..., 0] ** 2 + xyz[..., 2] ** 2), -xyz[..., 1])
            azim_s = jnp.arctan2(xyz[..., 0], xyz[..., 2])
            x_coords = (azim_s + PI) / (2 * PI) * width - 0.5
            y_coords = polar_s / PI * height - 0.5
            return (x_coords, y_coords)

        def bilinear_sample(x, gx, gy):
            B, C, H, W = x.shape
            x0f = jnp.floor(gx)
            y0f = jnp.floor(gy)
            wx = gx - x0f
            wy = gy - y0f
            x0 = x0f.astype(jnp.int32)
            y0 = y0f.astype(jnp.int32)
            x1 = x0 + 1
            y1 = y0 + 1
            x0 = jnp.mod(x0, W)
            x1 = jnp.mod(x1, W)
            y0 = jnp.clip(y0, 0, H - 1)
            y1 = jnp.clip(y1, 0, H - 1)
            xf = x.reshape(B, C, H * W)

            def gather(yi, xi):
                idx = (yi * W + xi).reshape(-1)
                return xf[:, :, idx].reshape(B, C, *yi.shape)
            v = gather(y0, x0) * ((1 - wx) * (1 - wy)) + gather(y0, x1) * (wx * (1 - wy)) + gather(y1, x0) * ((1 - wx) * wy) + gather(y1, x1) * (wx * wy)
            return v
        key = jax.random.key(seed)
        k1, k2, k3 = jax.random.split(key, 3)
        B, C, H, W = (2, 8, 256, 512)
        out_c, ky, kx = (8, 3, 3)
        x = jax.random.normal(k1, (B, C, H, W), dtype=jnp.float32)
        weight = jax.random.normal(k2, (out_c, C, ky, kx), dtype=jnp.float32) * 0.1
        bias = jax.random.normal(k3, (out_c,), dtype=jnp.float32) * 0.05
        return {'x': x, 'weight': weight, 'bias': bias}
    _L1_conv_all = _L1_conv_setup()
    _L1_conv_in = {k: v for k, v in _L1_conv_all.items() if k in ('weight', 'bias')}
    del _L1_conv_all
    return {'x': x, 'L0_conv_Wq': _L0_conv_in['Wq'], 'L0_conv_bq': _L0_conv_in['bq'], 'L0_conv_q_conv_w': _L0_conv_in['q_conv_w'], 'L0_conv_q_conv_b': _L0_conv_in['q_conv_b'], 'L0_conv_Wk': _L0_conv_in['Wk'], 'L0_conv_bk': _L0_conv_in['bk'], 'L0_conv_k_conv_w': _L0_conv_in['k_conv_w'], 'L0_conv_k_conv_b': _L0_conv_in['k_conv_b'], 'L0_conv_Wv': _L0_conv_in['Wv'], 'L0_conv_bv': _L0_conv_in['bv'], 'L0_conv_v_conv_w': _L0_conv_in['v_conv_w'], 'L0_conv_v_conv_b': _L0_conv_in['v_conv_b'], 'L0_conv_Wo': _L0_conv_in['Wo'], 'L0_conv_bo': _L0_conv_in['bo'], 'L0_conv_o_conv_w': _L0_conv_in['o_conv_w'], 'L0_conv_o_conv_b': _L0_conv_in['o_conv_b'], 'L1_conv_weight': _L1_conv_in['weight'], 'L1_conv_bias': _L1_conv_in['bias']}

def reference(x, L0_conv_Wq, L0_conv_bq, L0_conv_q_conv_w, L0_conv_q_conv_b, L0_conv_Wk, L0_conv_bk, L0_conv_k_conv_w, L0_conv_k_conv_b, L0_conv_Wv, L0_conv_bv, L0_conv_v_conv_w, L0_conv_v_conv_b, L0_conv_Wo, L0_conv_bo, L0_conv_o_conv_w, L0_conv_o_conv_b, L1_conv_weight, L1_conv_bias):
    import jax
    import jax.numpy as jnp

    def _L0_conv_ref(x, Wq, bq, q_conv_w, q_conv_b, Wk, bk, k_conv_w, k_conv_b, Wv, bv, v_conv_w, v_conv_b, Wo, bo, o_conv_w, o_conv_b):
        import jax, jax.numpy as jnp
        import numpy as np
        import math
        B, C, F, W = (2, 8, 256, 512)
        HEADS = 8

        def _mcl(x, Wm, b):
            return jnp.einsum('bcgw,cfg->bcfw', x, Wm) + b[None, :, :, None]

        def _conv(x, w, b, pad):
            y = jax.lax.conv_general_dilated(x, w, window_strides=(1, 1), padding=[(0, 0), (pad, pad)], dimension_numbers=('NCHW', 'OIHW', 'NCHW'))
            return y + b[None, :, None, None]

        def _rope(t):
            d = t.shape[-1]
            seq = t.shape[-2]
            inv_freq = 1.0 / 10000.0 ** (jnp.arange(0, d, 2, dtype=jnp.float32) / d)
            freqs = jnp.arange(seq, dtype=jnp.float32)[:, None] * inv_freq[None, :]
            emb = jnp.repeat(freqs, 2, axis=-1)
            cos, sin = (jnp.cos(emb), jnp.sin(emb))
            tp = t.reshape(t.shape[:-1] + (d // 2, 2))
            rot = jnp.stack([-tp[..., 1], tp[..., 0]], axis=-1).reshape(t.shape)
            return t * cos.astype(t.dtype) + rot * sin.astype(t.dtype)
        b, c, h, w = x.shape
        dh = h // HEADS

        def split_heads(y):
            return y.transpose(0, 1, 3, 2).reshape(b, c, w, HEADS, dh).transpose(0, 1, 3, 2, 4)
        q = _rope(split_heads(_conv(_mcl(x, Wq, bq), q_conv_w, q_conv_b, 3)))
        k = _rope(split_heads(_conv(_mcl(x, Wk, bk), k_conv_w, k_conv_b, 3)))
        v = split_heads(_conv(_mcl(x, Wv, bv), v_conv_w, v_conv_b, 3))
        qk = jnp.einsum('bceqd,bcekd->bceqk', q.astype(jnp.float32), k.astype(jnp.float32)) / math.sqrt(h)
        a = jax.nn.softmax(qk, axis=-1)
        o = jnp.einsum('bceqk,bcekd->bceqd', a, v.astype(jnp.float32))
        o = o.transpose(0, 1, 3, 2, 4).reshape(b, c, w, h).transpose(0, 1, 3, 2)
        return _conv(_mcl(o, Wo, bo), o_conv_w, o_conv_b, 0)

    def _L1_conv_ref(x, weight, bias):
        import jax, jax.numpy as jnp
        import numpy as np
        PI = np.float32(np.pi)

        def compute_maps(height, width, ky, kx, stride=1, dilation=1):
            az = jnp.linspace(-1.0 + 1.0 / width, 1.0 - 1.0 / width, width, dtype=jnp.float32) * PI
            po = jnp.linspace(1.0 / (2 * height), 1.0 - 1.0 / (2 * height), height, dtype=jnp.float32) * PI
            azimuth, polar = jnp.meshgrid(az[::stride], po[::stride], indexing='xy')
            h, w = azimuth.shape
            sin_a, cos_a = (jnp.sin(azimuth), jnp.cos(azimuth))
            sin_p, cos_p = (jnp.sin(polar), jnp.cos(polar))
            axis_z = jnp.stack([sin_p * sin_a, -cos_p, sin_p * cos_a], axis=-1)
            axis_x = jnp.stack([cos_a, jnp.zeros_like(azimuth), -sin_a], axis=-1)
            axis_y = jnp.stack([cos_p * sin_a, sin_p, cos_p * cos_a], axis=-1)
            xv = jnp.arange(kx, dtype=jnp.float32) - kx // 2
            yv = jnp.arange(ky, dtype=jnp.float32) - ky // 2
            xx, yy = jnp.meshgrid(xv, yv, indexing='xy')
            scale = jnp.float32(dilation) * PI / height
            xyz = axis_z[:, :, None, None, :] + axis_x[:, :, None, None, :] * (xx * scale)[None, None, :, :, None] + axis_y[:, :, None, None, :] * (yy * scale)[None, None, :, :, None]
            xyz = xyz.reshape(h, w, ky * kx, 3)
            polar_s = jnp.arctan2(jnp.sqrt(xyz[..., 0] ** 2 + xyz[..., 2] ** 2), -xyz[..., 1])
            azim_s = jnp.arctan2(xyz[..., 0], xyz[..., 2])
            x_coords = (azim_s + PI) / (2 * PI) * width - 0.5
            y_coords = polar_s / PI * height - 0.5
            return (x_coords, y_coords)

        def bilinear_sample(x, gx, gy):
            B, C, H, W = x.shape
            x0f = jnp.floor(gx)
            y0f = jnp.floor(gy)
            wx = gx - x0f
            wy = gy - y0f
            x0 = x0f.astype(jnp.int32)
            y0 = y0f.astype(jnp.int32)
            x1 = x0 + 1
            y1 = y0 + 1
            x0 = jnp.mod(x0, W)
            x1 = jnp.mod(x1, W)
            y0 = jnp.clip(y0, 0, H - 1)
            y1 = jnp.clip(y1, 0, H - 1)
            xf = x.reshape(B, C, H * W)

            def gather(yi, xi):
                idx = (yi * W + xi).reshape(-1)
                return xf[:, :, idx].reshape(B, C, *yi.shape)
            v = gather(y0, x0) * ((1 - wx) * (1 - wy)) + gather(y0, x1) * (wx * (1 - wy)) + gather(y1, x0) * ((1 - wx) * wy) + gather(y1, x1) * (wx * wy)
            return v
        out_c, in_c, ky, kx = weight.shape
        H, W = (x.shape[-2], x.shape[-1])
        gx, gy = compute_maps(H, W, ky, kx, stride=1, dilation=1)
        v = bilinear_sample(x, gx, gy)
        w = weight.reshape(out_c, in_c, ky * kx)
        y = jnp.einsum('bchwk,ock->bohw', v, w) + bias[None, :, None, None]
        return y

    def _gn(v, G=4, eps=1e-05):
        B_, C_, H_, W_ = v.shape
        g = v.reshape(B_, G, C_ // G, H_, W_)
        m = jnp.mean(g, axis=(2, 3, 4), keepdims=True)
        s = jnp.var(g, axis=(2, 3, 4), keepdims=True)
        return ((g - m) / jnp.sqrt(s + eps)).reshape(v.shape)

    def _ln_c(v, eps=1e-06):
        m = jnp.mean(v, axis=1, keepdims=True)
        s = jnp.var(v, axis=1, keepdims=True)
        return (v - m) / jnp.sqrt(s + eps)

    def _ln_t(v, eps=1e-05):
        m = jnp.mean(v, axis=-1, keepdims=True)
        s = jnp.var(v, axis=-1, keepdims=True)
        return (v - m) / jnp.sqrt(s + eps)

    def _to_tokens(v):
        B_, C_, H_, W_ = v.shape
        return v.reshape(B_, C_, H_ * W_).transpose(0, 2, 1)

    def _from_tokens(t, like):
        B_, C_, H_, W_ = like.shape
        return t.transpose(0, 2, 1).reshape(B_, C_, H_, W_)
    x = x + _L0_conv_ref(_gn(x), L0_conv_Wq, L0_conv_bq, L0_conv_q_conv_w, L0_conv_q_conv_b, L0_conv_Wk, L0_conv_bk, L0_conv_k_conv_w, L0_conv_k_conv_b, L0_conv_Wv, L0_conv_bv, L0_conv_v_conv_w, L0_conv_v_conv_b, L0_conv_Wo, L0_conv_bo, L0_conv_o_conv_w, L0_conv_o_conv_b)
    x = x + _L1_conv_ref(_gn(x), L1_conv_weight, L1_conv_bias)
    return x

_drawn_inputs = setup_inputs


def setup_inputs(seed=0):
    import zlib

    import numpy as np

    out = dict(_drawn_inputs(seed))
    spreads = {'L0_conv_bq': (0.0, 0.8),
     'L0_conv_q_conv_b': (0.0, 0.8),
     'L0_conv_bk': (0.0, 0.8),
     'L0_conv_k_conv_b': (0.0, 0.8),
     'L0_conv_bv': (0.0, 0.8),
     'L0_conv_v_conv_b': (0.0, 0.8),
     'L0_conv_bo': (0.0, 0.8),
     'L0_conv_o_conv_b': (0.0, 0.1)}
    factors = {'L0_conv_Wq': 8.0,
     'L0_conv_q_conv_w': 8.0,
     'L0_conv_Wk': 8.0,
     'L0_conv_k_conv_w': 8.0,
     'L0_conv_Wv': 8.0,
     'L0_conv_v_conv_w': 8.0,
     'L0_conv_Wo': 8.0,
     'L0_conv_o_conv_w': 8.0,
     'L1_conv_bias': 3.633}
    for name, (base, spread) in spreads.items():
        noise = np.random.default_rng([zlib.crc32(name.encode()), seed]).standard_normal(out[name].shape)
        drawn = base * np.exp(spread * noise) if base else spread * noise
        out[name] = jnp.asarray(drawn.astype(out[name].dtype))
    for name, factor in factors.items():
        out[name] = (out[name] * factor).astype(out[name].dtype)
    return out
```

```python
import math
from contextlib import ExitStack

import numpy as np

import concourse.bass as bass
from concourse import mybir

FP32 = mybir.dt.float32
BF16 = mybir.dt.bfloat16
ALU = mybir.AluOpType
ACT = mybir.ActivationFunctionType
AX = mybir.AxisListType

B, C, F, W = 2, 8, 256, 512
P = 128
HEADS = 8
DH = F // HEADS
GROUPS = 4
CPG = C // GROUPS
FH = F // P
QKV = 3 * F
TAPS = 7
PAD = TAPS // 2

KW = P // C
OW = KW - TAPS + 1
WINDOWS = -(-W // OW)
WIN_UNROLL = 4
WPAD = WINDOWS * OW
YROWS = WPAD + 2 * PAD

KR = P // C
OR = KR - 3
BLOCKS = -(-F // OR)


def sphere_taps():
    polar = np.linspace(1.0 / (2 * F), 1.0 - 1.0 / (2 * F), F) * np.pi
    sin_p, cos_p = np.sin(polar), np.cos(polar)
    scale = np.pi / F
    taps = [dict() for _ in range(F)]
    for ky in range(3):
        for kx in range(3):
            dx, dy = (kx - 1) * scale, (ky - 1) * scale
            radial, height = sin_p + cos_p * dy, -cos_p + sin_p * dy
            shift = np.arctan2(dx, radial) / (2 * np.pi) * W
            row = np.arctan2(np.sqrt(radial ** 2 + dx ** 2), -height) / np.pi * F - 0.5
            for h in range(F):
                y0, x0 = int(np.floor(row[h])), int(np.floor(shift[h]))
                wy, wx = row[h] - y0, shift[h] - x0
                for yy, cy in ((y0, 1 - wy), (y0 + 1, wy)):
                    for xx, cx in ((x0, 1 - wx), (x0 + 1, wx)):
                        at = taps[h].setdefault((min(max(yy, 0), F - 1), xx), {})
                        at[(ky, kx)] = at.get((ky, kx), 0.0) + cy * cx
    return taps


def sphere_plan():
    taps = sphere_taps()
    blocks, entries = [], []
    for i in range(BLOCKS):
        h0, n = OR * i, min(OR, F - OR * i)
        used = [(h, at, k) for h in range(h0, h0 + n) for at, k in taps[h].items()]
        r0 = min(min(at[0] for _, at, _ in used), F - KR)
        assert max(at[0] for _, at, _ in used) < r0 + KR
        shifts = sorted({at[1] for _, at, _ in used})
        blocks.append((h0, n, r0, shifts, len(entries)))
        for s in shifts:
            coef = np.zeros((3, 3, KR, OR))
            for h, (r, sh), k in used:
                if sh == s:
                    for (ky, kx), v in k.items():
                        coef[kx, ky, r - r0, h - h0] += v
            entries.append(coef)
    e = np.stack(entries, 3)
    side = e[[0, 2]].reshape(2 * 3 * KR, -1)
    centre = e[1].reshape(3 * KR, -1)
    return blocks, np.concatenate([side, np.zeros((P - 6 * KR, side.shape[1]))]).astype(np.float32), \
        np.concatenate([centre, np.zeros((P - 3 * KR, side.shape[1]))]).astype(np.float32)


SPHERE_BLOCKS, SPHERE_SIDE, SPHERE_CENTRE = sphere_plan()
ENTRIES = SPHERE_SIDE.shape[1] // OR
CHUNK = 36
CHUNKS = -(-ENTRIES // CHUNK)
SPHERE_SIDE, SPHERE_CENTRE = (np.pad(a, ((0, 0), (0, (CHUNKS * CHUNK - ENTRIES) * OR))) for a in (SPHERE_SIDE, SPHERE_CENTRE))


def sphere_runs():
    runs = []
    for i, (h0, n, r0, shifts, _) in enumerate(SPHERE_BLOCKS):
        j = runs[-1][0] if runs else None
        if runs and (n, h0 - r0, shifts) == (SPHERE_BLOCKS[j][1], SPHERE_BLOCKS[j][0] - SPHERE_BLOCKS[j][2], SPHERE_BLOCKS[j][3]):
            runs[-1] = (j, runs[-1][1] + 1)
        else:
            runs.append((i, 1))
    return runs


SPHERE_RUNS = sphere_runs()
MAX_SHIFT = max(max(abs(s) for s in blk[3]) for blk in SPHERE_BLOCKS)
PAD_L = max(-min(min(blk[3]) for blk in SPHERE_BLOCKS), 0)
PAD_R = max(max(blk[3]) for blk in SPHERE_BLOCKS)
XROW = PAD_L + W + PAD_R


def rope_tables():
    inv = (np.float32(1.0) / np.float32(10000.0) ** (np.arange(0, DH, 2, dtype=np.float32) / np.float32(DH))).astype(np.float32)
    angle = (np.arange(W, dtype=np.float32)[:, None] * inv[None, :]).astype(np.float32)
    cos = np.repeat(np.cos(angle.astype(np.float64)), 2, -1).T
    sin = np.repeat(np.sin(angle.astype(np.float64)), 2, -1).T
    sin = sin * np.where(np.arange(DH) % 2 == 0, -1.0, 1.0)[:, None]
    scale = 1.0 / math.sqrt(F)
    out = [np.tile(np.stack([t * scale, t], 1), (P // DH, 1, 1)).astype(np.float32) for t in (cos, sin)]
    return out


def constants():
    cos, sin = rope_tables()
    part = np.arange(P)
    same_group = (part[:, None] % C // CPG == part[None, :] % C // CPG) / float(P // C * CPG)
    slot = np.zeros((P, KR), np.float32)
    slot[part, part % KR] = 1.0
    return {
        "ident": np.eye(P, dtype=np.float32),
        "cos": cos, "sin": sin,
        "same_group": same_group.astype(np.float32),
        "slot": slot,
        "side": SPHERE_SIDE, "centre": SPHERE_CENTRE,
    }


def allocators(nc, ctx):
    def sb(name, shape, dt=FP32):
        return ctx.enter_context(nc.sbuf_tensor(name, shape, dt))

    def ps(name, shape):
        return ctx.enter_context(nc.psum_tensor(name, shape, FP32))

    def sem(name):
        return ctx.enter_context(nc.semaphore(name))

    return sb, ps, sem


def primed(engine, sems):
    for s in sems:
        engine.sem_inc(s, 1)


def project(nc, T, Y):
    with ExitStack() as ctx:
        sb, ps, sem = allocators(nc, ctx)
        GT = CPG * FH
        x = sb("p_x", [P, B * C * FH, W])
        xh = sb("p_xh", [P, B * C * FH, W], BF16)
        xl = sb("p_xl", [P, B * C * FH, W], BF16)
        stats = sb("p_stats", [P, B * GROUPS, GT * 6])
        mv = sb("p_mv", [P, B * GROUPS, 2])
        mean = sb("p_mean", [P, B * GROUPS])
        dev = sb("p_dev", [P, B * GROUPS])
        dev2 = sb("p_dev2", [P, B * GROUPS])
        var = sb("p_var", [P, B * GROUPS])
        vare = sb("p_vare", [P, B * GROUPS])
        std = sb("p_std", [P, B * GROUPS])
        rstd = sb("p_rstd", [P, B * GROUPS])
        shift = sb("p_shift", [P, B * GROUPS])
        ones = sb("p_ones", [P, P])
        zero = sb("p_zero", [2 * PAD * C, QKV])
        w = [sb(f"p_w{s}", [P, FH, QKV]) for s in range(2)]
        wh = [sb(f"p_wh{s}", [P, FH, QKV], BF16) for s in range(2)]
        wl = [sb(f"p_wl{s}", [P, FH, QKV], BF16) for s in range(2)]
        bias = [sb(f"p_bias{s}", [P, 2, QKV // 2]) for s in range(2)]
        WT = W // P
        y = [sb(f"p_y{s}", [P, 2, QKV // 2]) for s in range(WT)]
        acc = [ps(f"p_acc{s}", [P, 2, 512]) for s in range(WT)]

        x_in = [sem(f"p_x_in{k}") for k in range(B * GROUPS)]
        w_in = [sem(f"p_w_in{s}") for s in range(2)]
        bias_in = [sem(f"p_bias_in{s}") for s in range(2)]
        w_split = sem("p_w_split")
        wh_done = sem("p_wh_done")
        ones_set = sem("p_ones_set")
        zero_set = sem("p_zero_set")
        zero_out = sem("p_zero_out")
        tile_stats = sem("p_tile_stats")
        group_stats = sem("p_group_stats")
        stat_sums = sem("p_stat_sums")
        dve = sem("p_dve")
        std_ready = sem("p_std_ready")
        normed = sem("p_normed")
        x_hi = sem("p_x_hi")
        x_lo = sem("p_x_lo")
        acc_full = [sem(f"p_acc_full{s}") for s in range(2)]
        y_ready = [sem(f"p_y_ready{s}") for s in range(WT)]
        y_out = [sem(f"p_y_out{s}") for s in range(WT)]
        ORDER = [(b, g) for g in range(GROUPS) for b in range(B)]

        block = ctx.enter_context(nc.Block())

        @block.sync
        def _(sp):
            primed(sp, y_out)
            for k, (b, g) in enumerate(ORDER):
                t0 = (b * C + g * CPG) * FH
                sp.dma_start(x[:, t0:t0 + GT, :],
                             T["x"][b, g * CPG:(g + 1) * CPG].rearrange("c (f p) w -> p (c f) w", p=P)).then_inc(x_in[k], 16)
            sp.wait_ge(zero_set, 1)
            for b in range(B):
                sp.dma_start(Y[b, 0:PAD].rearrange("w c f -> (w c) f"), zero[0:PAD * C]).then_inc(zero_out, 16)
                for r0 in range(PAD + W, YROWS, 2 * PAD):
                    n = min(2 * PAD, YROWS - r0)
                    sp.dma_start(Y[b, r0:r0 + n].rearrange("w c f -> (w c) f"), zero[0:n * C]).then_inc(zero_out, 16)
            with sp.Fori(0, C // 2) as i:
                for cc in range(2):
                    for b in range(B):
                        for t in range(WT):
                            sp.wait_ge(y_ready[t], 1 + (i * 2 + cc) * B + b + 1)
                            sp.dma_start(Y[b, PAD + t * P:PAD + (t + 1) * P, bass.ds(i * 2 + cc, 1)].rearrange("w a f -> w (a f)"),
                                         y[t][:].rearrange("p a n -> p (a n)")).then_inc(y_out[t], 16)
            for t in range(WT):
                sp.wait_ge(y_out[t], 1 + 16 * B * C)
            sp.wait_ge(zero_out, 16 * B * (1 + len(range(PAD + W, YROWS, 2 * PAD))))

        @block.scalar
        def _(act):
            for cc in range(2):
                act.dma_start(w[cc][:], T["w_qkv"][cc].rearrange("(h p) n -> p h n", p=P)).then_inc(w_in[cc], 16)
                act.dma_start(bias[cc][:], T["b_qkv"][cc:cc + 1].rearrange("a (h n) -> a h n", h=2)
                              .broadcast_to([P, 2, QKV // 2])).then_inc(bias_in[cc], 16)
            act.wait_ge(dve, 3)
            nc.scalar.activation(std[:], vare[:], ACT.Sqrt).then_inc(std_ready, 1)
            for k, (b, g) in enumerate(ORDER):
                t0 = (b * C + g * CPG) * FH
                act.wait_ge(normed, k + 1)
                nc.scalar.activation(xh[:, t0:t0 + GT, :], x[:, t0:t0 + GT, :], ACT.Copy).then_inc(x_hi, 1)
            def high_part(i, cc):
                act.wait_ge(w_in[cc], 16 * (i + 1))
                act.wait_ge(acc_full[cc], 1 + i * B * WT)
                nc.scalar.activation(wh[cc][:], w[cc][:], ACT.Copy).then_inc(wh_done, 1)

            for cc in range(2):
                high_part(0, cc)
            with act.Fori(1, C // 2) as i:
                for cc in range(2):
                    act.wait_ge(w_split, 2 * i + cc - 1)
                    act.dma_start(w[cc][:], T["w_qkv"][bass.ds(2 * i + cc, 1)].rearrange("a (h p) n -> p (a h) n", p=P)).then_inc(w_in[cc], 16)
                    act.wait_ge(y_ready[WT - 1], 1 + B * (2 * i + cc - 1))
                    act.dma_start(bias[cc][:], T["b_qkv"][bass.ds(2 * i + cc, 1)].rearrange("a (h n) -> a h n", h=2)
                                  .broadcast_to([P, 2, QKV // 2])).then_inc(bias_in[cc], 16)
                    high_part(i, cc)

        @block.gpsimd
        def _(pool):
            nc.gpsimd.memset(ones[:], 1.0 / P).then_inc(ones_set, 1)
            nc.gpsimd.memset(zero[:], 0.0).then_inc(zero_set, 1)
            with pool.Fori(0, C // 2) as i:
                for cc in range(2):
                    pool.wait_ge(wh_done, 2 * i + cc + 1)
                    nc.gpsimd.tensor_tensor(wl[cc][:], w[cc][:], wh[cc][:], ALU.subtract).then_inc(w_split, 1)

        @block.vector
        def _(v):
            primed(v, y_ready)
            for k, (b, g) in enumerate(ORDER):
                t0 = (b * C + g * CPG) * FH
                v.wait_ge(x_in[k], 16)
                for t in range(GT):
                    nc.vector.bn_stats(stats[:, b * GROUPS + g, 6 * t:6 * t + 6], x[:, t0 + t, :]).then_inc(tile_stats, 1)
            v.wait_ge(tile_stats, B * GROUPS * GT)
            for k in range(B * GROUPS):
                nc.vector.bn_aggr(mv[:, k, :], stats[:, k, :]).then_inc(group_stats, 1)
            v.wait_ge(stat_sums, 1)
            nc.vector.tensor_copy(mean[:], acc[WT - 1][:, 0, 0:B * GROUPS]).then_inc(dve, 1)
            nc.vector.tensor_tensor(dev[:], mv[:, :, 0], acc[WT - 1][:, 0, 0:B * GROUPS], ALU.subtract).then_inc(group_stats, 1)
            v.wait_ge(group_stats, B * GROUPS + 1)
            nc.vector.tensor_tensor(dev2[:], dev[:], dev[:], ALU.mult).then_inc(group_stats, 1)
            v.wait_ge(stat_sums, 2)
            nc.vector.tensor_copy(var[:], acc[WT - 1][:, 0, B * GROUPS:2 * B * GROUPS]).then_inc(dve, 1)
            v.wait_ge(dve, 2)
            nc.vector.tensor_scalar(vare[:], var[:], 1e-5, None, ALU.add).then_inc(dve, 1)
            v.wait_ge(std_ready, 1)
            nc.vector.reciprocal(rstd[:], std[:]).then_inc(dve, 1)
            v.wait_ge(dve, 4)
            nc.vector.scalar_tensor_tensor(shift[:], mean[:], -1.0, rstd[:], ALU.mult, ALU.mult).then_inc(dve, 1)
            v.wait_ge(dve, 5)
            for k, (b, g) in enumerate(ORDER):
                t0, kg = (b * C + g * CPG) * FH, b * GROUPS + g
                nc.vector.tensor_scalar(x[:, t0:t0 + GT, :], x[:, t0:t0 + GT, :], rstd[:, kg:kg + 1], shift[:, kg:kg + 1],
                                        ALU.mult, ALU.add).then_inc(normed, 1)
            for k, (b, g) in enumerate(ORDER):
                t0 = (b * C + g * CPG) * FH
                v.wait_ge(x_hi, k + 1)
                nc.vector.tensor_tensor(xl[:, t0:t0 + GT, :], x[:, t0:t0 + GT, :], xh[:, t0:t0 + GT, :], ALU.subtract).then_inc(x_lo, 1)
            with v.Fori(0, C // 2) as i:
                for cc in range(2):
                    v.wait_ge(bias_in[cc], 16 * (i + 1))
                    for b in range(B):
                        for t in range(WT):
                            n = (i * 2 + cc) * B + b
                            v.wait_ge(acc_full[cc], 1 + (i * B + b) * WT + t + 1)
                            v.wait_ge(y_out[t], 1 + 16 * n)
                            nc.vector.tensor_tensor(y[t][:], acc[t][:, :, 0:QKV // 2], bias[cc][:], ALU.add).then_inc(y_ready[t], 1)

        @block.tensor
        def _(pe):
            primed(pe, acc_full)
            pe.wait_ge(ones_set, 1)
            pe.wait_ge(group_stats, B * GROUPS)
            nc.tensor.matmul(acc[WT - 1][:, 0, 0:B * GROUPS], ones[:], mv[:, :, 0], start=True, stop=True)
            nc.tensor.matmul(acc[WT - 1][:, 0, B * GROUPS:2 * B * GROUPS], ones[:], mv[:, :, 1], start=True, stop=False).then_inc(stat_sums, 1)
            pe.wait_ge(group_stats, B * GROUPS + 2)
            nc.tensor.matmul(acc[WT - 1][:, 0, B * GROUPS:2 * B * GROUPS], ones[:], dev2[:], start=False, stop=True).then_inc(stat_sums, 1)
            with pe.Fori(0, C // 2) as i:
                for cc in range(2):
                    pe.wait_ge(w_split, 2 * i + cc + 1)
                    for b in range(B):
                        pe.wait_ge(x_lo, i * 2 + b + 1)
                        for t in range(WT):
                            n = (i * 2 + cc) * B + b
                            pe.wait_ge(y_ready[t], 1 + n)
                            for half in range(2):
                                cols = slice(half * (QKV // 2), (half + 1) * (QKV // 2))
                                for fh in range(FH):
                                    tile = bass.ds(i * (2 * FH) + (b * C + cc) * FH + fh, 1)
                                    hi = xh[:, tile, t * P:(t + 1) * P].rearrange("p a n -> p (a n)")
                                    lo = xl[:, tile, t * P:(t + 1) * P].rearrange("p a n -> p (a n)")
                                    out = acc[t][:, half, 0:QKV // 2]
                                    nc.tensor.matmul(out, hi, wh[cc][:, fh, cols], start=fh == 0, stop=False)
                                    nc.tensor.matmul(out, hi, wl[cc][:, fh, cols], start=False, stop=False)
                                    last = nc.tensor.matmul(out, lo, wh[cc][:, fh, cols], start=False, stop=fh == FH - 1)
                            last.then_inc(acc_full[cc], 1)


def convolve(nc, T, Y, QK, V):
    with ExitStack() as ctx:
        sb, ps, sem = allocators(nc, ctx)
        KF = 2 * FH
        band = sb("c_band", [P, 3, C * OW])
        qk = sb("c_qk", [P, KF, C, WPAD])
        qk_bias = sb("c_qk_bias", [P, 2, FH, C])
        v_bias = sb("c_v_bias", [C * OW, 1])
        cos = sb("c_cos", [P, 2, W])
        sin = sb("c_sin", [P, 2, W])
        win = [sb(f"c_win{s}", [P, QKV]) for s in range(WIN_UNROLL)]
        vout = [sb(f"c_v{s}", [C * OW, F]) for s in range(WIN_UNROLL)]
        turned = [sb(f"c_turned{s}", [P, KF, W]) for s in range(2)]
        hi = [sb(f"c_hi{s}", [P, KF, W], BF16) for s in range(2)]
        lo = [sb(f"c_lo{s}", [P, KF, W], BF16) for s in range(2)]
        acc_qk = [ps(f"c_acc_qk{s}", [P, 512]) for s in range(WIN_UNROLL)]
        acc_v = [ps(f"c_acc_v{s}", [P, 512]) for s in range(WIN_UNROLL)]

        band_zero = sem("c_band_zero")
        consts_in = sem("c_consts_in")
        win_in = [sem(f"c_win_in{s}") for s in range(WIN_UNROLL)]
        acc_full = [sem(f"c_acc_full{s}") for s in range(WIN_UNROLL)]
        qk_read = [sem(f"c_qk_read{s}") for s in range(WIN_UNROLL)]
        v_read = [sem(f"c_v_read{s}") for s in range(WIN_UNROLL)]
        v_stored = [sem(f"c_v_stored{s}") for s in range(WIN_UNROLL)]
        turn_done = sem("c_turn_done")
        sin_done = sem("c_sin_done")
        cos_done = sem("c_cos_done")
        rope_done = sem("c_rope_done")
        hi_done = sem("c_hi_done")
        lo_done = sem("c_lo_done")
        hi_stored = [sem(f"c_hi_stored{s}") for s in range(2)]
        lo_stored = [sem(f"c_lo_stored{s}") for s in range(2)]
        TURNS = WINDOWS // WIN_UNROLL
        NCONST = KW + 2 * FH + 1 + 2
        block = ctx.enter_context(nc.Block())

        @block.sync
        def _(sp):
            for w in range(KW):
                sp.dma_start(band[w * C:(w + 1) * C].rearrange("c k (o w) -> c (k o) w", w=OW),
                             T["taps"][:, :, KW - 1 - w:KW - 1 - w + OW]).then_inc(consts_in, 16)
            for kind in range(2):
                for fh in range(FH):
                    sp.dma_start(qk_bias[:, kind, fh, :],
                                 T["qkv_conv_b"][kind:kind + 1].broadcast_to([P, C])).then_inc(consts_in, 16)
            sp.dma_start(v_bias[:],
                         T["qkv_conv_b"][2].rearrange("(o w a) -> o w a", w=1, a=1).broadcast_to([C, OW, 1])).then_inc(consts_in, 16)
            sp.dma_start(cos[:], T["cos"]).then_inc(consts_in, 16)
            sp.dma_start(sin[:], T["sin"]).then_inc(consts_in, 16)
            for b in range(B):
                with sp.Fori(0, WINDOWS // WIN_UNROLL) as i:
                    for s in range(WIN_UNROLL):
                        sp.wait_ge(acc_full[s], 1 + b * TURNS + i)
                        sp.dma_start(win[s][:], Y[b, bass.ds((i * WIN_UNROLL + s) * OW, KW)].rearrange("w c f -> (w c) f")
                                     ).then_inc(win_in[s], 16)

        @block.tensor
        def _(pe):
            primed(pe, acc_full)
            pe.wait_ge(consts_in, 16 * NCONST)
            for b in range(B):
                with pe.Fori(0, WINDOWS // WIN_UNROLL) as i:
                    for s in range(WIN_UNROLL):
                        pe.wait_ge(win_in[s], 16 * (b * TURNS + i + 1))
                        pe.wait_ge(qk_read[s], 1 + b * TURNS + i)
                        pe.wait_ge(v_read[s], 1 + b * TURNS + i)
                        for kf in range(KF):
                            nc.tensor.matmul(acc_qk[s][:, kf * C * OW:(kf + 1) * C * OW], win[s][:, kf * P:(kf + 1) * P],
                                             band[:, kf // FH, :], start=True, stop=True)
                        nc.tensor.matmul(acc_v[s][0:C * OW, 0:F], band[:, 2, :], win[s][:, 2 * F:3 * F],
                                         start=True, stop=True).then_inc(acc_full[s], 1)

        @block.vector
        def _(v):
            primed(v, qk_read)
            v.wait_ge(consts_in, 16 * NCONST)
            for b in range(B):
                if b:
                    v.wait_ge(lo_done, b * C)
                with v.Fori(0, WINDOWS // WIN_UNROLL) as i:
                    for s in range(WIN_UNROLL):
                        v.wait_ge(acc_full[s], 1 + b * TURNS + i + 1)
                        w0 = (i * WIN_UNROLL + s) * OW
                        nc.vector.tensor_tensor(
                            qk[:, :, :, bass.ds(w0, OW)].rearrange("p a o w -> p (a o) w"),
                            acc_qk[s][:, 0:KF * C * OW].rearrange("p (a w) -> p a w", w=OW),
                            qk_bias[:].rearrange("p k f (o w) -> p (k f o) w", w=1).broadcast_to([P, KF * C, OW]),
                            ALU.add).then_inc(qk_read[s], 1)
                for s in range(WIN_UNROLL):
                    v.wait_ge(qk_read[s], 1 + (b + 1) * TURNS)
                for o in range(C):
                    n = b * C + o
                    if n >= 2:
                        v.wait_ge(rope_done, n - 1)
                    nc.vector.stream_shuffle(turned[n % 2][:], qk[:, :, o, 0:W], [d ^ 1 for d in range(32)]).then_inc(turn_done, 1)
                    v.wait_ge(sin_done, n + 1)
                    v.wait_ge(cos_done, n + 1)
                    nc.vector.tensor_tensor(qk[:, :, o, 0:W], qk[:, :, o, 0:W], turned[n % 2][:], ALU.add).then_inc(rope_done, 1)
                    v.wait_ge(hi_done, n + 1)
                    if n >= 2:
                        v.wait_ge(lo_stored[n % 2], 16 * (n // 2))
                    nc.vector.tensor_tensor(lo[n % 2][:], qk[:, :, o, 0:W], hi[n % 2][:], ALU.subtract).then_inc(lo_done, 1)

        @block.gpsimd
        def _(pool):
            for b in range(B):
                for o in range(C):
                    n = b * C + o
                    tab = [t[:].rearrange("p k (a w) -> p k a w", a=1).broadcast_to([P, 2, FH, W]) for t in (cos, sin)]
                    pool.wait_ge(turn_done, n + 1)
                    mine = qk[:, :, o, 0:W].rearrange("p (k f) w -> p k f w", k=2)
                    nc.gpsimd.tensor_tensor(mine, mine, tab[0], ALU.mult).then_inc(cos_done, 1)
                    other = turned[n % 2][:].rearrange("p (k f) w -> p k f w", k=2)
                    nc.gpsimd.tensor_tensor(other, other, tab[1], ALU.mult).then_inc(sin_done, 1)

        @block.scalar
        def _(act):
            primed(act, v_read + v_stored)
            act.wait_ge(consts_in, 16 * NCONST)
            for b in range(B):
                with act.Fori(0, WINDOWS // WIN_UNROLL) as i:
                    for s in range(WIN_UNROLL):
                        act.wait_ge(acc_full[s], 1 + b * TURNS + i + 1)
                        act.wait_ge(v_stored[s], 1 + 16 * (b * TURNS + i))
                        nc.scalar.activation(vout[s][:], acc_v[s][0:C * OW, 0:F], ACT.Identity, bias=v_bias[:]).then_inc(v_read[s], 1)
                        act.wait_ge(v_read[s], 1 + b * TURNS + i + 1)
                        act.dma_start(V[b, :, bass.ds((i * WIN_UNROLL + s) * OW, OW), :], vout[s][:]).then_inc(v_stored[s], 16)
                for o in range(C):
                    n = b * C + o
                    act.wait_ge(rope_done, n + 1)
                    if n >= 2:
                        act.wait_ge(hi_stored[n % 2], 16 * (n // 2))
                        act.wait_ge(lo_done, n - 1)
                    nc.scalar.activation(hi[n % 2][:], qk[:, :, o, 0:W], ACT.Copy).then_inc(hi_done, 1)
                    act.wait_ge(hi_done, n + 1)
                    act.dma_start(QK[b, o, 0].rearrange("k (f p) w -> p (k f) w", p=P), hi[n % 2][:]).then_inc(hi_stored[n % 2], 16)
                    act.wait_ge(lo_done, n + 1)
                    act.dma_start(QK[b, o, 1].rearrange("k (f p) w -> p (k f) w", p=P), lo[n % 2][:]).then_inc(lo_stored[n % 2], 16)
            for s in range(WIN_UNROLL):
                act.wait_ge(v_stored[s], 1 + 16 * B * TURNS)
            for s in range(2):
                act.wait_ge(hi_stored[s], 16 * B * C // 2)
                act.wait_ge(lo_stored[s], 16 * B * C // 2)


def attend(nc, T, QK, V, Z):
    with ExitStack() as ctx:
        sb, ps, sem = allocators(nc, ctx)
        QT = W // P
        PB = 4
        HB = B * HEADS
        STEPS = HB * QT
        ident = sb("a_ident", [P, P])
        q = [sb(f"a_q{s}", [P, HEADS, W], BF16) for s in range(B)]
        k = [sb(f"a_k{s}", [P, HEADS, W], BF16) for s in range(B)]
        v = [sb(f"a_v{s}", [P, QT, F]) for s in range(B)]
        wo = sb("a_wo", [P, FH, F])
        bo = sb("a_bo", [P, FH])
        negmax = sb("a_negmax", [P, 2 * QT])
        total = sb("a_total", [P, 2 * QT])
        inverse = sb("a_inverse", [P, 2 * QT])
        prob = [sb(f"a_prob{s}", [P, W]) for s in range(PB)]
        probT = [sb(f"a_probT{s}", [P, QT, W]) for s in range(2)]
        o = [sb(f"a_o{s}", [P, QT, F]) for s in range(B)]
        oT = sb("a_oT", [P, FH, W])
        z = [sb(f"a_z{s}", [P, W]) for s in range(FH)]
        score = [ps(f"a_score{s}", [P, W]) for s in range(PB)]
        turn = [ps(f"a_turn{s}", [P, QT, P]) for s in range(2)]
        mix = ps("a_mix", [P, 2, QT, DH])
        out = ps("a_out", [P, W])

        const_in = sem("a_const_in")
        qk_in = [sem(f"a_qk_in{s}") for s in range(B)]
        v_in = [sem(f"a_v_in{s}") for s in range(B)]
        wo_in = sem("a_wo_in")
        score_full = sem("a_score_full")
        max_done = sem("a_max_done")
        exp_done = sem("a_exp_done")
        turned = sem("a_turned")
        kept = [sem(f"a_kept{s}") for s in range(2)]
        mixed = sem("a_mixed")
        inverted = sem("a_inverted")
        normed = [sem(f"a_normed{s}") for s in range(B)]
        out_full = [sem(f"a_out_full{s}") for s in range(B)]
        out_kept = [sem(f"a_out_kept{s}") for s in range(B)]
        z_stored = [sem(f"a_z_stored{s}") for s in range(FH)]
        QK_LOADS = 8

        TURN_LAG = 3
        MIX_AT = {QT * (hh + 1) + 1: hh for hh in range(HB)}
        TAIL_AT = {QT * HEADS * (s + 1) + 5 + 2 * j: (s, j) for s in range(B) for j in range(4)}
        LAST = STEPS + TURN_LAG + 16
        block = ctx.enter_context(nc.Block())

        @block.sync
        def _(sp):
            sp.dma_start(ident[:], T["ident"]).then_inc(const_in, 16)
            with sp.Fori(0, C) as i:
                for s in range(B):
                    sp.wait_ge(normed[s], 1 + i * HEADS)
                    src = QK[s, bass.ds(i, 1)].rearrange("a p k f w -> (a p) k f w")
                    for r in range(2):
                        for part in range(2):
                            row = (2 * r + part) * DH
                            sp.dma_start(q[s][row:row + DH], src[part, 0].rearrange("(h d) w -> d h w", d=DH)).then_inc(qk_in[s], 16)
                            row = (2 * part + r) * DH
                            sp.dma_start(k[s][row:row + DH], src[part, 1].rearrange("(h d) w -> d h w", d=DH)).then_inc(qk_in[s], 16)
                    sp.dma_start(v[s][:], V[s, bass.ds(i, 1), 0:W].rearrange("a (t p) f -> p (a t) f", p=P)).then_inc(v_in[s], 16)
                    if s == 0:
                        sp.wait_ge(out_kept[1], 1 + 4 * i)
                        sp.dma_start(wo[:], T["w_o"][bass.ds(i, 1)].rearrange("a (h p) f -> p (a h) f", p=P)).then_inc(wo_in, 16)
                        sp.dma_start(bo[:], T["b_o"][bass.ds(i, 1)].rearrange("a p h -> p (a h)")).then_inc(wo_in, 16)

        @block.tensor
        def _(pe):
            primed(pe, [mixed, turned])
            pe.wait_ge(const_in, 16)

            def scores(i, t):
                s, h, qt = t // (HEADS * QT), t // QT % HEADS, t % QT
                if t % (HEADS * QT) == 0:
                    pe.wait_ge(qk_in[s], 16 * QK_LOADS * (i + 1))
                pe.wait_ge(exp_done, 1 + i * STEPS + max(t - PB + 1, 0))
                nc.tensor.matmul(score[t % PB][:], q[s][:, h, qt * P:(qt + 1) * P], k[s][:, h, :],
                                 start=True, stop=True).then_inc(score_full, 1)

            def turn_probs(i, t):
                pe.wait_ge(exp_done, 1 + i * STEPS + t + 1)
                pe.wait_ge(kept[t % 2], 1 + i * (STEPS // 2) + t // 2)
                for kt in range(QT):
                    last = nc.tensor.transpose(turn[t % 2][:, kt, :], prob[t % PB][:, kt * P:(kt + 1) * P], ident[:])
                last.then_inc(turned, 1)

            def mix_head(i, hh):
                s, h = hh // HEADS, hh % HEADS
                if h == 0:
                    pe.wait_ge(v_in[s], 16 * (i + 1))
                for par in range(2):
                    pe.wait_ge(kept[par], 1 + i * (STEPS // 2) + (hh + 1) * QT // 2)
                if hh >= 2:
                    pe.wait_ge(normed[(hh - 2) // HEADS], 1 + i * HEADS + (hh - 2) % HEADS + 1)
                for qt in range(QT):
                    for kt in range(QT):
                        last = nc.tensor.matmul(mix[:, hh % 2, qt, :], probT[hh % 2][:, kt, qt * P:(qt + 1) * P],
                                                v[s][:, kt, h * DH:(h + 1) * DH], start=kt == 0, stop=kt == QT - 1)
                last.then_inc(mixed, 1)

            def tail(i, s, j):
                if j == 0:
                    pe.wait_ge(normed[s], 1 + (i + 1) * HEADS)
                    pe.wait_ge(out_kept[1 - s], 1 + 4 * (i + s))
                else:
                    pe.wait_ge(out_kept[s], 1 + 4 * i + j)
                if j < FH:
                    for qt in range(QT):
                        last = nc.tensor.transpose(out[:, qt * P:(qt + 1) * P], o[s][:, qt, j * P:(j + 1) * P], ident[:])
                else:
                    fo = j - FH
                    pe.wait_ge(wo_in, 32 * (i + 1))
                    for fh in range(FH):
                        last = nc.tensor.matmul(out[:], wo[:, fh, fo * P:(fo + 1) * P], oT[:, fh, :],
                                                start=fh == 0, stop=fh == FH - 1)
                last.then_inc(out_full[s], 1)

            with pe.Fori(0, C) as i:
                for t in range(LAST):
                    if t < STEPS:
                        scores(i, t)
                    if 0 <= t - TURN_LAG < STEPS:
                        turn_probs(i, t - TURN_LAG)
                    if t - TURN_LAG in MIX_AT:
                        mix_head(i, MIX_AT[t - TURN_LAG])
                    if t - TURN_LAG in TAIL_AT:
                        tail(i, *TAIL_AT[t - TURN_LAG])

        def keep(engine, copy, i, t):
            engine.wait_ge(turned, 1 + i * STEPS + t + 1)
            hh, qt = t // QT, t % QT
            if qt < 2:
                engine.wait_ge(mixed, 1 + i * HB + max(hh - 1, 0))
            copy(probT[hh % 2][:, :, qt * P:(qt + 1) * P], turn[t % 2][:]).then_inc(kept[t % 2], 1)

        @block.vector
        def _(ve):
            primed(ve, normed + kept[1:] + [inverted])
            def norm_head(i, hh):
                s, h, c0 = hh // HEADS, hh % HEADS, hh % 2 * QT
                ve.wait_ge(exp_done, 1 + i * STEPS + (hh + 1) * QT)
                nc.vector.reciprocal(inverse[:, c0:c0 + QT], total[:, c0:c0 + QT]).then_inc(inverted, 1)
                ve.wait_ge(inverted, 1 + i * HB + hh + 1)
                ve.wait_ge(mixed, 1 + i * HB + hh + 1)
                if h == 0:
                    ve.wait_ge(out_kept[s], 1 + 4 * i)
                nc.vector.tensor_tensor(o[s][:, :, h * DH:(h + 1) * DH], mix[:, hh % 2],
                                        inverse[:, c0:c0 + QT].unsqueeze(2).broadcast_to([P, QT, DH]),
                                        ALU.mult).then_inc(normed[s], 1)

            with ve.Fori(0, C) as i:
                for t in range(LAST):
                    if t < STEPS:
                        ve.wait_ge(score_full, i * STEPS + t + 1)
                        nc.vector.reduce_max(negmax[:, t % (2 * QT):t % (2 * QT) + 1], score[t % PB][:], AX.X,
                                             negate=True).then_inc(max_done, 1)
                    if 0 <= t - TURN_LAG < STEPS and (t - TURN_LAG) % 2:
                        keep(ve, nc.vector.tensor_copy, i, t - TURN_LAG)
                    if t - TURN_LAG - 1 in MIX_AT:
                        norm_head(i, MIX_AT[t - TURN_LAG - 1])

        @block.scalar
        def _(act):
            primed(act, out_kept + z_stored + kept[:1] + [exp_done])
            def keep_out(i, s, j):
                act.wait_ge(out_full[s], 4 * i + j + 1)
                if j < FH:
                    nc.scalar.activation(oT[:, j, :], out[:], ACT.Copy).then_inc(out_kept[s], 1)
                else:
                    if j == FH:
                        act.wait_ge(wo_in, 32 * (i + 1))
                    act.wait_ge(z_stored[j - FH], 1 + 16 * (2 * i + s))
                    nc.scalar.activation(z[j - FH][:], out[:], ACT.Identity, bias=bo[:, j - FH:j - FH + 1]).then_inc(out_kept[s], 1)

            def store_z(i, s, j):
                if j >= FH:
                    fo = j - FH
                    act.wait_ge(out_kept[s], 1 + 4 * i + j + 1)
                    act.dma_start(Z[s, fo * P:(fo + 1) * P, bass.ds(i, 1)].rearrange("f a w -> f (a w)"),
                                  z[fo][:]).then_inc(z_stored[fo], 16)

            with act.Fori(0, C) as i:
                for t in range(LAST):
                    if t < STEPS:
                        hh = t // QT
                        act.wait_ge(max_done, i * STEPS + t + 1)
                        act.wait_ge(turned, 1 + i * STEPS + max(t - PB + 1, 0))
                        if t % QT == 0:
                            act.wait_ge(inverted, 1 + i * HB + max(hh - 1, 0))
                        nc.scalar.activation(prob[t % PB][:], score[t % PB][:], ACT.Exp,
                                             bias=negmax[:, t % (2 * QT):t % (2 * QT) + 1],
                                             accum_out=total[:, t % (2 * QT):t % (2 * QT) + 1]).then_inc(exp_done, 1)
                    if 0 <= t - TURN_LAG < STEPS and (t - TURN_LAG) % 2 == 0:
                        keep(act, lambda to, frm: nc.scalar.activation(to, frm, ACT.Copy), i, t - TURN_LAG)
                    if t - TURN_LAG - 1 in TAIL_AT:
                        keep_out(i, *TAIL_AT[t - TURN_LAG - 1])
                    if t - TURN_LAG - 2 in TAIL_AT:
                        store_z(i, *TAIL_AT[t - TURN_LAG - 2])
            for fo in range(FH):
                act.wait_ge(z_stored[fo], 1 + 16 * B * C)


def residual(nc, T, Z, X1, S):
    with ExitStack() as ctx:
        sb, ps, sem = allocators(nc, ctx)
        NB = F // KR
        U = 4
        wmix = sb("r_wmix", [P, P])
        bmix = sb("r_bmix", [P, 1])
        group = sb("r_group", [P, P])
        z = [sb(f"r_z{s}", [P, W]) for s in range(U)]
        x = [sb(f"r_x{s}", [P, W]) for s in range(U)]
        x1 = [sb(f"r_x1{s}", [P, W]) for s in range(U)]
        stats = sb("r_stats", [P, B, NB, 6])
        mv = sb("r_mv", [P, B, 2])
        small = sb("r_small", [P, 8, B])
        out = sb("r_out", [P, B, 2])
        acc = [ps(f"r_acc{s}", [P, W]) for s in range(U)]
        sums = ps("r_sums", [P, 2, B])

        consts_in = sem("r_consts_in")
        wzero = sem("r_wzero")
        z_in = [sem(f"r_z_in{s}") for s in range(U)]
        x_in = [sem(f"r_x_in{s}") for s in range(U)]
        acc_full = [sem(f"r_acc_full{s}") for s in range(U)]
        x1_ready = [sem(f"r_x1_ready{s}") for s in range(U)]
        stats_done = [sem(f"r_stats_done{s}") for s in range(U)]
        x1_stored = [sem(f"r_x1_stored{s}") for s in range(U)]
        aggregated = sem("r_aggregated")
        summed = sem("r_summed")
        dve = sem("r_dve")
        std_ready = sem("r_std_ready")
        s_stored = sem("r_s_stored")
        NCONST = 2 * KR + 1
        STORES = 3
        block = ctx.enter_context(nc.Block())

        @block.sync
        def _(sp):
            sp.wait_ge(wzero, 1)
            for r in range(KR):
                sp.dma_start(wmix[r * C:(r + 1) * C, r * C:(r + 1) * C], T["w_mix"]).then_inc(consts_in, 16)
                sp.dma_start(bmix[r * C:(r + 1) * C], T["b_mix"]).then_inc(consts_in, 16)
            sp.dma_start(group[:], T["same_group"]).then_inc(consts_in, 16)
            for b in range(B):
                with sp.Fori(0, NB // U) as i:
                    for s in range(U):
                        rows = bass.ds((i * U + s) * KR, KR)
                        sp.wait_ge(acc_full[s], 1 + b * (NB // U) + i)
                        sp.dma_start(z[s][:], Z[b, rows].rearrange("h c w -> (h c) w")).then_inc(z_in[s], 16)
                        sp.wait_ge(x1_ready[s], 1 + b * (NB // U) + i)
                        sp.dma_start(x[s][:],
                                     T["x"][b, :, rows].rearrange("c h w -> h c w")).then_inc(x_in[s], 16)

        @block.gpsimd
        def _(pool):
            nc.gpsimd.memset(wmix[:], 0.0).then_inc(wzero, 1)

        @block.tensor
        def _(pe):
            primed(pe, acc_full)
            pe.wait_ge(consts_in, 16 * NCONST)
            for b in range(B):
                with pe.Fori(0, NB // U) as i:
                    for s in range(U):
                        pe.wait_ge(z_in[s], 16 * (b * (NB // U) + i + 1))
                        pe.wait_ge(x1_ready[s], 1 + b * (NB // U) + i)
                        nc.tensor.matmul(acc[s][:], wmix[:], z[s][:], start=True, stop=True).then_inc(acc_full[s], 1)
            pe.wait_ge(aggregated, B)
            nc.tensor.matmul(sums[:, 0, :], group[:], mv[:, :, 0], start=True, stop=True)
            nc.tensor.matmul(sums[:, 1, :], group[:], mv[:, :, 1], start=True, stop=False).then_inc(summed, 1)
            pe.wait_ge(dve, 3)
            nc.tensor.matmul(sums[:, 1, :], group[:], small[:, 2, :], start=False, stop=True).then_inc(summed, 1)

        @block.vector
        def _(v):
            primed(v, x1_ready)
            v.wait_ge(consts_in, 16 * NCONST)
            for b in range(B):
                with v.Fori(0, NB // U) as i:
                    for s in range(U):
                        turn = b * (NB // U) + i
                        v.wait_ge(acc_full[s], 1 + turn + 1)
                        v.wait_ge(x_in[s], 16 * (turn + 1))
                        v.wait_ge(x1_stored[s], 1 + 16 * STORES * turn)
                        nc.vector.scalar_tensor_tensor(x1[s][:], acc[s][:], bmix[:], x[s][:], ALU.add, ALU.add).then_inc(x1_ready[s], 1)
                        v.wait_ge(x1_ready[s], 1 + turn + 1)
                        nc.vector.bn_stats(stats[:, b, bass.ds(i * U + s, 1), :].rearrange("p a n -> p (a n)"), x1[s][:]).then_inc(stats_done[s], 1)
            for s in range(U):
                v.wait_ge(stats_done[s], B * NB // U)
            for b in range(B):
                nc.vector.bn_aggr(mv[:, b, :], stats[:, b].rearrange("p n s -> p (n s)")).then_inc(aggregated, 1)
            v.wait_ge(summed, 1)
            nc.vector.tensor_copy(small[:, 0, :], sums[:, 0, :]).then_inc(dve, 1)
            nc.vector.tensor_tensor(small[:, 1, :], mv[:, :, 0], sums[:, 0, :], ALU.subtract).then_inc(dve, 1)
            v.wait_ge(dve, 2)
            nc.vector.tensor_tensor(small[:, 2, :], small[:, 1, :], small[:, 1, :], ALU.mult).then_inc(dve, 1)
            v.wait_ge(summed, 2)
            nc.vector.tensor_scalar(small[:, 4, :], sums[:, 1, :], 1e-5, None, ALU.add).then_inc(dve, 1)
            v.wait_ge(std_ready, 1)
            nc.vector.reciprocal(out[:, :, 0], small[:, 5, :]).then_inc(dve, 1)
            v.wait_ge(dve, 5)
            nc.vector.scalar_tensor_tensor(out[:, :, 1], small[:, 0, :], -1.0, out[:, :, 0], ALU.mult, ALU.mult).then_inc(dve, 1)

        @block.scalar
        def _(act):
            primed(act, x1_stored)
            for b in range(B):
                with act.Fori(0, NB // U) as i:
                    for s in range(U):
                        rows = bass.ds((i * U + s) * KR, KR)
                        act.wait_ge(x1_ready[s], 1 + b * (NB // U) + i + 1)
                        for to, frm, n in ((PAD_L, 0, W), (0, W - PAD_L, PAD_L), (PAD_L + W, 0, PAD_R)):
                            act.dma_start(X1[b, rows, :, to:to + n].rearrange("h c w -> (h c) w"),
                                          x1[s][:, frm:frm + n]).then_inc(x1_stored[s], 16)
            act.wait_ge(dve, 4)
            nc.scalar.activation(small[:, 5, :], small[:, 4, :], ACT.Sqrt).then_inc(std_ready, 1)
            act.wait_ge(dve, 6)
            act.dma_start(S, out[:]).then_inc(s_stored, 16)
            act.wait_ge(s_stored, 16)
            for s in range(U):
                act.wait_ge(x1_stored[s], 1 + 16 * STORES * B * NB // U)


def sphere(nc, T, X1, S, out):
    with ExitStack() as ctx:
        sb, ps, sem = allocators(nc, ctx)
        M = OR * C
        side = sb("s_side", [P, CHUNKS * CHUNK * OR])
        centre = sb("s_centre", [P, CHUNKS * CHUNK * OR])
        slot = sb("s_slot", [P, KR])
        w_side = sb("s_w_side", [P, C, C])
        w_centre = sb("s_w_centre", [P, C, C])
        l_side = sb("s_l_side", [P, C, P])
        l_centre = sb("s_l_centre", [P, C, P])
        mat_h = sb("s_mat_h", [P, CHUNKS * CHUNK, M], BF16)
        mat_l = sb("s_mat_l", [P, CHUNKS * CHUNK, M], BF16)
        bias = sb("s_bias", [M, 1])
        norm = sb("s_norm", [P, B, 2])
        raw = [sb(f"s_raw{s}", [P, XROW]) for s in range(B)]
        xn = [sb(f"s_xn{s}", [P, XROW]) for s in range(B)]
        xh = [sb(f"s_xh{s}", [P, XROW], BF16) for s in range(B)]
        xl = [sb(f"s_xl{s}", [P, XROW], BF16) for s in range(B)]
        res = [sb(f"s_res{s}", [M, W]) for s in range(B)]
        y = [sb(f"s_y{s}", [M, W]) for s in range(B)]
        made = [ps(f"s_made{s}", [P, CHUNK * OR]) for s in range(4)]
        acc = [ps(f"s_acc{s}", [P, W]) for s in range(B)]

        consts_in = sem("s_consts_in")
        l_ready = sem("s_l_ready")
        made_full = [sem(f"s_made_full{s}") for s in range(4)]
        mat_hi = [sem(f"s_mat_hi{s}") for s in range(4)]
        mat_lo = [sem(f"s_mat_lo{s}") for s in range(4)]
        raw_in = [sem(f"s_raw_in{s}") for s in range(B)]
        res_in = [sem(f"s_res_in{s}") for s in range(B)]
        xn_done = [sem(f"s_xn_done{s}") for s in range(B)]
        xh_done = [sem(f"s_xh_done{s}") for s in range(B)]
        xl_done = [sem(f"s_xl_done{s}") for s in range(B)]
        acc_full = [sem(f"s_acc_full{s}") for s in range(B)]
        y_ready = [sem(f"s_y_ready{s}") for s in range(B)]
        y_stored = [sem(f"s_y_stored{s}") for s in range(B)]
        KS = 2 * 3 * KR
        KC = 3 * KR
        NCONST = 3 + 9 + OR + 1
        block = ctx.enter_context(nc.Block())

        def blocks(engine):
            for first, count in SPHERE_RUNS:
                h0, n, r0, shifts, e0 = SPHERE_BLOCKS[first]
                if count == 1:
                    yield first, h0, n, r0, shifts, e0
                else:
                    with engine.Fori(0, count) as i:
                        yield i + first, i * OR + h0, n, i * OR + r0, shifts, i * len(shifts) + e0

        def span(shifts):
            a = min(shifts)
            return PAD_L + a, W + max(shifts) - a

        @block.sync
        def _(sp):
            sp.dma_start(side[:], T["side"]).then_inc(consts_in, 16)
            sp.dma_start(centre[:], T["centre"]).then_inc(consts_in, 16)
            sp.dma_start(slot[:], T["slot"]).then_inc(consts_in, 16)
            for kx in range(3):
                for ky in range(3):
                    to = w_centre if kx == 1 else w_side
                    p0 = (ky if kx == 1 else kx // 2 * 3 + ky) * KR
                    sp.dma_start(to[p0:p0 + KR], T["w_sphere"][kx, ky:ky + 1].broadcast_to([KR, C, C])).then_inc(consts_in, 16)
            for r in range(OR):
                sp.dma_start(bias[r * C:(r + 1) * C], T["b_sphere"]).then_inc(consts_in, 16)
            sp.dma_start(norm[:], S).then_inc(consts_in, 16)
            for at, h0, n, r0, shifts, e0 in blocks(sp):
                c0, cols = span(shifts)
                for b in range(B):
                    sp.wait_ge(xn_done[b], at)
                    sp.dma_start(raw[b][:, 0:cols], X1[b, bass.ds(r0, KR), :, c0:c0 + cols].rearrange("h c w -> (h c) w")
                                 ).then_inc(raw_in[b], 16)
                    sp.wait_ge(y_ready[b], at)
                    sp.dma_start(res[b][0:n * C], X1[b, bass.ds(h0, n), :, PAD_L:PAD_L + W].rearrange("h c w -> (h c) w")
                                 ).then_inc(res_in[b], 16)

        @block.gpsimd
        def _(pool):
            for at, h0, n, r0, shifts, e0 in blocks(pool):
                for b in range(B):
                    pool.wait_ge(y_ready[b], at + 1)
                    pool.dma_start(out[b, :, bass.ds(h0, n)].rearrange("c h w -> h c w"),
                                   y[b][0:n * C]).then_inc(y_stored[b], 16)
            for b in range(B):
                pool.wait_ge(y_stored[b], 16 * BLOCKS)

        @block.scalar
        def _(act):
            act.wait_ge(consts_in, 16 * NCONST)
            with act.Fori(0, CHUNKS) as i:
                for o in range(C):
                    act.wait_ge(made_full[o % 4], i * (C // 4) + o // 4 + 1)
                    nc.scalar.activation(mat_h[:, bass.ds(i * CHUNK, CHUNK), o::C].rearrange("p e h -> p (e h)"),
                                         made[o % 4][:], ACT.Copy).then_inc(mat_hi[o % 4], 1)
            for at, h0, n, r0, shifts, e0 in blocks(act):
                c0, cols = span(shifts)
                for b in range(B):
                    act.wait_ge(raw_in[b], 16 * (at + 1))
                    act.wait_ge(xl_done[b], at)
                    nc.scalar.activation(xn[b][:, 0:cols], raw[b][:, 0:cols], ACT.Identity, bias=norm[:, b, 1:2],
                                         scale=norm[:, b, 0:1]).then_inc(xn_done[b], 1)
                    act.wait_ge(xn_done[b], at + 1)
                    act.wait_ge(acc_full[b], at)
                    nc.scalar.activation(xh[b][:, 0:cols], xn[b][:, 0:cols], ACT.Copy).then_inc(xh_done[b], 1)

        @block.vector
        def _(v):
            primed(v, mat_lo)
            v.wait_ge(consts_in, 16 * NCONST)
            for o in range(C):
                for k, w_, l_ in ((KS, w_side, l_side), (KC, w_centre, l_centre)):
                    nc.vector.tensor_tensor(l_[0:k, o, :].rearrange("p (s c) -> p s c", c=C),
                                            w_[0:k, o, :].unsqueeze(1).broadcast_to([k, KR, C]),
                                            slot[0:k].unsqueeze(2).broadcast_to([k, KR, C]), ALU.mult).then_inc(l_ready, 1)
            with v.Fori(0, CHUNKS) as i:
                for o in range(C):
                    v.wait_ge(mat_hi[o % 4], i * (C // 4) + o // 4 + 1)
                    at = bass.ds(i * CHUNK, CHUNK)
                    nc.vector.tensor_tensor(mat_l[:, at, o::C].rearrange("p e h -> p (e h)"), made[o % 4][:],
                                            mat_h[:, at, o::C].rearrange("p e h -> p (e h)"), ALU.subtract).then_inc(mat_lo[o % 4], 1)
            for at, h0, n, r0, shifts, e0 in blocks(v):
                c0, cols = span(shifts)
                for b in range(B):
                    v.wait_ge(xh_done[b], at + 1)
                    nc.vector.tensor_tensor(xl[b][:, 0:cols], xn[b][:, 0:cols], xh[b][:, 0:cols], ALU.subtract).then_inc(xl_done[b], 1)
                for b in range(B):
                    v.wait_ge(acc_full[b], at + 1)
                    v.wait_ge(res_in[b], 16 * (at + 1))
                    v.wait_ge(y_stored[b], 16 * at)
                    nc.vector.scalar_tensor_tensor(y[b][0:n * C], acc[b][0:n * C, :], bias[0:n * C], res[b][0:n * C],
                                                   ALU.add, ALU.add).then_inc(y_ready[b], 1)

        @block.tensor
        def _(pe):
            pe.wait_ge(l_ready, 2 * C)
            with pe.Fori(0, CHUNKS) as i:
                for o in range(C):
                    pe.wait_ge(mat_lo[o % 4], 1 + i * (C // 4) + o // 4)
                    cols = bass.ds(i * (CHUNK * OR), CHUNK * OR)
                    nc.tensor.matmul(made[o % 4][:], l_side[0:KS, o, :], side[0:KS, cols], start=True, stop=False)
                    nc.tensor.matmul(made[o % 4][:], l_centre[0:KC, o, :], centre[0:KC, cols],
                                     start=False, stop=True).then_inc(made_full[o % 4], 1)
            for s in range(4):
                pe.wait_ge(mat_lo[s], 1 + CHUNKS * C // 4)
            for at, h0, n, r0, shifts, e0 in blocks(pe):
                for b in range(B):
                    pe.wait_ge(xl_done[b], at + 1)
                    pe.wait_ge(y_ready[b], at)
                    for j, s in enumerate(shifts):
                        c0 = s - min(shifts)
                        hi = mat_h[:, bass.ds(e0 + j, 1), :].rearrange("p a m -> p (a m)")
                        lo = mat_l[:, bass.ds(e0 + j, 1), :].rearrange("p a m -> p (a m)")
                        nc.tensor.matmul(acc[b][0:M, :], hi, xh[b][:, c0:c0 + W], start=j == 0, stop=False)
                        nc.tensor.matmul(acc[b][0:M, :], hi, xl[b][:, c0:c0 + W], start=False, stop=False)
                        last = nc.tensor.matmul(acc[b][0:M, :], lo, xh[b][:, c0:c0 + W], start=False, stop=j == len(shifts) - 1)
                    last.then_inc(acc_full[b], 1)


def program(nc, T, out):
    def dram(name, shape, dt=FP32):
        return nc.dram_tensor(name, shape, dt).ap()

    Y = dram("Y", (B, YROWS, C, QKV))
    QK = dram("QK", (B, C, 2, 2, F, W), BF16)
    V = dram("V", (B, C, WPAD, F))
    Z = dram("Z", (B, F, C, W))
    X1 = dram("X1", (B, F, C, XROW))
    S = dram("S", (P, B, 2))
    project(nc, T, Y)
    convolve(nc, T, Y, QK, V)
    attend(nc, T, QK, V, Z)
    residual(nc, T, Z, X1, S)
    sphere(nc, T, X1, S, out)


def kernel(**inputs):
    import concourse.bacc as bacc
    from concourse.bass_utils import run_bass_kernel_spmd as run

    a = {name: np.asarray(v) for name, v in inputs.items()}
    layer = lambda name: a["L0_conv_" + name]
    taps = np.stack([layer(n + "_conv_w")[:, :, 0, :] for n in "qkv"])
    taps = np.ascontiguousarray(taps.transpose(2, 0, 1, 3)[..., ::-1]).reshape(C, 3 * C, TAPS)
    arrays = {
        "x": a["x"],
        "w_qkv": np.concatenate([layer("W" + n).transpose(0, 2, 1) for n in "qkv"], 2),
        "b_qkv": np.concatenate([layer("b" + n) for n in "qkv"], 1),
        "taps": np.pad(taps, ((0, 0), (0, 0), (KW - TAPS, OW - 1))),
        "qkv_conv_b": np.stack([layer(n + "_conv_b") for n in "qkv"]),
        "w_o": layer("Wo").transpose(0, 2, 1),
        "b_o": layer("bo").reshape(C, FH, P).transpose(0, 2, 1),
        "w_mix": layer("o_conv_w")[:, :, 0, 0].T,
        "b_mix": layer("o_conv_b").reshape(C, 1),
        "w_sphere": a["L1_conv_weight"].transpose(3, 2, 0, 1),
        "b_sphere": a["L1_conv_bias"].reshape(C, 1),
        **constants(),
    }
    nc = bacc.Bacc("TRN2", target_bir_lowering=False, num_devices=1)
    T, ins = {}, {}
    for name, v in arrays.items():
        v = np.ascontiguousarray(v)
        ins["in_" + name] = v
        T[name] = nc.dram_tensor("in_" + name, v.shape, mybir.dt.from_np(v.dtype), kind="ExternalInput").ap()
    out = nc.dram_tensor("out", a["x"].shape, mybir.dt.from_np(a["x"].dtype), kind="ExternalOutput").ap()
    program(nc, T, out)
    return run(nc, [ins], core_ids=[0]).results[0]["out"]
```

```python
import math
from contextlib import ExitStack

import numpy as np

import concourse.bass as bass
from concourse import mybir

FP32 = mybir.dt.float32
BF16 = mybir.dt.bfloat16
ALU = mybir.AluOpType
ACT = mybir.ActivationFunctionType
AX = mybir.AxisListType

B, C, F, W = 2, 8, 256, 512
P = 128
HEADS = 8
DH = F // HEADS
GROUPS = 4
CPG = C // GROUPS
FH = F // P
QKV = 3 * F
TAPS = 7
PAD = TAPS // 2

KW = P // C
OW = KW - TAPS + 1
WINDOWS = -(-W // OW)
WIN_UNROLL = 4
WPAD = WINDOWS * OW
YROWS = WPAD + 2 * PAD

KR = P // C
OR = KR - 3
BLOCKS = -(-F // OR)


def sphere_taps():
    polar = np.linspace(1.0 / (2 * F), 1.0 - 1.0 / (2 * F), F) * np.pi
    sin_p, cos_p = np.sin(polar), np.cos(polar)
    scale = np.pi / F
    taps = [dict() for _ in range(F)]
    for ky in range(3):
        for kx in range(3):
            dx, dy = (kx - 1) * scale, (ky - 1) * scale
            radial, height = sin_p + cos_p * dy, -cos_p + sin_p * dy
            shift = np.arctan2(dx, radial) / (2 * np.pi) * W
            row = np.arctan2(np.sqrt(radial ** 2 + dx ** 2), -height) / np.pi * F - 0.5
            for h in range(F):
                y0, x0 = int(np.floor(row[h])), int(np.floor(shift[h]))
                wy, wx = row[h] - y0, shift[h] - x0
                for yy, cy in ((y0, 1 - wy), (y0 + 1, wy)):
                    for xx, cx in ((x0, 1 - wx), (x0 + 1, wx)):
                        at = taps[h].setdefault((min(max(yy, 0), F - 1), xx), {})
                        at[(ky, kx)] = at.get((ky, kx), 0.0) + cy * cx
    return taps


def sphere_plan():
    taps = sphere_taps()
    blocks, entries = [], []
    for i in range(BLOCKS):
        h0, n = OR * i, min(OR, F - OR * i)
        used = [(h, at, k) for h in range(h0, h0 + n) for at, k in taps[h].items()]
        r0 = min(min(at[0] for _, at, _ in used), F - KR)
        assert max(at[0] for _, at, _ in used) < r0 + KR
        shifts = sorted({at[1] for _, at, _ in used})
        blocks.append((h0, n, r0, shifts, len(entries)))
        for s in shifts:
            coef = np.zeros((3, 3, KR, OR))
            for h, (r, sh), k in used:
                if sh == s:
                    for (ky, kx), v in k.items():
                        coef[kx, ky, r - r0, h - h0] += v
            entries.append(coef)
    e = np.stack(entries, 3)
    side = e[[0, 2]].reshape(2 * 3 * KR, -1)
    centre = e[1].reshape(3 * KR, -1)
    return blocks, np.concatenate([side, np.zeros((P - 6 * KR, side.shape[1]))]).astype(np.float32), \
        np.concatenate([centre, np.zeros((P - 3 * KR, side.shape[1]))]).astype(np.float32)


SPHERE_BLOCKS, SPHERE_SIDE, SPHERE_CENTRE = sphere_plan()
ENTRIES = SPHERE_SIDE.shape[1] // OR
CHUNK = 36
CHUNKS = -(-ENTRIES // CHUNK)
SPHERE_SIDE, SPHERE_CENTRE = (np.pad(a, ((0, 0), (0, (CHUNKS * CHUNK - ENTRIES) * OR))) for a in (SPHERE_SIDE, SPHERE_CENTRE))


def sphere_runs():
    runs = []
    for i, (h0, n, r0, shifts, _) in enumerate(SPHERE_BLOCKS):
        j = runs[-1][0] if runs else None
        if runs and (n, h0 - r0, shifts) == (SPHERE_BLOCKS[j][1], SPHERE_BLOCKS[j][0] - SPHERE_BLOCKS[j][2], SPHERE_BLOCKS[j][3]):
            runs[-1] = (j, runs[-1][1] + 1)
        else:
            runs.append((i, 1))
    return runs


SPHERE_RUNS = sphere_runs()
MAX_SHIFT = max(max(abs(s) for s in blk[3]) for blk in SPHERE_BLOCKS)
PAD_L = max(-min(min(blk[3]) for blk in SPHERE_BLOCKS), 0)
PAD_R = max(max(blk[3]) for blk in SPHERE_BLOCKS)
XROW = PAD_L + W + PAD_R


def rope_tables():
    inv = (np.float32(1.0) / np.float32(10000.0) ** (np.arange(0, DH, 2, dtype=np.float32) / np.float32(DH))).astype(np.float32)
    angle = (np.arange(W, dtype=np.float32)[:, None] * inv[None, :]).astype(np.float32)
    cos = np.repeat(np.cos(angle.astype(np.float64)), 2, -1).T
    sin = np.repeat(np.sin(angle.astype(np.float64)), 2, -1).T
    sin = sin * np.where(np.arange(DH) % 2 == 0, -1.0, 1.0)[:, None]
    scale = 1.0 / math.sqrt(F)
    out = [np.tile(np.stack([t * scale, t], 1), (P // DH, 1, 1)).astype(np.float32) for t in (cos, sin)]
    return out


def constants():
    cos, sin = rope_tables()
    part = np.arange(P)
    same_group = (part[:, None] % C // CPG == part[None, :] % C // CPG) / float(P // C * CPG)
    slot = np.zeros((P, KR), np.float32)
    slot[part, part % KR] = 1.0
    return {
        "ident": np.eye(P, dtype=np.float32),
        "cos": cos, "sin": sin,
        "same_group": same_group.astype(np.float32),
        "slot": slot,
        "side": SPHERE_SIDE, "centre": SPHERE_CENTRE,
    }


def allocators(nc, ctx):
    def sb(name, shape, dt=FP32):
        return ctx.enter_context(nc.sbuf_tensor(name, shape, dt))

    def ps(name, shape):
        return ctx.enter_context(nc.psum_tensor(name, shape, FP32))

    def sem(name):
        return ctx.enter_context(nc.semaphore(name))

    return sb, ps, sem


def used(n):
    return not isinstance(n, int) or n > 0


def primed(engine, sems, n):
    for s in sems:
        engine.sem_inc(s, n)


def project(nc, T, Y):
    with ExitStack() as ctx:
        sb, ps, sem = allocators(nc, ctx)
        GT = CPG * FH
        x = sb("p_x", [P, B * C * FH, W])
        xh = sb("p_xh", [P, B * C * FH, W], BF16)
        xl = sb("p_xl", [P, B * C * FH, W], BF16)
        stats = sb("p_stats", [P, B * GROUPS, GT * 6])
        mv = sb("p_mv", [P, B * GROUPS, 2])
        mean = sb("p_mean", [P, B * GROUPS])
        dev = sb("p_dev", [P, B * GROUPS])
        dev2 = sb("p_dev2", [P, B * GROUPS])
        var = sb("p_var", [P, B * GROUPS])
        vare = sb("p_vare", [P, B * GROUPS])
        std = sb("p_std", [P, B * GROUPS])
        rstd = sb("p_rstd", [P, B * GROUPS])
        shift = sb("p_shift", [P, B * GROUPS])
        ones = sb("p_ones", [P, P])
        zero = sb("p_zero", [2 * PAD * C, QKV])
        w = [sb(f"p_w{s}", [P, FH, QKV]) for s in range(2)]
        wh = [sb(f"p_wh{s}", [P, FH, QKV], BF16) for s in range(2)]
        wl = [sb(f"p_wl{s}", [P, FH, QKV], BF16) for s in range(2)]
        bias = [sb(f"p_bias{s}", [P, 2, QKV // 2]) for s in range(2)]
        WT = W // P
        y = [sb(f"p_y{s}", [P, 2, QKV // 2]) for s in range(WT)]
        acc = [ps(f"p_acc{s}", [P, 2, 512]) for s in range(WT)]

        x_in = [sem(f"p_x_in{k}") for k in range(B * GROUPS)]
        w_in = [sem(f"p_w_in{s}") for s in range(2)]
        bias_in = [sem(f"p_bias_in{s}") for s in range(2)]
        w_split = sem("p_w_split")
        wh_done = sem("p_wh_done")
        ones_set = sem("p_ones_set")
        zero_set = sem("p_zero_set")
        zero_out = sem("p_zero_out")
        tile_stats = sem("p_tile_stats")
        group_stats = sem("p_group_stats")
        stat_sums = sem("p_stat_sums")
        dve = sem("p_dve")
        std_ready = sem("p_std_ready")
        normed = sem("p_normed")
        x_hi = sem("p_x_hi")
        x_lo = sem("p_x_lo")
        acc_full = [sem(f"p_acc_full{s}") for s in range(2)]
        y_ready = [sem(f"p_y_ready{s}") for s in range(WT)]
        y_out = [sem(f"p_y_out{s}") for s in range(WT)]
        ORDER = [(b, g) for g in range(GROUPS) for b in range(B)]

        block = ctx.enter_context(nc.Block())

        @block.sync
        def _(sp):
            primed(sp, y_out, 1)
            for k, (b, g) in enumerate(ORDER):
                t0 = (b * C + g * CPG) * FH
                sp.dma_start(x[:, t0:t0 + GT, :],
                             T["x"][b, g * CPG:(g + 1) * CPG].rearrange("c (f p) w -> p (c f) w", p=P)).then_inc(x_in[k], 16)
            sp.wait_ge(zero_set, 1)
            for b in range(B):
                sp.dma_start(Y[b, 0:PAD].rearrange("w c f -> (w c) f"), zero[0:PAD * C]).then_inc(zero_out, 16)
                for r0 in range(PAD + W, YROWS, 2 * PAD):
                    n = min(2 * PAD, YROWS - r0)
                    sp.dma_start(Y[b, r0:r0 + n].rearrange("w c f -> (w c) f"), zero[0:n * C]).then_inc(zero_out, 16)
            with sp.Fori(0, C // 2) as i:
                for cc in range(2):
                    for b in range(B):
                        for t in range(WT):
                            sp.wait_ge(y_ready[t], 1 + (i * 2 + cc) * B + b + 1)
                            sp.dma_start(Y[b, PAD + t * P:PAD + (t + 1) * P, bass.ds(i * 2 + cc, 1)].rearrange("w a f -> w (a f)"),
                                         y[t][:].rearrange("p a n -> p (a n)")).then_inc(y_out[t], 16)
            for t in range(WT):
                sp.wait_ge(y_out[t], 1 + 16 * B * C)
            sp.wait_ge(zero_out, 16 * B * (1 + len(range(PAD + W, YROWS, 2 * PAD))))

        @block.scalar
        def _(act):
            for cc in range(2):
                act.dma_start(w[cc][:], T["w_qkv"][cc].rearrange("(h p) n -> p h n", p=P)).then_inc(w_in[cc], 16)
                act.dma_start(bias[cc][:], T["b_qkv"][cc:cc + 1].rearrange("a (h n) -> a h n", h=2)
                              .broadcast_to([P, 2, QKV // 2])).then_inc(bias_in[cc], 16)
            act.wait_ge(dve, 3)
            nc.scalar.activation(std[:], vare[:], ACT.Sqrt).then_inc(std_ready, 1)
            for k, (b, g) in enumerate(ORDER):
                t0 = (b * C + g * CPG) * FH
                act.wait_ge(normed, k + 1)
                nc.scalar.activation(xh[:, t0:t0 + GT, :], x[:, t0:t0 + GT, :], ACT.Copy).then_inc(x_hi, 1)
            def high_part(i, cc):
                act.wait_ge(w_in[cc], 16 * (i + 1))
                act.wait_ge(acc_full[cc], 1 + i * B * WT)
                nc.scalar.activation(wh[cc][:], w[cc][:], ACT.Copy).then_inc(wh_done, 1)

            for cc in range(2):
                high_part(0, cc)
            with act.Fori(1, C // 2) as i:
                for cc in range(2):
                    act.wait_ge(w_split, 2 * i + cc - 1)
                    act.dma_start(w[cc][:], T["w_qkv"][bass.ds(2 * i + cc, 1)].rearrange("a (h p) n -> p (a h) n", p=P)).then_inc(w_in[cc], 16)
                    act.wait_ge(y_ready[WT - 1], 1 + B * (2 * i + cc - 1))
                    act.dma_start(bias[cc][:], T["b_qkv"][bass.ds(2 * i + cc, 1)].rearrange("a (h n) -> a h n", h=2)
                                  .broadcast_to([P, 2, QKV // 2])).then_inc(bias_in[cc], 16)
                    high_part(i, cc)

        @block.gpsimd
        def _(pool):
            nc.gpsimd.memset(ones[:], 1.0 / P).then_inc(ones_set, 1)
            nc.gpsimd.memset(zero[:], 0.0).then_inc(zero_set, 1)
            with pool.Fori(0, C // 2) as i:
                for cc in range(2):
                    pool.wait_ge(wh_done, 2 * i + cc + 1)
                    nc.gpsimd.tensor_tensor(wl[cc][:], w[cc][:], wh[cc][:], ALU.subtract).then_inc(w_split, 1)

        @block.vector
        def _(v):
            primed(v, y_ready, 1)
            for k, (b, g) in enumerate(ORDER):
                t0 = (b * C + g * CPG) * FH
                v.wait_ge(x_in[k], 16)
                for t in range(GT):
                    nc.vector.bn_stats(stats[:, b * GROUPS + g, 6 * t:6 * t + 6], x[:, t0 + t, :]).then_inc(tile_stats, 1)
            v.wait_ge(tile_stats, B * GROUPS * GT)
            for k in range(B * GROUPS):
                nc.vector.bn_aggr(mv[:, k, :], stats[:, k, :]).then_inc(group_stats, 1)
            v.wait_ge(stat_sums, 1)
            nc.vector.tensor_copy(mean[:], acc[WT - 1][:, 0, 0:B * GROUPS]).then_inc(dve, 1)
            nc.vector.tensor_tensor(dev[:], mv[:, :, 0], acc[WT - 1][:, 0, 0:B * GROUPS], ALU.subtract).then_inc(group_stats, 1)
            v.wait_ge(group_stats, B * GROUPS + 1)
            nc.vector.tensor_tensor(dev2[:], dev[:], dev[:], ALU.mult).then_inc(group_stats, 1)
            v.wait_ge(stat_sums, 2)
            nc.vector.tensor_copy(var[:], acc[WT - 1][:, 0, B * GROUPS:2 * B * GROUPS]).then_inc(dve, 1)
            v.wait_ge(dve, 2)
            nc.vector.tensor_scalar(vare[:], var[:], 1e-5, None, ALU.add).then_inc(dve, 1)
            v.wait_ge(std_ready, 1)
            nc.vector.reciprocal(rstd[:], std[:]).then_inc(dve, 1)
            v.wait_ge(dve, 4)
            nc.vector.scalar_tensor_tensor(shift[:], mean[:], -1.0, rstd[:], ALU.mult, ALU.mult).then_inc(dve, 1)
            v.wait_ge(dve, 5)
            for k, (b, g) in enumerate(ORDER):
                t0, kg = (b * C + g * CPG) * FH, b * GROUPS + g
                nc.vector.tensor_scalar(x[:, t0:t0 + GT, :], x[:, t0:t0 + GT, :], rstd[:, kg:kg + 1], shift[:, kg:kg + 1],
                                        ALU.mult, ALU.add).then_inc(normed, 1)
            for k, (b, g) in enumerate(ORDER):
                t0 = (b * C + g * CPG) * FH
                v.wait_ge(x_hi, k + 1)
                nc.vector.tensor_tensor(xl[:, t0:t0 + GT, :], x[:, t0:t0 + GT, :], xh[:, t0:t0 + GT, :], ALU.subtract).then_inc(x_lo, 1)
            with v.Fori(0, C // 2) as i:
                for cc in range(2):
                    v.wait_ge(bias_in[cc], 16 * (i + 1))
                    for b in range(B):
                        for t in range(WT):
                            n = (i * 2 + cc) * B + b
                            v.wait_ge(acc_full[cc], 1 + (i * B + b) * WT + t + 1)
                            v.wait_ge(y_out[t], 1 + 16 * n)
                            nc.vector.tensor_tensor(y[t][:], acc[t][:, :, 0:QKV // 2], bias[cc][:], ALU.add).then_inc(y_ready[t], 1)

        @block.tensor
        def _(pe):
            primed(pe, acc_full, 1)
            pe.wait_ge(ones_set, 1)
            pe.wait_ge(group_stats, B * GROUPS)
            nc.tensor.matmul(acc[WT - 1][:, 0, 0:B * GROUPS], ones[:], mv[:, :, 0], start=True, stop=True)
            nc.tensor.matmul(acc[WT - 1][:, 0, B * GROUPS:2 * B * GROUPS], ones[:], mv[:, :, 1], start=True, stop=False).then_inc(stat_sums, 1)
            pe.wait_ge(group_stats, B * GROUPS + 2)
            nc.tensor.matmul(acc[WT - 1][:, 0, B * GROUPS:2 * B * GROUPS], ones[:], dev2[:], start=False, stop=True).then_inc(stat_sums, 1)
            with pe.Fori(0, C // 2) as i:
                for cc in range(2):
                    pe.wait_ge(w_split, 2 * i + cc + 1)
                    for b in range(B):
                        pe.wait_ge(x_lo, i * 2 + b + 1)
                        for t in range(WT):
                            n = (i * 2 + cc) * B + b
                            pe.wait_ge(y_ready[t], 1 + n)
                            for half in range(2):
                                cols = slice(half * (QKV // 2), (half + 1) * (QKV // 2))
                                for fh in range(FH):
                                    tile = bass.ds(i * (2 * FH) + (b * C + cc) * FH + fh, 1)
                                    hi = xh[:, tile, t * P:(t + 1) * P].rearrange("p a n -> p (a n)")
                                    lo = xl[:, tile, t * P:(t + 1) * P].rearrange("p a n -> p (a n)")
                                    out = acc[t][:, half, 0:QKV // 2]
                                    nc.tensor.matmul(out, hi, wh[cc][:, fh, cols], start=fh == 0, stop=False)
                                    nc.tensor.matmul(out, hi, wl[cc][:, fh, cols], start=False, stop=False)
                                    last = nc.tensor.matmul(out, lo, wh[cc][:, fh, cols], start=False, stop=fh == FH - 1)
                            last.then_inc(acc_full[cc], 1)


def convolve(nc, T, Y, QK, V):
    with ExitStack() as ctx:
        sb, ps, sem = allocators(nc, ctx)
        KF = 2 * FH
        band = sb("c_band", [P, 3, C * OW])
        qk = sb("c_qk", [P, KF, C, WPAD])
        qk_bias = sb("c_qk_bias", [P, 2, FH, C])
        v_bias = sb("c_v_bias", [C * OW, 1])
        cos = sb("c_cos", [P, 2, W])
        sin = sb("c_sin", [P, 2, W])
        win = [sb(f"c_win{s}", [P, QKV]) for s in range(WIN_UNROLL)]
        vout = [sb(f"c_v{s}", [C * OW, F]) for s in range(WIN_UNROLL)]
        turned = [sb(f"c_turned{s}", [P, KF, W]) for s in range(2)]
        hi = [sb(f"c_hi{s}", [P, KF, W], BF16) for s in range(2)]
        lo = [sb(f"c_lo{s}", [P, KF, W], BF16) for s in range(2)]
        acc_qk = [ps(f"c_acc_qk{s}", [P, 512]) for s in range(WIN_UNROLL)]
        acc_v = [ps(f"c_acc_v{s}", [P, 512]) for s in range(WIN_UNROLL)]

        band_zero = sem("c_band_zero")
        consts_in = sem("c_consts_in")
        win_in = [sem(f"c_win_in{s}") for s in range(WIN_UNROLL)]
        acc_full = [sem(f"c_acc_full{s}") for s in range(WIN_UNROLL)]
        qk_read = [sem(f"c_qk_read{s}") for s in range(WIN_UNROLL)]
        v_read = [sem(f"c_v_read{s}") for s in range(WIN_UNROLL)]
        v_stored = [sem(f"c_v_stored{s}") for s in range(WIN_UNROLL)]
        turn_done = sem("c_turn_done")
        sin_done = sem("c_sin_done")
        cos_done = sem("c_cos_done")
        rope_done = sem("c_rope_done")
        hi_done = sem("c_hi_done")
        lo_done = sem("c_lo_done")
        hi_stored = [sem(f"c_hi_stored{s}") for s in range(2)]
        lo_stored = [sem(f"c_lo_stored{s}") for s in range(2)]
        TURNS = WINDOWS // WIN_UNROLL
        NCONST = KW + 2 * FH + 1 + 2
        block = ctx.enter_context(nc.Block())

        @block.sync
        def _(sp):
            for w in range(KW):
                sp.dma_start(band[w * C:(w + 1) * C].rearrange("c k (o w) -> c (k o) w", w=OW),
                             T["taps"][:, :, KW - 1 - w:KW - 1 - w + OW]).then_inc(consts_in, 16)
            for kind in range(2):
                for fh in range(FH):
                    sp.dma_start(qk_bias[:, kind, fh, :],
                                 T["qkv_conv_b"][kind:kind + 1].broadcast_to([P, C])).then_inc(consts_in, 16)
            sp.dma_start(v_bias[:],
                         T["qkv_conv_b"][2].rearrange("(o w a) -> o w a", w=1, a=1).broadcast_to([C, OW, 1])).then_inc(consts_in, 16)
            sp.dma_start(cos[:], T["cos"]).then_inc(consts_in, 16)
            sp.dma_start(sin[:], T["sin"]).then_inc(consts_in, 16)
            for b in range(B):
                with sp.Fori(0, WINDOWS // WIN_UNROLL) as i:
                    for s in range(WIN_UNROLL):
                        sp.wait_ge(acc_full[s], 1 + b * TURNS + i)
                        sp.dma_start(win[s][:], Y[b, bass.ds((i * WIN_UNROLL + s) * OW, KW)].rearrange("w c f -> (w c) f")
                                     ).then_inc(win_in[s], 16)

        @block.tensor
        def _(pe):
            primed(pe, acc_full, 1)
            pe.wait_ge(consts_in, 16 * NCONST)
            for b in range(B):
                with pe.Fori(0, WINDOWS // WIN_UNROLL) as i:
                    for s in range(WIN_UNROLL):
                        pe.wait_ge(win_in[s], 16 * (b * TURNS + i + 1))
                        pe.wait_ge(qk_read[s], 1 + b * TURNS + i)
                        pe.wait_ge(v_read[s], 1 + b * TURNS + i)
                        for kf in range(KF):
                            nc.tensor.matmul(acc_qk[s][:, kf * C * OW:(kf + 1) * C * OW], win[s][:, kf * P:(kf + 1) * P],
                                             band[:, kf // FH, :], start=True, stop=True)
                        nc.tensor.matmul(acc_v[s][0:C * OW, 0:F], band[:, 2, :], win[s][:, 2 * F:3 * F],
                                         start=True, stop=True).then_inc(acc_full[s], 1)

        @block.vector
        def _(v):
            primed(v, qk_read, 1)
            v.wait_ge(consts_in, 16 * NCONST)
            for b in range(B):
                if b:
                    v.wait_ge(lo_done, b * C)
                with v.Fori(0, WINDOWS // WIN_UNROLL) as i:
                    for s in range(WIN_UNROLL):
                        v.wait_ge(acc_full[s], 1 + b * TURNS + i + 1)
                        w0 = (i * WIN_UNROLL + s) * OW
                        nc.vector.tensor_tensor(
                            qk[:, :, :, bass.ds(w0, OW)].rearrange("p a o w -> p (a o) w"),
                            acc_qk[s][:, 0:KF * C * OW].rearrange("p (a w) -> p a w", w=OW),
                            qk_bias[:].rearrange("p k f (o w) -> p (k f o) w", w=1).broadcast_to([P, KF * C, OW]),
                            ALU.add).then_inc(qk_read[s], 1)
                for s in range(WIN_UNROLL):
                    v.wait_ge(qk_read[s], 1 + (b + 1) * TURNS)
                for o in range(C):
                    n = b * C + o
                    if n >= 2:
                        v.wait_ge(rope_done, n - 1)
                    nc.vector.stream_shuffle(turned[n % 2][:], qk[:, :, o, 0:W], [d ^ 1 for d in range(32)]).then_inc(turn_done, 1)
                    v.wait_ge(sin_done, n + 1)
                    v.wait_ge(cos_done, n + 1)
                    nc.vector.tensor_tensor(qk[:, :, o, 0:W], qk[:, :, o, 0:W], turned[n % 2][:], ALU.add).then_inc(rope_done, 1)
                    v.wait_ge(hi_done, n + 1)
                    if n >= 2:
                        v.wait_ge(lo_stored[n % 2], 16 * (n // 2))
                    nc.vector.tensor_tensor(lo[n % 2][:], qk[:, :, o, 0:W], hi[n % 2][:], ALU.subtract).then_inc(lo_done, 1)

        @block.gpsimd
        def _(pool):
            for b in range(B):
                for o in range(C):
                    n = b * C + o
                    tab = [t[:].rearrange("p k (a w) -> p k a w", a=1).broadcast_to([P, 2, FH, W]) for t in (cos, sin)]
                    pool.wait_ge(turn_done, n + 1)
                    mine = qk[:, :, o, 0:W].rearrange("p (k f) w -> p k f w", k=2)
                    nc.gpsimd.tensor_tensor(mine, mine, tab[0], ALU.mult).then_inc(cos_done, 1)
                    other = turned[n % 2][:].rearrange("p (k f) w -> p k f w", k=2)
                    nc.gpsimd.tensor_tensor(other, other, tab[1], ALU.mult).then_inc(sin_done, 1)

        @block.scalar
        def _(act):
            primed(act, v_read + v_stored, 1)
            act.wait_ge(consts_in, 16 * NCONST)
            for b in range(B):
                with act.Fori(0, WINDOWS // WIN_UNROLL) as i:
                    for s in range(WIN_UNROLL):
                        act.wait_ge(acc_full[s], 1 + b * TURNS + i + 1)
                        act.wait_ge(v_stored[s], 1 + 16 * (b * TURNS + i))
                        nc.scalar.activation(vout[s][:], acc_v[s][0:C * OW, 0:F], ACT.Identity, bias=v_bias[:]).then_inc(v_read[s], 1)
                        act.wait_ge(v_read[s], 1 + b * TURNS + i + 1)
                        act.dma_start(V[b, :, bass.ds((i * WIN_UNROLL + s) * OW, OW), :], vout[s][:]).then_inc(v_stored[s], 16)
                for o in range(C):
                    n = b * C + o
                    act.wait_ge(rope_done, n + 1)
                    if n >= 2:
                        act.wait_ge(hi_stored[n % 2], 16 * (n // 2))
                        act.wait_ge(lo_done, n - 1)
                    nc.scalar.activation(hi[n % 2][:], qk[:, :, o, 0:W], ACT.Copy).then_inc(hi_done, 1)
                    act.wait_ge(hi_done, n + 1)
                    act.dma_start(QK[b, o, 0].rearrange("k (f p) w -> p (k f) w", p=P), hi[n % 2][:]).then_inc(hi_stored[n % 2], 16)
                    act.wait_ge(lo_done, n + 1)
                    act.dma_start(QK[b, o, 1].rearrange("k (f p) w -> p (k f) w", p=P), lo[n % 2][:]).then_inc(lo_stored[n % 2], 16)
            for s in range(WIN_UNROLL):
                act.wait_ge(v_stored[s], 1 + 16 * B * TURNS)
            for s in range(2):
                act.wait_ge(hi_stored[s], 16 * B * C // 2)
                act.wait_ge(lo_stored[s], 16 * B * C // 2)


def attend(nc, T, QK, V, Z):
    with ExitStack() as ctx:
        sb, ps, sem = allocators(nc, ctx)
        QT = W // P
        STEPS = HEADS * QT
        CHANNELS = 2
        UNITS = B * CHANNELS
        ITERATIONS = C // CHANNELS
        DV = DH + 1
        KROWS = 3 * DH
        SHIFTED = KROWS + 2
        PROBS = 2
        PARTS = 4
        ident = sb("a_ident", [P, P])
        ident16 = sb("a_ident16", [P, P], BF16)
        o = [sb(f"a_o{s}", [P, QT, F]) for s in range(2)]
        q = [sb(f"a_q{u}", [SHIFTED, HEADS, W], BF16) for u in range(UNITS)]
        k = [sb(f"a_k{u}", [SHIFTED, HEADS, W], BF16) for u in range(UNITS)]
        v = [sb(f"a_v{s}", [P, QT, F]) for s in range(2)]
        vp = [sb(f"a_vp{s}", [P, QT * HEADS, DV + DH], BF16) for s in range(2)]
        wo = [sb(f"a_wo{s}", [P, FH, F]) for s in range(CHANNELS)]
        bo = [sb(f"a_bo{s}", [P, FH]) for s in range(CHANNELS)]
        negmax = [sb(f"a_negmax{u}", [P, STEPS]) for u in range(UNITS)]
        maxparts = [sb(f"a_maxparts{u}", [P, 2 * HEADS, QT], BF16) for u in range(UNITS)]
        maxrows = [sb(f"a_maxrows{u}", [2 * HEADS, W], BF16) for u in range(UNITS)]
        prob = [sb(f"a_prob{s}", [P, QT, W]) for s in range(PROBS)]
        ph = [sb(f"a_ph{s}", [P, QT, W], BF16) for s in range(PARTS)]
        pl = [sb(f"a_pl{s}", [P, QT, W], BF16) for s in range(PARTS)]
        inverse = [sb(f"a_inverse{s}", [P, QT]) for s in range(2)]
        oT = sb("a_oT", [P, FH, W])
        z = [sb(f"a_z{s}", [P, W]) for s in range(FH)]
        row = [ps(f"a_row{s}", [P, W]) for s in range(2)]
        col = [ps(f"a_col{s}", [P, W]) for s in range(2)]
        mix = [ps(f"a_mix{s}", [P, QT, DV]) for s in range(2)]
        turned = ps("a_turned", [2 * HEADS, W])
        out = ps("a_out", [P, W])

        const_in = sem("a_const_in")
        ident16_set = sem("a_ident16_set")
        ones_set = sem("a_ones_set")
        qk_in = [sem(f"a_qk_in{u}") for u in range(UNITS)]
        max_in = [sem(f"a_max_in{u}") for u in range(UNITS)]
        v_in = [sem(f"a_v_in{s}") for s in range(2)]
        wo_in = [sem(f"a_wo_in{s}") for s in range(CHANNELS)]
        v_hi = sem("a_v_hi")
        v_lo = sem("a_v_lo")
        row_full = sem("a_row_full")
        max_done = sem("a_max_done")
        max_hi = sem("a_max_hi")
        max_split = sem("a_max_split")
        max_turned = sem("a_max_turned")
        max_kept = sem("a_max_kept")
        col_full = sem("a_col_full")
        exp_done = sem("a_exp_done")
        hi_act = sem("a_hi_act")
        hi_dve = sem("a_hi_dve")
        lo_dve = sem("a_lo_dve")
        lo_pool = sem("a_lo_pool")
        mixed = sem("a_mixed")
        inverted = sem("a_inverted")
        normed = sem("a_normed")
        out_full = sem("a_out_full")
        out_kept = sem("a_out_kept")
        z_stored = [sem(f"a_z_stored{s}") for s in range(FH)]
        QK_LOADS = 6
        HI_ACT, LO_DVE, LO_POOL = 3, 1, 3

        SPLIT = STEPS
        EXP = STEPS + 7
        MIX = EXP + 2 * QT + 1
        NORM = MIX + QT
        TAIL = NORM + (HEADS - 1) * QT + 3
        BODY = UNITS * STEPS
        assert TAIL + 2 * 2 * FH + 2 < BODY

        def pipeline(engine, ops):
            at = [[f for p, f in ops if p == t] for t in range(2 * BODY)]
            for t in range(BODY):
                for f in at[t]:
                    f(0)
            with engine.Fori(0, ITERATIONS - 1) as i:
                for t in range(BODY):
                    for f in at[BODY + t]:
                        f(i)
                    for f in at[t]:
                        f(i + 1)
            for t in range(BODY, 2 * BODY):
                for f in at[t]:
                    f(ITERATIONS - 1)

        def steps(first, emit, kinds=range(QT)):
            return [(STEPS * u + first + t, lambda i, u=u, t=t: emit(i, u, t // QT, t % QT))
                    for u in range(UNITS) for t in range(STEPS) if t % QT in kinds]

        def heads(first, emit):
            return [(STEPS * u + first + QT * h, lambda i, u=u, h=h: emit(i, u, h)) for u in range(UNITS) for h in range(HEADS)]

        def units(first, emit):
            return [(STEPS * u + first, lambda i, u=u: emit(i, u)) for u in range(UNITS)]

        def tails(first, emit, kinds=range(2 * FH)):
            return [(STEPS * u + first + 2 * j, lambda i, u=u, j=j: emit(i, u, j)) for u in range(UNITS) for j in kinds]

        block = ctx.enter_context(nc.Block())

        @block.sync
        def _(sp):
            sp.dma_start(ident[:], T["ident"]).then_inc(const_in, 16)

            def load(i):
                for u in range(UNITS):
                    s, c, unit = u % B, CHANNELS * i + u // B, UNITS * i + u
                    if used(unit - UNITS + 1):
                        sp.wait_ge(col_full, STEPS * (unit - UNITS + 1))
                    src = QK[s, bass.ds(c, 1)].rearrange("a p k (h d) w -> p k (a d) h w", d=DH)
                    for r, (qpart, kpart) in enumerate(((0, 0), (0, 1), (1, 0))):
                        sp.dma_start(q[u][r * DH:(r + 1) * DH], src[qpart, 0]).then_inc(qk_in[u], 16)
                        sp.dma_start(k[u][r * DH:(r + 1) * DH], src[kpart, 1]).then_inc(qk_in[u], 16)
                    if used(unit - 1):
                        sp.wait_ge(v_lo, unit - 1)
                    sp.dma_start(v[u % 2][:], V[s, bass.ds(c, 1), 0:W].rearrange("a (t p) f -> p (a t) f", p=P)).then_inc(v_in[u % 2], 16)
                    if s == B - 1:
                        if used(unit - UNITS + 1):
                            sp.wait_ge(out_kept, 2 * FH * (unit - UNITS + 1))
                        sp.dma_start(wo[u // B][:], T["w_o"][bass.ds(c, 1)].rearrange("a (h p) f -> p (a h) f", p=P)).then_inc(wo_in[u // B], 16)
                        sp.dma_start(bo[u // B][:], T["b_o"][bass.ds(c, 1)].rearrange("a p h -> p (a h)")).then_inc(wo_in[u // B], 16)

            load(0)
            with sp.Fori(1, ITERATIONS) as i:
                load(i)

        @block.tensor
        def _(pe):
            pe.wait_ge(const_in, 16)
            pe.wait_ge(ident16_set, 1)
            pe.wait_ge(ones_set, UNITS)

            def row_scores(i, u, h, qt):
                step = BODY * i + STEPS * u + QT * h + qt
                if h == 0 and qt == 0:
                    pe.wait_ge(qk_in[u], 16 * QK_LOADS * (i + 1))
                if used(step - 1):
                    pe.wait_ge(max_done, step - 1)
                nc.tensor.matmul(row[qt % 2][:], q[u][0:KROWS, h, qt * P:(qt + 1) * P], k[u][0:KROWS, h, :],
                                 start=True, stop=True).then_inc(row_full, 1)

            def turn_max(i, u):
                unit = UNITS * i + u
                pe.wait_ge(max_split, unit + 1)
                if used(unit):
                    pe.wait_ge(max_kept, unit)
                for qt in range(QT):
                    last = nc.tensor.matmul(turned[:, qt * P:(qt + 1) * P], maxparts[u][:, :, qt], ident16[:], start=True, stop=True)
                last.then_inc(max_turned, 1)

            def col_scores(i, u, h, kt):
                step = BODY * i + STEPS * u + QT * h + kt
                if h == 0 and kt == 0:
                    pe.wait_ge(max_in[u], 16 * (i + 1))
                if used(step - 1):
                    pe.wait_ge(exp_done, step - 1)
                nc.tensor.matmul(col[kt % 2][:], k[u][:, h, kt * P:(kt + 1) * P], q[u][:, h, :],
                                 start=True, stop=True).then_inc(col_full, 1)

            def mix_step(i, u, h, qt):
                head = HEADS * (UNITS * i + u) + h
                if qt == 0:
                    if h == 0:
                        pe.wait_ge(v_lo, UNITS * i + u + 1)
                    pe.wait_ge(lo_dve, LO_DVE * (head + 1))
                    pe.wait_ge(lo_pool, LO_POOL * (head + 1))
                    if used(head - 1):
                        pe.wait_ge(normed, head - 1)
                at = slice(qt * P, (qt + 1) * P)
                for kt in range(QT):
                    vpart = vp[u % 2][:, kt * HEADS + h, :]
                    nc.tensor.matmul(mix[h % 2][:, qt, :], ph[h % PARTS][:, kt, at], vpart[:, 0:DV], start=kt == 0, stop=False)
                    nc.tensor.matmul(mix[h % 2][:, qt, 0:DH], ph[h % PARTS][:, kt, at], vpart[:, DV:], start=False, stop=False)
                    last = nc.tensor.matmul(mix[h % 2][:, qt, :], pl[h % PARTS][:, kt, at], vpart[:, 0:DV],
                                            start=False, stop=kt == QT - 1)
                last.then_inc(mixed, 1)

            def tail(i, u, j):
                unit = UNITS * i + u
                if j == 0:
                    pe.wait_ge(normed, HEADS * (unit + 1))
                if used(2 * FH * unit + j):
                    pe.wait_ge(out_kept, 2 * FH * unit + j)
                if j < FH:
                    for qt in range(QT):
                        last = nc.tensor.transpose(out[:, qt * P:(qt + 1) * P], o[u % 2][:, qt, j * P:(j + 1) * P], ident[:])
                else:
                    fo = j - FH
                    if fo == 0:
                        pe.wait_ge(wo_in[u // B], 32 * (i + 1))
                    for fh in range(FH):
                        last = nc.tensor.matmul(out[:], wo[u // B][:, fh, fo * P:(fo + 1) * P], oT[:, fh, :],
                                                start=fh == 0, stop=fh == FH - 1)
                last.then_inc(out_full, 1)

            pipeline(pe, steps(0, row_scores) + units(SPLIT + 1, turn_max) + steps(EXP, col_scores) + steps(MIX, mix_step)
                     + tails(TAIL, tail))

        @block.vector
        def _(ve):
            ve.wait_ge(const_in, 16)
            nc.vector.tensor_copy(ident16[:], ident[:]).then_inc(ident16_set, 1)
            for u in range(UNITS):
                nc.vector.memset(k[u][KROWS:SHIFTED], 1.0).then_inc(ones_set, 1)
            for s in range(2):
                nc.vector.memset(vp[s][:, :, DH:DV], 1.0).then_inc(ones_set, 1)

            def row_max(i, u, h, qt):
                step = BODY * i + STEPS * u + QT * h + qt
                ve.wait_ge(row_full, step + 1)
                nc.vector.reduce_max(negmax[u][:, QT * h + qt:QT * h + qt + 1], row[qt % 2][:], AX.X, negate=True).then_inc(max_done, 1)

            def split_max(i, u):
                unit = UNITS * i + u
                high, low = (maxparts[u][:, n * HEADS:(n + 1) * HEADS, :].rearrange("p h t -> p (h t)") for n in range(2))
                ve.wait_ge(max_done, STEPS * (unit + 1))
                nc.vector.tensor_copy(high, negmax[u][:]).then_inc(max_hi, 1)
                ve.wait_ge(max_hi, unit + 1)
                nc.vector.tensor_tensor(low, negmax[u][:], high, ALU.subtract).then_inc(max_split, 1)

            def high_part(i, u, h, kt):
                head = HEADS * (UNITS * i + u) + h
                ve.wait_ge(exp_done, QT * head + kt + 1)
                nc.vector.tensor_copy(ph[h % PARTS][:, kt, :], prob[h % PROBS][:, kt, :]).then_inc(hi_dve, 1)

            def low_part(i, u, h, kt):
                head = HEADS * (UNITS * i + u) + h
                ve.wait_ge(hi_act, HI_ACT * head + kt + 1)
                nc.vector.tensor_tensor(pl[h % PARTS][:, kt, :], prob[h % PROBS][:, kt, :], ph[h % PARTS][:, kt, :],
                                        ALU.subtract).then_inc(lo_dve, 1)

            def invert(i, u, h):
                ve.wait_ge(mixed, QT * (HEADS * (UNITS * i + u) + h + 1))
                nc.vector.reciprocal(inverse[h % 2][:].unsqueeze(2), mix[h % 2][:, :, DH:DV]).then_inc(inverted, 1)

            def norm(i, u, h):
                unit, head = UNITS * i + u, HEADS * (UNITS * i + u) + h
                if h == 0 and used(unit - 1):
                    ve.wait_ge(out_full, 2 * FH * (unit - 2) + FH)
                ve.wait_ge(inverted, head + 1)
                nc.vector.tensor_tensor(o[u % 2][:, :, h * DH:(h + 1) * DH], mix[h % 2][:, :, 0:DH],
                                        inverse[h % 2][:].unsqueeze(2).broadcast_to([P, QT, DH]), ALU.mult).then_inc(normed, 1)

            pipeline(ve, steps(0, row_max) + units(SPLIT, split_max) + steps(EXP + 1, high_part, kinds=(3,))
                     + steps(EXP + 2, low_part, kinds=(0,)) + heads(NORM, invert) + heads(NORM + 1, norm))

        @block.scalar
        def _(act):
            act.wait_ge(ones_set, UNITS + 2)

            def v_high(i, u):
                unit = UNITS * i + u
                act.wait_ge(v_in[u % 2], 16 * (UNITS // 2 * i + u // 2 + 1))
                if used(unit - 1):
                    act.wait_ge(mixed, STEPS * (unit - 1))
                nc.scalar.activation(vp[u % 2][:, :, 0:DH], v[u % 2][:].rearrange("p t (h d) -> p (t h) d", d=DH), ACT.Copy).then_inc(v_hi, 1)

            def keep_max(i, u):
                unit = UNITS * i + u
                act.wait_ge(max_turned, unit + 1)
                nc.scalar.activation(maxrows[u][:], turned[:], ACT.Copy).then_inc(max_kept, 1)

            def load_max(i, u):
                act.wait_ge(max_kept, UNITS * i + u + 1)
                act.dma_start(q[u][KROWS:SHIFTED], maxrows[u][:]).then_inc(max_in[u], 16)

            def exp(i, u, h, kt):
                head = HEADS * (UNITS * i + u) + h
                if kt == 0:
                    if used(head - PROBS + 1):
                        act.wait_ge(lo_dve, LO_DVE * (head - PROBS + 1))
                        act.wait_ge(lo_pool, LO_POOL * (head - PROBS + 1))
                    if used(head - PARTS + 1):
                        act.wait_ge(mixed, QT * (head - PARTS + 1))
                act.wait_ge(col_full, QT * head + kt + 1)
                nc.scalar.activation(prob[h % PROBS][:, kt, :], col[kt % 2][:], ACT.Exp).then_inc(exp_done, 1)

            def high_part(i, u, h, kt):
                head = HEADS * (UNITS * i + u) + h
                act.wait_ge(exp_done, QT * head + kt + 1)
                nc.scalar.activation(ph[h % PARTS][:, kt, :], prob[h % PROBS][:, kt, :], ACT.Copy).then_inc(hi_act, 1)

            def keep_out(i, u, j):
                unit = UNITS * i + u
                act.wait_ge(out_full, 2 * FH * unit + j + 1)
                if j < FH:
                    nc.scalar.activation(oT[:, j, :], out[:], ACT.Copy).then_inc(out_kept, 1)
                else:
                    if used(unit):
                        act.wait_ge(z_stored[j - FH], 16 * unit)
                    nc.scalar.activation(z[j - FH][:], out[:], ACT.Identity, bias=bo[u // B][:, j - FH:j - FH + 1]).then_inc(out_kept, 1)

            def store_z(i, u, j):
                unit, fo = UNITS * i + u, j - FH
                act.wait_ge(out_kept, 2 * FH * unit + j + 1)
                act.dma_start(Z[u % B, fo * P:(fo + 1) * P, bass.ds(CHANNELS * i + u // B, 1)].rearrange("f a w -> f (a w)"),
                              z[fo][:]).then_inc(z_stored[fo], 16)

            pipeline(act, units(SPLIT + 2, keep_max) + units(SPLIT + 3, load_max) + units(EXP - 2, v_high) + steps(EXP, exp)
                     + steps(EXP + 1, high_part, kinds=(0, 1, 2))
                     + tails(TAIL + 1, keep_out) + tails(TAIL + 2, store_z, kinds=range(FH, 2 * FH)))
            for fo in range(FH):
                act.wait_ge(z_stored[fo], 16 * B * C)

        @block.gpsimd
        def _(pool):
            def v_low(i, u):
                pool.wait_ge(v_hi, UNITS * i + u + 1)
                nc.gpsimd.tensor_tensor(vp[u % 2][:, :, DV:], v[u % 2][:].rearrange("p t (h d) -> p (t h) d", d=DH),
                                        vp[u % 2][:, :, 0:DH], ALU.subtract).then_inc(v_lo, 1)

            def low_part(i, u, h, kt):
                head = HEADS * (UNITS * i + u) + h
                if kt < HI_ACT:
                    pool.wait_ge(hi_act, HI_ACT * head + kt + 1)
                else:
                    pool.wait_ge(hi_dve, head + 1)
                nc.gpsimd.tensor_tensor(pl[h % PARTS][:, kt, :], prob[h % PROBS][:, kt, :], ph[h % PARTS][:, kt, :],
                                        ALU.subtract).then_inc(lo_pool, 1)

            pipeline(pool, units(EXP - 1, v_low) + steps(EXP + 2, low_part, kinds=(1, 2, 3)))


def residual(nc, T, Z, X1, S):
    with ExitStack() as ctx:
        sb, ps, sem = allocators(nc, ctx)
        NB = F // KR
        U = 4
        wmix = sb("r_wmix", [P, P])
        bmix = sb("r_bmix", [P, 1])
        group = sb("r_group", [P, P])
        z = [sb(f"r_z{s}", [P, W]) for s in range(U)]
        x = [sb(f"r_x{s}", [P, W]) for s in range(U)]
        x1 = [sb(f"r_x1{s}", [P, W]) for s in range(U)]
        stats = sb("r_stats", [P, B, NB, 6])
        mv = sb("r_mv", [P, B, 2])
        small = sb("r_small", [P, 8, B])
        out = sb("r_out", [P, B, 2])
        acc = [ps(f"r_acc{s}", [P, W]) for s in range(U)]
        sums = ps("r_sums", [P, 2, B])

        consts_in = sem("r_consts_in")
        wzero = sem("r_wzero")
        z_in = [sem(f"r_z_in{s}") for s in range(U)]
        x_in = [sem(f"r_x_in{s}") for s in range(U)]
        acc_full = sem("r_acc_full")
        x1_ready = sem("r_x1_ready")
        stats_done = sem("r_stats_done")
        x1_stored = [sem(f"r_x1_stored{s}") for s in range(U)]
        aggregated = sem("r_aggregated")
        summed = sem("r_summed")
        dve = sem("r_dve")
        std_ready = sem("r_std_ready")
        s_stored = sem("r_s_stored")
        NCONST = 2 * KR + 1
        STORES = 3
        block = ctx.enter_context(nc.Block())

        def before(b, i, s):
            return b * NB + i * U + s


        @block.sync
        def _(sp):
            sp.wait_ge(wzero, 1)
            for r in range(KR):
                sp.dma_start(wmix[r * C:(r + 1) * C, r * C:(r + 1) * C], T["w_mix"]).then_inc(consts_in, 16)
                sp.dma_start(bmix[r * C:(r + 1) * C], T["b_mix"]).then_inc(consts_in, 16)
            sp.dma_start(group[:], T["same_group"]).then_inc(consts_in, 16)
            for b in range(B):
                with sp.Fori(0, NB // U) as i:
                    for s in range(U):
                        rows = bass.ds((i * U + s) * KR, KR)
                        sp.wait_ge(acc_full, U + before(b, i, s) - U + 1)
                        sp.dma_start(z[s][:], Z[b, rows].rearrange("h c w -> (h c) w")).then_inc(z_in[s], 16)
                        sp.wait_ge(x1_ready, U + before(b, i, s) - U + 1)
                        sp.dma_start(x[s][:],
                                     T["x"][b, :, rows].rearrange("c h w -> h c w")).then_inc(x_in[s], 16)

        @block.gpsimd
        def _(pool):
            nc.gpsimd.memset(wmix[:], 0.0).then_inc(wzero, 1)

        @block.tensor
        def _(pe):
            primed(pe, [acc_full], U)
            pe.wait_ge(consts_in, 16 * NCONST)
            for b in range(B):
                with pe.Fori(0, NB // U) as i:
                    for s in range(U):
                        pe.wait_ge(z_in[s], 16 * (b * (NB // U) + i + 1))
                        pe.wait_ge(x1_ready, U + before(b, i, s) - U + 1)
                        nc.tensor.matmul(acc[s][:], wmix[:], z[s][:], start=True, stop=True).then_inc(acc_full, 1)
            pe.wait_ge(aggregated, B)
            nc.tensor.matmul(sums[:, 0, :], group[:], mv[:, :, 0], start=True, stop=True)
            nc.tensor.matmul(sums[:, 1, :], group[:], mv[:, :, 1], start=True, stop=False).then_inc(summed, 1)
            pe.wait_ge(dve, 3)
            nc.tensor.matmul(sums[:, 1, :], group[:], small[:, 2, :], start=False, stop=True).then_inc(summed, 1)

        @block.vector
        def _(v):
            primed(v, [x1_ready], U)
            v.wait_ge(consts_in, 16 * NCONST)
            for b in range(B):
                with v.Fori(0, NB // U) as i:
                    for s in range(U):
                        turn = b * (NB // U) + i
                        v.wait_ge(acc_full, U + before(b, i, s) + 1)
                        v.wait_ge(x_in[s], 16 * (turn + 1))
                        v.wait_ge(x1_stored[s], U + 16 * STORES * turn)
                        nc.vector.scalar_tensor_tensor(x1[s][:], acc[s][:], bmix[:], x[s][:], ALU.add, ALU.add).then_inc(x1_ready, 1)
                        v.wait_ge(x1_ready, U + before(b, i, s) + 1)
                        nc.vector.bn_stats(stats[:, b, bass.ds(i * U + s, 1), :].rearrange("p a n -> p (a n)"), x1[s][:]).then_inc(stats_done, 1)
            v.wait_ge(stats_done, B * NB)
            for b in range(B):
                nc.vector.bn_aggr(mv[:, b, :], stats[:, b].rearrange("p n s -> p (n s)")).then_inc(aggregated, 1)
            v.wait_ge(summed, 1)
            nc.vector.tensor_copy(small[:, 0, :], sums[:, 0, :]).then_inc(dve, 1)
            nc.vector.tensor_tensor(small[:, 1, :], mv[:, :, 0], sums[:, 0, :], ALU.subtract).then_inc(dve, 1)
            v.wait_ge(dve, 2)
            nc.vector.tensor_tensor(small[:, 2, :], small[:, 1, :], small[:, 1, :], ALU.mult).then_inc(dve, 1)
            v.wait_ge(summed, 2)
            nc.vector.tensor_scalar(small[:, 4, :], sums[:, 1, :], 1e-5, None, ALU.add).then_inc(dve, 1)
            v.wait_ge(std_ready, 1)
            nc.vector.reciprocal(out[:, :, 0], small[:, 5, :]).then_inc(dve, 1)
            v.wait_ge(dve, 5)
            nc.vector.scalar_tensor_tensor(out[:, :, 1], small[:, 0, :], -1.0, out[:, :, 0], ALU.mult, ALU.mult).then_inc(dve, 1)

        @block.scalar
        def _(act):
            primed(act, x1_stored, U)
            for b in range(B):
                with act.Fori(0, NB // U) as i:
                    for s in range(U):
                        rows = bass.ds((i * U + s) * KR, KR)
                        act.wait_ge(x1_ready, U + before(b, i, s) + 1)
                        for to, frm, n in ((PAD_L, 0, W), (0, W - PAD_L, PAD_L), (PAD_L + W, 0, PAD_R)):
                            act.dma_start(X1[b, rows, :, to:to + n].rearrange("h c w -> (h c) w"),
                                          x1[s][:, frm:frm + n]).then_inc(x1_stored[s], 16)
            act.wait_ge(dve, 4)
            nc.scalar.activation(small[:, 5, :], small[:, 4, :], ACT.Sqrt).then_inc(std_ready, 1)
            act.wait_ge(dve, 6)
            act.dma_start(S, out[:]).then_inc(s_stored, 16)
            act.wait_ge(s_stored, 16)
            for s in range(U):
                act.wait_ge(x1_stored[s], U + 16 * STORES * B * NB // U)


def sphere(nc, T, X1, S, out):
    with ExitStack() as ctx:
        sb, ps, sem = allocators(nc, ctx)
        M = OR * C
        side = sb("s_side", [P, CHUNKS * CHUNK * OR])
        centre = sb("s_centre", [P, CHUNKS * CHUNK * OR])
        slot = sb("s_slot", [P, KR])
        w_side = sb("s_w_side", [P, C, C])
        w_centre = sb("s_w_centre", [P, C, C])
        l_side = sb("s_l_side", [P, C, P])
        l_centre = sb("s_l_centre", [P, C, P])
        mat_h = sb("s_mat_h", [P, CHUNKS * CHUNK, M], BF16)
        mat_l = sb("s_mat_l", [P, CHUNKS * CHUNK, M], BF16)
        bias = sb("s_bias", [M, 1])
        norm = sb("s_norm", [P, B, 2])
        raw = [sb(f"s_raw{s}", [P, XROW]) for s in range(B)]
        xn = [sb(f"s_xn{s}", [P, XROW]) for s in range(B)]
        xh = [sb(f"s_xh{s}", [P, XROW], BF16) for s in range(B)]
        xl = [sb(f"s_xl{s}", [P, XROW], BF16) for s in range(B)]
        res = [sb(f"s_res{s}", [M, W]) for s in range(B)]
        y = [sb(f"s_y{s}", [P, W]) for s in range(B)]
        made = [ps(f"s_made{s}", [P, CHUNK * OR]) for s in range(4)]
        acc = [ps(f"s_acc{s}", [P, W]) for s in range(B)]

        consts_in = sem("s_consts_in")
        l_ready = sem("s_l_ready")
        made_full = sem("s_made_full")
        mat_hi = sem("s_mat_hi")
        mat_lo = sem("s_mat_lo")
        raw_in = [sem(f"s_raw_in{s}") for s in range(B)]
        res_in = [sem(f"s_res_in{s}") for s in range(B)]
        xn_done = [sem(f"s_xn_done{s}") for s in range(B)]
        xh_done = [sem(f"s_xh_done{s}") for s in range(B)]
        xl_done = [sem(f"s_xl_done{s}") for s in range(B)]
        acc_full = [sem(f"s_acc_full{s}") for s in range(B)]
        y_ready = [sem(f"s_y_ready{s}") for s in range(B)]
        y_stored = [sem(f"s_y_stored{s}") for s in range(B)]
        MADE = 4
        KS = 2 * 3 * KR
        KC = 3 * KR
        NCONST = 3 + 9 + OR + 1
        block = ctx.enter_context(nc.Block())

        def blocks(engine):
            for first, count in SPHERE_RUNS:
                h0, n, r0, shifts, e0 = SPHERE_BLOCKS[first]
                if count == 1:
                    yield first, h0, n, r0, shifts, e0
                else:
                    with engine.Fori(0, count) as i:
                        yield i + first, i * OR + h0, n, i * OR + r0, shifts, i * len(shifts) + e0

        def span(shifts):
            a = min(shifts)
            return PAD_L + a, W + max(shifts) - a

        @block.sync
        def _(sp):
            sp.dma_start(side[:], T["side"]).then_inc(consts_in, 16)
            sp.dma_start(centre[:], T["centre"]).then_inc(consts_in, 16)
            sp.dma_start(slot[:], T["slot"]).then_inc(consts_in, 16)
            for kx in range(3):
                for ky in range(3):
                    to = w_centre if kx == 1 else w_side
                    p0 = (ky if kx == 1 else kx // 2 * 3 + ky) * KR
                    sp.dma_start(to[p0:p0 + KR], T["w_sphere"][kx, ky:ky + 1].broadcast_to([KR, C, C])).then_inc(consts_in, 16)
            for r in range(OR):
                sp.dma_start(bias[r * C:(r + 1) * C], T["b_sphere"]).then_inc(consts_in, 16)
            sp.dma_start(norm[:], S).then_inc(consts_in, 16)
            for at, h0, n, r0, shifts, e0 in blocks(sp):
                c0, cols = span(shifts)
                for b in range(B):
                    sp.wait_ge(xn_done[b], at)
                    sp.dma_start(raw[b][:, 0:cols], X1[b, bass.ds(r0, KR), :, c0:c0 + cols].rearrange("h c w -> (h c) w")
                                 ).then_inc(raw_in[b], 16)
                    sp.wait_ge(y_ready[b], at)
                    sp.dma_start(res[b][0:n * C], X1[b, bass.ds(h0, n), :, PAD_L:PAD_L + W].rearrange("h c w -> (h c) w")
                                 ).then_inc(res_in[b], 16)

        @block.gpsimd
        def _(pool):
            for at, h0, n, r0, shifts, e0 in blocks(pool):
                for b in range(B):
                    pool.wait_ge(y_ready[b], at + 1)
                    pool.dma_start(out[b, :, bass.ds(h0, n)].rearrange("c h w -> h c w"),
                                   y[b][0:n * C]).then_inc(y_stored[b], 16)
            for b in range(B):
                pool.wait_ge(y_stored[b], 16 * BLOCKS)

        @block.scalar
        def _(act):
            act.wait_ge(consts_in, 16 * NCONST)
            with act.Fori(0, CHUNKS) as i:
                for o in range(C):
                    act.wait_ge(made_full, i * C + o + 1)
                    nc.scalar.activation(mat_h[:, bass.ds(i * CHUNK, CHUNK), o::C].rearrange("p e h -> p (e h)"),
                                         made[o % 4][:], ACT.Copy).then_inc(mat_hi, 1)
            for at, h0, n, r0, shifts, e0 in blocks(act):
                c0, cols = span(shifts)
                for b in range(B):
                    act.wait_ge(raw_in[b], 16 * (at + 1))
                    act.wait_ge(xl_done[b], at)
                    nc.scalar.activation(xn[b][:, 0:cols], raw[b][:, 0:cols], ACT.Identity, bias=norm[:, b, 1:2],
                                         scale=norm[:, b, 0:1]).then_inc(xn_done[b], 1)
                    act.wait_ge(xn_done[b], at + 1)
                    act.wait_ge(acc_full[b], at)
                    nc.scalar.activation(xh[b][:, 0:cols], xn[b][:, 0:cols], ACT.Copy).then_inc(xh_done[b], 1)

        @block.vector
        def _(v):
            primed(v, [mat_lo], MADE)
            v.wait_ge(consts_in, 16 * NCONST)
            for o in range(C):
                for k, w_, l_ in ((KS, w_side, l_side), (KC, w_centre, l_centre)):
                    nc.vector.tensor_tensor(l_[0:k, o, :].rearrange("p (s c) -> p s c", c=C),
                                            w_[0:k, o, :].unsqueeze(1).broadcast_to([k, KR, C]),
                                            slot[0:k].unsqueeze(2).broadcast_to([k, KR, C]), ALU.mult).then_inc(l_ready, 1)
            with v.Fori(0, CHUNKS) as i:
                for o in range(C):
                    v.wait_ge(mat_hi, i * C + o + 1)
                    at = bass.ds(i * CHUNK, CHUNK)
                    nc.vector.tensor_tensor(mat_l[:, at, o::C].rearrange("p e h -> p (e h)"), made[o % 4][:],
                                            mat_h[:, at, o::C].rearrange("p e h -> p (e h)"), ALU.subtract).then_inc(mat_lo, 1)
            for at, h0, n, r0, shifts, e0 in blocks(v):
                c0, cols = span(shifts)
                for b in range(B):
                    v.wait_ge(xh_done[b], at + 1)
                    nc.vector.tensor_tensor(xl[b][:, 0:cols], xn[b][:, 0:cols], xh[b][:, 0:cols], ALU.subtract).then_inc(xl_done[b], 1)
                for b in range(B):
                    v.wait_ge(acc_full[b], at + 1)
                    v.wait_ge(res_in[b], 16 * (at + 1))
                    v.wait_ge(y_stored[b], 16 * at)
                    nc.vector.scalar_tensor_tensor(y[b][0:n * C], acc[b][0:n * C, :], bias[0:n * C], res[b][0:n * C],
                                                   ALU.add, ALU.add).then_inc(y_ready[b], 1)

        @block.tensor
        def _(pe):
            pe.wait_ge(l_ready, 2 * C)
            with pe.Fori(0, CHUNKS) as i:
                for o in range(C):
                    pe.wait_ge(mat_lo, MADE + i * C + o - MADE + 1)
                    cols = bass.ds(i * (CHUNK * OR), CHUNK * OR)
                    nc.tensor.matmul(made[o % 4][:], l_side[0:KS, o, :], side[0:KS, cols], start=True, stop=False)
                    nc.tensor.matmul(made[o % 4][:], l_centre[0:KC, o, :], centre[0:KC, cols],
                                     start=False, stop=True).then_inc(made_full, 1)
            pe.wait_ge(mat_lo, MADE + CHUNKS * C)
            for at, h0, n, r0, shifts, e0 in blocks(pe):
                for b in range(B):
                    pe.wait_ge(xl_done[b], at + 1)
                    pe.wait_ge(y_ready[b], at)
                    for j, s in enumerate(shifts):
                        c0 = s - min(shifts)
                        hi = mat_h[:, bass.ds(e0 + j, 1), :].rearrange("p a m -> p (a m)")
                        lo = mat_l[:, bass.ds(e0 + j, 1), :].rearrange("p a m -> p (a m)")
                        nc.tensor.matmul(acc[b][0:M, :], hi, xh[b][:, c0:c0 + W], start=j == 0, stop=False)
                        nc.tensor.matmul(acc[b][0:M, :], hi, xl[b][:, c0:c0 + W], start=False, stop=False)
                        last = nc.tensor.matmul(acc[b][0:M, :], lo, xh[b][:, c0:c0 + W], start=False, stop=j == len(shifts) - 1)
                    last.then_inc(acc_full[b], 1)


def program(nc, T, out):
    def dram(name, shape, dt=FP32):
        return nc.dram_tensor(name, shape, dt).ap()

    Y = dram("Y", (B, YROWS, C, QKV))
    QK = dram("QK", (B, C, 2, 2, F, W), BF16)
    V = dram("V", (B, C, WPAD, F))
    Z = dram("Z", (B, F, C, W))
    X1 = dram("X1", (B, F, C, XROW))
    S = dram("S", (P, B, 2))
    project(nc, T, Y)
    convolve(nc, T, Y, QK, V)
    attend(nc, T, QK, V, Z)
    residual(nc, T, Z, X1, S)
    sphere(nc, T, X1, S, out)


def kernel(**inputs):
    import concourse.bacc as bacc
    from concourse.bass_utils import run_bass_kernel_spmd as run

    a = {name: np.asarray(v) for name, v in inputs.items()}
    layer = lambda name: a["L0_conv_" + name]
    taps = np.stack([layer(n + "_conv_w")[:, :, 0, :] for n in "qkv"])
    taps = np.ascontiguousarray(taps.transpose(2, 0, 1, 3)[..., ::-1]).reshape(C, 3 * C, TAPS)
    arrays = {
        "x": a["x"],
        "w_qkv": np.concatenate([layer("W" + n).transpose(0, 2, 1) for n in "qkv"], 2),
        "b_qkv": np.concatenate([layer("b" + n) for n in "qkv"], 1),
        "taps": np.pad(taps, ((0, 0), (0, 0), (KW - TAPS, OW - 1))),
        "qkv_conv_b": np.stack([layer(n + "_conv_b") for n in "qkv"]),
        "w_o": layer("Wo").transpose(0, 2, 1),
        "b_o": layer("bo").reshape(C, FH, P).transpose(0, 2, 1),
        "w_mix": layer("o_conv_w")[:, :, 0, 0].T,
        "b_mix": layer("o_conv_b").reshape(C, 1),
        "w_sphere": a["L1_conv_weight"].transpose(3, 2, 0, 1),
        "b_sphere": a["L1_conv_bias"].reshape(C, 1),
        **constants(),
    }
    nc = bacc.Bacc("TRN2", target_bir_lowering=False, num_devices=1)
    T, ins = {}, {}
    for name, v in arrays.items():
        v = np.ascontiguousarray(v)
        ins["in_" + name] = v
        T[name] = nc.dram_tensor("in_" + name, v.shape, mybir.dt.from_np(v.dtype), kind="ExternalInput").ap()
    out = nc.dram_tensor("out", a["x"].shape, mybir.dt.from_np(a["x"].dtype), kind="ExternalOutput").ap()
    program(nc, T, out)
    return run(nc, [ins], core_ids=[0]).results[0]["out"]
```

```python
import math
from contextlib import ExitStack

import numpy as np

import concourse.bass as bass
from concourse import mybir

FP32 = mybir.dt.float32
BF16 = mybir.dt.bfloat16
ALU = mybir.AluOpType
ACT = mybir.ActivationFunctionType
AX = mybir.AxisListType

B, C, F, W = 2, 8, 256, 512
P = 128
HEADS = 8
DH = F // HEADS
GROUPS = 4
CPG = C // GROUPS
FH = F // P
QKV = 3 * F
TAPS = 7
PAD = TAPS // 2

KW = P // C
OW = KW - TAPS + 1
WINDOWS = -(-W // OW)
WPAD = WINDOWS * OW
YROWS = WPAD + 2 * PAD

KR = P // C
OR = KR - 3
BLOCKS = -(-F // OR)


def sphere_taps():
    polar = np.linspace(1.0 / (2 * F), 1.0 - 1.0 / (2 * F), F) * np.pi
    sin_p, cos_p = np.sin(polar), np.cos(polar)
    scale = np.pi / F
    taps = [dict() for _ in range(F)]
    for ky in range(3):
        for kx in range(3):
            dx, dy = (kx - 1) * scale, (ky - 1) * scale
            radial, height = sin_p + cos_p * dy, -cos_p + sin_p * dy
            shift = np.arctan2(dx, radial) / (2 * np.pi) * W
            row = np.arctan2(np.sqrt(radial ** 2 + dx ** 2), -height) / np.pi * F - 0.5
            for h in range(F):
                y0, x0 = int(np.floor(row[h])), int(np.floor(shift[h]))
                wy, wx = row[h] - y0, shift[h] - x0
                for yy, cy in ((y0, 1 - wy), (y0 + 1, wy)):
                    for xx, cx in ((x0, 1 - wx), (x0 + 1, wx)):
                        at = taps[h].setdefault((min(max(yy, 0), F - 1), xx), {})
                        at[(ky, kx)] = at.get((ky, kx), 0.0) + cy * cx
    return taps


def sphere_plan():
    taps = sphere_taps()
    windows, polar, entries = [], [], []

    def add_entry(used):
        coef = np.zeros((3, 3, KR, OR))
        for slot, h, k in used:
            for (ky, kx), v in k.items():
                coef[kx, ky, slot, h] += v
        entries.append(coef)

    spans = [(OR * i, min(OR, F - OR * i)) for i in range(BLOCKS)]
    uses = {h0: [(h - h0, r, s, k) for h in range(h0, h0 + n) for (r, s), k in taps[h].items()] for h0, n in spans}
    shifts = {h0: sorted({s for _, _, s, _ in uses[h0]}) for h0, _ in spans}
    for h0, n in spans:
        if len(shifts[h0]) <= KR:
            r0 = min(min(r for _, r, _, _ in uses[h0]), F - KR)
            assert max(r for _, r, _, _ in uses[h0]) < r0 + KR
            windows.append((h0, n, r0, shifts[h0], len(entries)))
            for s in shifts[h0]:
                add_entry([(r - r0, h, k) for h, r, sh, k in uses[h0] if sh == s])
    for h0, n in spans:
        if len(shifts[h0]) > KR:
            slots = []
            for r in sorted({r for _, r, _, _ in uses[h0]}):
                for s in sorted({sh for _, row, sh, _ in uses[h0] if row == r}):
                    if not slots or slots[-1] != (s - 1, r):
                        slots.append((s, r))
            slots.sort()
            place = {(r, s + d): (m // KR, d, m % KR) for d in (1, 0) for m, (s, r) in enumerate(slots)}
            tiles = [slots[m:m + KR] for m in range(0, len(slots), KR)]
            polar.append((h0, n, tiles, len(entries)))
            for t in range(len(tiles)):
                for d in range(2):
                    add_entry([(place[r, s][2], h, k) for h, r, s, k in uses[h0] if place[r, s][:2] == (t, d)])
    e = np.stack(entries, 3)
    side = e[[0, 2]].reshape(2 * 3 * KR, -1)
    centre = e[1].reshape(3 * KR, -1)
    return windows, polar, np.concatenate([side, np.zeros((P - 6 * KR, side.shape[1]))]).astype(np.float32), \
        np.concatenate([centre, np.zeros((P - 3 * KR, side.shape[1]))]).astype(np.float32)


SPHERE_WINDOWS, SPHERE_POLAR, SPHERE_SIDE, SPHERE_CENTRE = sphere_plan()
ENTRIES = SPHERE_SIDE.shape[1] // OR
CHUNK = 32
CHUNKS = -(-ENTRIES // CHUNK)
SPHERE_SIDE, SPHERE_CENTRE = (np.pad(a, ((0, 0), (0, (CHUNKS * CHUNK - ENTRIES) * OR))) for a in (SPHERE_SIDE, SPHERE_CENTRE))


def sphere_runs():
    runs = []
    for i, (h0, n, r0, shifts, _) in enumerate(SPHERE_WINDOWS):
        j = runs[-1][0] if runs else None
        if runs and (n, h0 - r0, shifts) == (SPHERE_WINDOWS[j][1], SPHERE_WINDOWS[j][0] - SPHERE_WINDOWS[j][2], SPHERE_WINDOWS[j][3]):
            runs[-1] = (j, runs[-1][1] + 1)
        else:
            runs.append((i, 1))
    return runs


SPHERE_RUNS = sphere_runs()
NEAR = max(abs(s) for blk in SPHERE_WINDOWS for s in blk[3])
POLAR_SLOTS = [(s, r) for blk in SPHERE_POLAR for t in blk[2] for s, r in t]
PAD_L = -min(s for s, _ in POLAR_SLOTS)
PAD_R = max(s for s, _ in POLAR_SLOTS) + 1
TOP = max(r for _, r in POLAR_SLOTS if r < F // 2) + 1
BOTTOM = F - min(r for _, r in POLAR_SLOTS if r >= F // 2)


def rope_tables():
    inv = (np.float32(1.0) / np.float32(10000.0) ** (np.arange(0, DH, 2, dtype=np.float32) / np.float32(DH))).astype(np.float32)
    angle = (np.arange(WPAD, dtype=np.float32)[:, None] * inv[None, :]).astype(np.float32)
    cos = np.repeat(np.cos(angle.astype(np.float64)), 2, -1).T
    sin = np.repeat(np.sin(angle.astype(np.float64)), 2, -1).T
    sin = sin * np.where(np.arange(DH) % 2 == 0, -1.0, 1.0)[:, None]
    scale = 1.0 / math.sqrt(F)
    out = []
    for t in (cos, sin):
        t = np.tile(np.stack([t * scale, t], 1), (P // DH, 1, 1)).reshape(P, 2, 1, 2, WPAD // 2)
        out.append(np.repeat(t, FH, 2).transpose(0, 3, 1, 2, 4).reshape(P, 2, -1).astype(np.float32))
    return out


def constants():
    cos, sin = rope_tables()
    part = np.arange(P)
    same_group = (part[:, None] % C // CPG == part[None, :] % C // CPG) / float(P // C * CPG)
    slot = np.zeros((P, KR), np.float32)
    slot[part, part % KR] = 1.0
    return {
        "ident": np.eye(P, dtype=np.float32),
        "cos": cos, "sin": sin,
        "same_group": same_group.astype(np.float32),
        "slot": slot,
        "side": SPHERE_SIDE, "centre": SPHERE_CENTRE,
    }


def allocators(nc, ctx):
    def sb(name, shape, dt=FP32):
        return ctx.enter_context(nc.sbuf_tensor(name, shape, dt))

    def ps(name, shape):
        return ctx.enter_context(nc.psum_tensor(name, shape, FP32))

    def sem(name):
        return ctx.enter_context(nc.semaphore(name))

    return sb, ps, sem


def used(n):
    return not isinstance(n, int) or n > 0


def primed(engine, sems, n):
    for s in sems:
        engine.sem_inc(s, n)


def project(nc, T, Y, band, qk_bias, v_bias):
    with ExitStack() as ctx:
        sb, ps, sem = allocators(nc, ctx)
        GT = CPG * FH
        x = sb("p_x", [P, B * C * FH, W])
        xh = sb("p_xh", [P, B * C * FH, W], BF16)
        xl = sb("p_xl", [P, B * C * FH, W], BF16)
        stats = sb("p_stats", [P, B * GROUPS, GT * 6])
        mv = sb("p_mv", [P, B * GROUPS, 2])
        mean = sb("p_mean", [P, B * GROUPS])
        dev = sb("p_dev", [P, B * GROUPS])
        dev2 = sb("p_dev2", [P, B * GROUPS])
        var = sb("p_var", [P, B * GROUPS])
        vare = sb("p_vare", [P, B * GROUPS])
        std = sb("p_std", [P, B * GROUPS])
        rstd = sb("p_rstd", [P, B * GROUPS])
        shift = sb("p_shift", [P, B * GROUPS])
        ones = sb("p_ones", [P, P])
        zero = sb("p_zero", [2 * PAD * C, QKV])
        w = [sb(f"p_w{s}", [P, FH, QKV]) for s in range(2)]
        wh = [sb(f"p_wh{s}", [P, FH, QKV], BF16) for s in range(2)]
        wl = [sb(f"p_wl{s}", [P, FH, QKV], BF16) for s in range(2)]
        bias = [sb(f"p_bias{s}", [P, 2, QKV // 2]) for s in range(2)]
        WT = W // P
        y = [sb(f"p_y{s}", [P, 2, QKV // 2]) for s in range(WT)]
        acc = [ps(f"p_acc{s}", [P, 2, 512]) for s in range(WT)]

        x_in = [sem(f"p_x_in{k}") for k in range(B * GROUPS)]
        w_in = [sem(f"p_w_in{s}") for s in range(2)]
        bias_in = [sem(f"p_bias_in{s}") for s in range(2)]
        w_split = sem("p_w_split")
        wh_done = sem("p_wh_done")
        ones_set = sem("p_ones_set")
        zero_set = sem("p_zero_set")
        zero_out = sem("p_zero_out")
        band_in = sem("p_band_in")
        tile_stats = sem("p_tile_stats")
        group_stats = sem("p_group_stats")
        stat_sums = sem("p_stat_sums")
        dve = sem("p_dve")
        std_ready = sem("p_std_ready")
        normed = sem("p_normed")
        normed_late = sem("p_normed_late")
        x_hi = sem("p_x_hi")
        x_lo = sem("p_x_lo")
        acc_full = [sem(f"p_acc_full{s}") for s in range(2)]
        y_ready = [sem(f"p_y_ready{s}") for s in range(WT)]
        y_out = [sem(f"p_y_out{s}") for s in range(WT)]
        EARLY = 2
        ORDER = [(b, g) for g in range(GROUPS) for b in range(B)]

        block = ctx.enter_context(nc.Block())

        @block.sync
        def _(sp):
            primed(sp, y_out, 1)
            for k, (b, g) in enumerate(ORDER):
                t0 = (b * C + g * CPG) * FH
                sp.dma_start(x[:, t0:t0 + GT, :],
                             T["x"][b, g * CPG:(g + 1) * CPG].rearrange("c (f p) w -> p (c f) w", p=P)).then_inc(x_in[k], 16)
            sp.wait_ge(zero_set, 1)
            for b in range(B):
                sp.dma_start(Y[b, 0:PAD].rearrange("w c f -> (w c) f"), zero[0:PAD * C]).then_inc(zero_out, 16)
                for r0 in range(PAD + W, YROWS, 2 * PAD):
                    n = min(2 * PAD, YROWS - r0)
                    sp.dma_start(Y[b, r0:r0 + n].rearrange("w c f -> (w c) f"), zero[0:n * C]).then_inc(zero_out, 16)
            for w in range(KW):
                sp.dma_start(band[w * C:(w + 1) * C].rearrange("c k (o w) -> c (k o) w", w=OW),
                             T["taps"][:, :, KW - 1 - w:KW - 1 - w + OW]).then_inc(band_in, 16)
            for kf in range(2 * FH):
                sp.dma_start(qk_bias[:, kf, :],
                             T["qkv_conv_b"][kf // FH:kf // FH + 1].broadcast_to([P, C])).then_inc(band_in, 16)
            sp.dma_start(v_bias[:],
                         T["qkv_conv_b"][2].rearrange("(o w a) -> o w a", w=1, a=1).broadcast_to([C, OW, 1])).then_inc(band_in, 16)
            with sp.Fori(0, C // 2) as i:
                for cc in range(2):
                    for b in range(B):
                        for t in range(WT):
                            sp.wait_ge(y_ready[t], 1 + (i * 2 + cc) * B + b + 1)
                            sp.dma_start(Y[b, PAD + t * P:PAD + (t + 1) * P, bass.ds(i * 2 + cc, 1)].rearrange("w a f -> w (a f)"),
                                         y[t][:].rearrange("p a n -> p (a n)")).then_inc(y_out[t], 16)
            for t in range(WT):
                sp.wait_ge(y_out[t], 1 + 16 * B * C)
            sp.wait_ge(band_in, 16 * (KW + 2 * FH + 1))
            sp.wait_ge(zero_out, 16 * B * (1 + len(range(PAD + W, YROWS, 2 * PAD))))

        @block.scalar
        def _(act):
            for cc in range(2):
                act.dma_start(w[cc][:], T["w_qkv"][cc].rearrange("(h p) n -> p h n", p=P)).then_inc(w_in[cc], 16)
                act.dma_start(bias[cc][:], T["b_qkv"][cc:cc + 1].rearrange("a (h n) -> a h n", h=2)
                              .broadcast_to([P, 2, QKV // 2])).then_inc(bias_in[cc], 16)
            def load_weights(i, cc):
                act.wait_ge(w_split, 2 * i + cc - 1)
                act.dma_start(w[cc][:], T["w_qkv"][bass.ds(2 * i + cc, 1)].rearrange("a (h p) n -> p (a h) n", p=P)).then_inc(w_in[cc], 16)

            def load_bias(i, cc):
                act.wait_ge(y_ready[WT - 1], 1 + B * (2 * i + cc - 1))
                act.dma_start(bias[cc][:], T["b_qkv"][bass.ds(2 * i + cc, 1)].rearrange("a (h n) -> a h n", h=2)
                              .broadcast_to([P, 2, QKV // 2])).then_inc(bias_in[cc], 16)

            def high_part(i, cc):
                act.wait_ge(w_in[cc], 16 * (i + 1))
                act.wait_ge(acc_full[cc], 1 + i * B * WT)
                nc.scalar.activation(wh[cc][:], w[cc][:], ACT.Copy).then_inc(wh_done, 1)

            for cc in range(2):
                high_part(0, cc)
            act.wait_ge(dve, 3)
            nc.scalar.activation(std[:], vare[:], ACT.Sqrt).then_inc(std_ready, 1)
            act.wait_ge(dve, 5)
            for k, (b, g) in enumerate(ORDER):
                t0, kg = (b * C + g * CPG) * FH, b * GROUPS + g
                if k < EARLY:
                    act.wait_ge(normed, k + 1)
                else:
                    nc.scalar.activation(x[:, t0:t0 + GT, :], x[:, t0:t0 + GT, :], ACT.Identity, bias=shift[:, kg:kg + 1],
                                         scale=rstd[:, kg:kg + 1]).then_inc(normed_late, 1)
                    act.wait_ge(normed_late, k - EARLY + 1)
                nc.scalar.activation(xh[:, t0:t0 + GT, :], x[:, t0:t0 + GT, :], ACT.Copy).then_inc(x_hi, 1)
                if k == 2 * EARLY - 1:
                    for cc in range(2):
                        load_weights(1, cc)
            for cc in range(2):
                load_bias(1, cc)
                high_part(1, cc)
            with act.Fori(2, C // 2) as i:
                for cc in range(2):
                    load_weights(i, cc)
                    load_bias(i, cc)
                    high_part(i, cc)

        @block.gpsimd
        def _(pool):
            nc.gpsimd.memset(ones[:], 1.0 / P).then_inc(ones_set, 1)
            nc.gpsimd.memset(zero[:], 0.0).then_inc(zero_set, 1)
            for i in range(C // 2):
                for cc in range(2):
                    pool.wait_ge(wh_done, 2 * i + cc + 1)
                    nc.gpsimd.tensor_tensor(wl[cc][:], w[cc][:], wh[cc][:], ALU.subtract).then_inc(w_split, 1)
                for k in range(EARLY + 2 * i, min(EARLY + 2 * i + 2, len(ORDER))):
                    b, g = ORDER[k]
                    t0 = (b * C + g * CPG) * FH
                    if k == EARLY:
                        pool.wait_ge(x_lo, EARLY)
                    pool.wait_ge(x_hi, k + 1)
                    nc.gpsimd.tensor_tensor(xl[:, t0:t0 + GT, :], x[:, t0:t0 + GT, :], xh[:, t0:t0 + GT, :], ALU.subtract).then_inc(x_lo, 1)

        @block.vector
        def _(v):
            primed(v, y_ready, 1)
            for k, (b, g) in enumerate(ORDER):
                t0 = (b * C + g * CPG) * FH
                v.wait_ge(x_in[k], 16)
                for t in range(GT):
                    nc.vector.bn_stats(stats[:, b * GROUPS + g, 6 * t:6 * t + 6], x[:, t0 + t, :]).then_inc(tile_stats, 1)
            v.wait_ge(tile_stats, B * GROUPS * GT)
            for k in range(B * GROUPS):
                nc.vector.bn_aggr(mv[:, k, :], stats[:, k, :]).then_inc(group_stats, 1)
            v.wait_ge(stat_sums, 1)
            nc.vector.tensor_copy(mean[:], acc[WT - 1][:, 0, 0:B * GROUPS]).then_inc(dve, 1)
            nc.vector.tensor_tensor(dev[:], mv[:, :, 0], acc[WT - 1][:, 0, 0:B * GROUPS], ALU.subtract).then_inc(group_stats, 1)
            v.wait_ge(group_stats, B * GROUPS + 1)
            nc.vector.tensor_tensor(dev2[:], dev[:], dev[:], ALU.mult).then_inc(group_stats, 1)
            v.wait_ge(stat_sums, 2)
            nc.vector.tensor_copy(var[:], acc[WT - 1][:, 0, B * GROUPS:2 * B * GROUPS]).then_inc(dve, 1)
            v.wait_ge(dve, 2)
            nc.vector.tensor_scalar(vare[:], var[:], 1e-5, None, ALU.add).then_inc(dve, 1)
            v.wait_ge(std_ready, 1)
            nc.vector.reciprocal(rstd[:], std[:]).then_inc(dve, 1)
            v.wait_ge(dve, 4)
            nc.vector.scalar_tensor_tensor(shift[:], mean[:], -1.0, rstd[:], ALU.mult, ALU.mult).then_inc(dve, 1)
            v.wait_ge(dve, 5)

            def low_part(k):
                b, g = ORDER[k]
                t0 = (b * C + g * CPG) * FH
                v.wait_ge(x_hi, k + 1)
                nc.vector.tensor_tensor(xl[:, t0:t0 + GT, :], x[:, t0:t0 + GT, :], xh[:, t0:t0 + GT, :], ALU.subtract).then_inc(x_lo, 1)

            for k, (b, g) in enumerate(ORDER[:EARLY]):
                t0, kg = (b * C + g * CPG) * FH, b * GROUPS + g
                nc.vector.tensor_scalar(x[:, t0:t0 + GT, :], x[:, t0:t0 + GT, :], rstd[:, kg:kg + 1], shift[:, kg:kg + 1],
                                        ALU.mult, ALU.add).then_inc(normed, 1)
            for k in range(EARLY):
                low_part(k)
            with v.Fori(0, C // 2) as i:
                for cc in range(2):
                    v.wait_ge(bias_in[cc], 16 * (i + 1))
                    for b in range(B):
                        for t in range(WT):
                            n = (i * 2 + cc) * B + b
                            v.wait_ge(acc_full[cc], 1 + (i * B + b) * WT + t + 1)
                            v.wait_ge(y_out[t], 1 + 16 * n)
                            nc.vector.tensor_tensor(y[t][:], acc[t][:, :, 0:QKV // 2], bias[cc][:], ALU.add).then_inc(y_ready[t], 1)

        @block.tensor
        def _(pe):
            primed(pe, acc_full, 1)
            pe.wait_ge(ones_set, 1)
            pe.wait_ge(group_stats, B * GROUPS)
            nc.tensor.matmul(acc[WT - 1][:, 0, 0:B * GROUPS], ones[:], mv[:, :, 0], start=True, stop=True)
            nc.tensor.matmul(acc[WT - 1][:, 0, B * GROUPS:2 * B * GROUPS], ones[:], mv[:, :, 1], start=True, stop=False).then_inc(stat_sums, 1)
            pe.wait_ge(group_stats, B * GROUPS + 2)
            nc.tensor.matmul(acc[WT - 1][:, 0, B * GROUPS:2 * B * GROUPS], ones[:], dev2[:], start=False, stop=True).then_inc(stat_sums, 1)
            with pe.Fori(0, C // 2) as i:
                for cc in range(2):
                    pe.wait_ge(w_split, 2 * i + cc + 1)
                    for b in range(B):
                        pe.wait_ge(x_lo, i * 2 + b + 1)
                        for t in range(WT):
                            n = (i * 2 + cc) * B + b
                            pe.wait_ge(y_ready[t], 1 + n)
                            for half in range(2):
                                cols = slice(half * (QKV // 2), (half + 1) * (QKV // 2))
                                for fh in range(FH):
                                    tile = bass.ds(i * (2 * FH) + (b * C + cc) * FH + fh, 1)
                                    hi = xh[:, tile, t * P:(t + 1) * P].rearrange("p a n -> p (a n)")
                                    lo = xl[:, tile, t * P:(t + 1) * P].rearrange("p a n -> p (a n)")
                                    out = acc[t][:, half, 0:QKV // 2]
                                    nc.tensor.matmul(out, hi, wh[cc][:, fh, cols], start=fh == 0, stop=False)
                                    nc.tensor.matmul(out, hi, wl[cc][:, fh, cols], start=False, stop=False)
                                    last = nc.tensor.matmul(out, lo, wh[cc][:, fh, cols], start=False, stop=fh == FH - 1)
                            last.then_inc(acc_full[cc], 1)


def convolve(nc, T, Y, QK, V, band, qk_bias, v_bias):
    with ExitStack() as ctx:
        sb, ps, sem = allocators(nc, ctx)
        KF = 2 * FH
        SLOTS = 4
        LOADED = 8
        START = LOADED
        RW = WINDOWS // 4
        BR = WINDOWS // RW
        ROUNDS = B * BR
        CW = 2 * RW * OW
        OI = C // 4
        LEAD = 2
        gate = sb("c_gate", [1, 2])
        qk = sb("c_qk", [P, 2, C, KF, CW])
        cos = sb("c_cos", [P, 2, KF * CW])
        sin = sb("c_sin", [P, 2, KF * CW])
        win = [sb(f"c_win{s}", [P, QKV]) for s in range(LOADED)]
        vout = [sb(f"c_v{s}", [C * OW, F]) for s in range(LOADED)]
        straight = [sb(f"c_straight{s}", [P, OI, KF, CW]) for s in range(2)]
        turned = [sb(f"c_turned{s}", [P, OI, KF, CW]) for s in range(2)]
        hi = [sb(f"c_hi{s}", [P, OI, KF, CW], BF16) for s in range(2)]
        lo = [sb(f"c_lo{s}", [P, OI, KF, CW], BF16) for s in range(2)]
        acc_qk = [ps(f"c_acc_qk{s}", [P, 512]) for s in range(SLOTS)]
        acc_v = [ps(f"c_acc_v{s}", [P, 512]) for s in range(SLOTS)]

        tables_in = sem("c_tables_in")
        win_in = [sem(f"c_win_in{s}") for s in range(LOADED)]
        acc_full = sem("c_acc_full")
        qk_read = sem("c_qk_read")
        v_read = sem("c_v_read")
        v_stored = [sem(f"c_v_stored{s}") for s in range(LOADED)]
        item_taken = sem("c_item_taken")
        gated = sem("c_gated")
        turn_done = sem("c_turn_done")
        sin_done = sem("c_sin_done")
        cos_late = sem("c_cos_late")
        cos_done = sem("c_cos_done")
        rope_done = sem("c_rope_done")
        hi_done = sem("c_hi_done")
        lo_done = sem("c_lo_done")
        hi_stored = [sem(f"c_hi_stored{s}") for s in range(2)]
        lo_stored = [sem(f"c_lo_stored{s}") for s in range(2)]
        block = ctx.enter_context(nc.Block())

        def freed(r, j, slots=SLOTS):
            before = j - slots if j >= slots else (RW - 1 - j) // slots * slots + j - RW
            return START + r * RW + before + 1

        def uses(r, j, slots=SLOTS):
            return r * len(range(j % slots, RW, slots)) + j // slots

        def item(r, x):
            return 2 * (r - LEAD) + x

        def flat(tile):
            return tile[:].rearrange("p o k w -> p o (k w)")

        def taken(r, x):
            return not isinstance(r, int) or r < ROUNDS or (r, x) == (ROUNDS, 0)

        def values(r, x):
            if taken(r, x):
                return flat(straight[x])
            o = (r % 2 * 2 + x) * OI
            return flat(qk[:, (r - LEAD) // 2 % 2, o:o + OI])

        @block.sync
        def _(sp):
            primed(sp, v_stored, START)

            def store_v(b, i, j):
                sp.wait_ge(v_read, START + (b * BR + i) * RW + j + 1)
                sp.dma_start(V[b, :, bass.ds((i * RW + j) * OW, OW), :], vout[j % LOADED][:]).then_inc(v_stored[j % LOADED], 16)

            def load_and_store(b, i):
                for j in range(RW):
                    s = j % LOADED
                    sp.wait_ge(acc_full, freed(b * BR + i, j, LOADED))
                    sp.dma_start(win[s][:], Y[b, bass.ds((i * RW + j) * OW, KW)].rearrange("w c f -> (w c) f")).then_inc(win_in[s], 16)
                    if j >= LOADED:
                        store_v(b, i, j - LOADED)
                    elif used(i):
                        store_v(b, i - 1, RW - LOADED + j)
                    elif b:
                        store_v(b - 1, BR - 1, RW - LOADED + j)

            for b in range(B):
                load_and_store(b, 0)
                with sp.Fori(1, BR) as i:
                    load_and_store(b, i)
            for j in range(RW - LOADED, RW):
                store_v(B - 1, BR - 1, j)
            for s in range(LOADED):
                sp.wait_ge(v_stored[s], START + 16 * uses(ROUNDS, s, LOADED))

        @block.tensor
        def _(pe):
            primed(pe, [acc_full], START)
            with pe.Fori(0, ROUNDS) as r:
                for j in range(RW):
                    s = j % SLOTS
                    w = win[j % LOADED]
                    pe.wait_ge(win_in[j % LOADED], 16 * (uses(r, j, LOADED) + 1))
                    pe.wait_ge(qk_read, freed(r, j))
                    pe.wait_ge(v_read, freed(r, j))
                    for kf in range(KF):
                        nc.tensor.matmul(acc_qk[s][:, kf * C * OW:(kf + 1) * C * OW], w[:, kf * P:(kf + 1) * P],
                                         band[:, kf // FH, :], start=True, stop=True)
                    nc.tensor.matmul(acc_v[s][0:C * OW, 0:F], band[:, 2, :], w[:, 2 * F:3 * F],
                                     start=True, stop=True).then_inc(acc_full, 1)

        @block.vector
        def _(v):
            primed(v, [qk_read, rope_done, lo_done], START)
            nc.vector.memset(gate[:], 0.0).then_inc(gated, 1)
            v.wait_ge(gated, 1)

            def windows(r, js):
                for j in js:
                    v.wait_ge(acc_full, START + r * RW + j + 1)
                    nc.vector.tensor_tensor(
                        qk[:, bass.ds((r >> 1) & 1, 1), :, :, bass.ds((r & 1) * (RW * OW) + j * OW, OW)].rearrange("p a o k w -> p k (a o) w"),
                        acc_qk[j % SLOTS][:, 0:KF * C * OW].rearrange("p (k o w) -> p k o w", k=KF, w=OW),
                        qk_bias[:].unsqueeze(3).broadcast_to([P, KF, C, OW]), ALU.add).then_inc(qk_read, 1)

            def turn(r, x):
                if taken(r, x):
                    v.wait_ge(item_taken, item(r, x) + 1)
                else:
                    v.wait_ge(qk_read, START + ROUNDS * RW)
                v.wait_ge(rope_done, START + item(r, x) - 1)
                nc.vector.tensor_copy(gate[:, 1:2], gate[:, 0:1]).then_inc(gated, 1)
                nc.vector.stream_shuffle(flat(turned[x]), values(r, x), [d ^ 1 for d in range(32)]).then_inc(turn_done, 1)

            def add(r, x):
                v.wait_ge(sin_done, item(r, x) + 1)
                if isinstance(r, int) and r >= ROUNDS and x == 1:
                    v.wait_ge(cos_late, r - ROUNDS + 1)
                elif isinstance(r, int) and r >= ROUNDS:
                    v.wait_ge(cos_done, item(ROUNDS, 0) + r - ROUNDS + 1)
                else:
                    v.wait_ge(cos_done, item(r, x) + 1)
                nc.vector.tensor_tensor(values(r, x), values(r, x), flat(turned[x]), ALU.add).then_inc(rope_done, 1)

            def low(r, x):
                v.wait_ge(hi_done, item(r, x) + 1)
                v.wait_ge(lo_stored[x], START + 16 * OI * (r - LEAD))
                nc.vector.tensor_tensor(flat(lo[x]), values(r, x), flat(hi[x]), ALU.subtract).then_inc(lo_done, 1)

            def full_round(r, first=False, convolving=True):
                turn(r, 0)
                if not first:
                    add(r - 1, 1)
                if convolving:
                    if not first:
                        v.wait_ge(item_taken, item(r, 0))
                    windows(r, range(0, 4))
                if not first:
                    low(r - 1, 1)
                if convolving:
                    windows(r, range(4, 6))
                turn(r, 1)
                if not convolving:
                    v.wait_ge(turn_done, item(r, 1) + 1)
                    nc.vector.tensor_tensor(values(r, 1), values(r, 1), cos[:, 1:2].broadcast_to([P, OI, KF * CW]),
                                            ALU.mult).then_inc(cos_late, 1)
                add(r, 0)
                if convolving:
                    windows(r, range(6, 11))
                low(r, 0)
                if convolving:
                    windows(r, range(11, RW))

            with v.Fori(0, LEAD) as r:
                windows(r, range(RW))
            full_round(LEAD, first=True)
            with v.Fori(LEAD + 1, ROUNDS) as r:
                full_round(r)
            v.wait_ge(tables_in, 32)
            for r in range(ROUNDS, ROUNDS + LEAD):
                full_round(r, convolving=False)
            add(ROUNDS + LEAD - 1, 1)
            low(ROUNDS + LEAD - 1, 1)

        @block.gpsimd
        def _(pool):
            pool.wait_ge(tables_in, 32)

            def products(r, tables):
                for x in range(2):
                    pool.wait_ge(turn_done, item(r, x) + 1)
                    if not isinstance(r, int) or x == 0:
                        nc.gpsimd.tensor_tensor(values(r, x), values(r, x), tables[0], ALU.mult).then_inc(cos_done, 1)
                    nc.gpsimd.tensor_tensor(flat(turned[x]), flat(turned[x]), tables[1], ALU.mult).then_inc(sin_done, 1)

            for first in range(LEAD, ROUNDS + LEAD, 2):
                half = (first - LEAD) // 2 % 2
                tables = [t[:, half:half + 1].broadcast_to([P, OI, KF * CW]) for t in (cos, sin)]
                if first < ROUNDS:
                    with pool.Fori(first, first + 2) as r:
                        products(r, tables)
                else:
                    for r in range(first, first + 2):
                        products(r, tables)

        @block.scalar
        def _(act):
            LAST = ROUNDS + LEAD - 1
            primed(act, [v_read] + hi_stored + lo_stored, START)
            act.dma_start(cos[:], T["cos"]).then_inc(tables_in, 16)
            act.dma_start(sin[:], T["sin"]).then_inc(tables_in, 16)

            def windows(r, js):
                for j in js:
                    s = j % SLOTS
                    act.wait_ge(acc_full, START + r * RW + j + 1)
                    act.wait_ge(v_stored[j % LOADED], START + 16 * uses(r, j, LOADED))
                    nc.scalar.activation(vout[j % LOADED][:], acc_v[s][0:C * OW, 0:F], ACT.Identity, bias=v_bias[:]).then_inc(v_read, 1)

            def take(r, x, done):
                act.wait_ge(qk_read, START + done)
                act.wait_ge(lo_done, START + item(r, x) - 1)
                nc.scalar.activation(straight[x][:].rearrange("p o k w -> p (o k w)"),
                                     qk[:, bass.ds(((r - LEAD) >> 1) & 1, 1), bass.ds((r & 1) * (2 * OI) + x * OI, OI)].rearrange("p a o k w -> p (a o k w)"),
                                     ACT.Copy).then_inc(item_taken, 1)

            def store(r, x, part, parts, stored):
                b, half, o = ((r - LEAD) >> 2) & 1, ((r - LEAD) >> 1) & 1, (r & 1) * (2 * OI) + x * OI
                for m in range(OI):
                    act.dma_start(QK[bass.ds(b, 1), bass.ds(o + m, 1), part, :, :, bass.ds(half * CW, CW)].rearrange("a o k (f p) w -> p (a o k f) w", p=P),
                                  parts[x][:, m]).then_inc(stored[x], 16)

            def high(r, x):
                act.wait_ge(rope_done, START + item(r, x) + 1)
                act.wait_ge(hi_stored[x], START + 16 * OI * (r - LEAD))
                nc.scalar.activation(flat(hi[x]), values(r, x), ACT.Copy).then_inc(hi_done, 1)

            def store_high(r, x):
                act.wait_ge(hi_done, item(r, x) + 1)
                store(r, x, 0, hi, hi_stored)

            def store_low(r, x):
                act.wait_ge(lo_done, START + item(r, x) + 1)
                store(r, x, 1, lo, lo_stored)

            def full_round(r, done, first=False, convolving=True):
                if convolving:
                    windows(r, range(0, 4))
                if not first:
                    high(r - 1, 1)
                if taken(r, 1):
                    take(r, 1, done)
                if not first:
                    store_high(r - 1, 1)
                    store_low(r - 1, 1)
                if convolving:
                    windows(r, range(4, 10))
                high(r, 0)
                if convolving:
                    windows(r, range(10, RW))
                if convolving:
                    take(r + 1, 0, done + RW)
                store_high(r, 0)
                store_low(r, 0)

            with act.Fori(0, LEAD) as r:
                windows(r, range(RW))
            take(LEAD, 0, LEAD * RW)
            full_round(LEAD, LEAD * RW, first=True)
            with act.Fori(LEAD + 1, ROUNDS) as r:
                full_round(r, r * RW)
            for r in range(ROUNDS, ROUNDS + LEAD):
                full_round(r, ROUNDS * RW, convolving=False)
            high(LAST, 1)
            store_high(LAST, 1)
            store_low(LAST, 1)
            for s in range(2):
                act.wait_ge(hi_stored[s], START + 16 * OI * ROUNDS)
                act.wait_ge(lo_stored[s], START + 16 * OI * ROUNDS)


def attend(nc, T, QK, V, Z, mixing):
    with ExitStack() as ctx:
        sb, ps, sem = allocators(nc, ctx)
        wmix, bmix, group, slot, side, centre, w_side, w_centre = mixing
        QT = W // P
        STEPS = HEADS * QT
        CHANNELS = 2
        UNITS = B * CHANNELS
        ITERATIONS = C // CHANNELS
        DV = DH + 1
        KROWS = 3 * DH
        SHIFTED = KROWS + 2
        PROBS = 2
        PARTS = 4
        ident = sb("a_ident", [P, P])
        ident16 = sb("a_ident16", [P, P], BF16)
        o = [sb(f"a_o{s}", [P, QT, F]) for s in range(2)]
        q = [sb(f"a_q{u}", [SHIFTED, HEADS, W], BF16) for u in range(UNITS)]
        k = [sb(f"a_k{u}", [SHIFTED, HEADS, W], BF16) for u in range(UNITS)]
        v = [sb(f"a_v{s}", [P, QT, F]) for s in range(2)]
        vp = [sb(f"a_vp{s}", [P, QT * HEADS, DV + DH], BF16) for s in range(2)]
        wo = [sb(f"a_wo{s}", [P, FH, F]) for s in range(CHANNELS)]
        bo = [sb(f"a_bo{s}", [P, FH]) for s in range(CHANNELS)]
        negmax = [sb(f"a_negmax{u}", [P, STEPS]) for u in range(UNITS)]
        maxparts = [sb(f"a_maxparts{u}", [P, 2 * HEADS, QT], BF16) for u in range(UNITS)]
        maxrows = [sb(f"a_maxrows{u}", [2 * HEADS, W], BF16) for u in range(UNITS)]
        prob = [sb(f"a_prob{s}", [P, QT, W]) for s in range(PROBS)]
        ph = [sb(f"a_ph{s}", [P, QT, W], BF16) for s in range(PARTS)]
        pl = [sb(f"a_pl{s}", [P, QT, W], BF16) for s in range(PARTS)]
        inverse = [sb(f"a_inverse{s}", [P, QT]) for s in range(2)]
        oT = sb("a_oT", [P, FH, W])
        z = [sb(f"a_z{s}", [P, W]) for s in range(FH)]
        row = [ps(f"a_row{s}", [P, W]) for s in range(2)]
        col = [ps(f"a_col{s}", [P, W]) for s in range(2)]
        mix = [ps(f"a_mix{s}", [P, QT, DV]) for s in range(2)]
        turned = ps("a_turned", [2 * HEADS, W])
        out = ps("a_out", [P, W])

        const_in = sem("a_const_in")
        wzero = sem("a_wzero")
        mixing_in = sem("a_mixing_in")
        ident16_set = sem("a_ident16_set")
        ones_set = sem("a_ones_set")
        qk_in = [sem(f"a_qk_in{u}") for u in range(UNITS)]
        max_in = [sem(f"a_max_in{u}") for u in range(UNITS)]
        v_in = [sem(f"a_v_in{s}") for s in range(2)]
        wo_in = [sem(f"a_wo_in{s}") for s in range(CHANNELS)]
        v_hi = sem("a_v_hi")
        v_lo = sem("a_v_lo")
        row_full = sem("a_row_full")
        max_done = sem("a_max_done")
        max_hi = sem("a_max_hi")
        max_split = sem("a_max_split")
        max_turned = sem("a_max_turned")
        max_kept = sem("a_max_kept")
        col_full = sem("a_col_full")
        exp_done = sem("a_exp_done")
        hi_act = sem("a_hi_act")
        hi_dve = sem("a_hi_dve")
        lo_dve = sem("a_lo_dve")
        lo_pool = sem("a_lo_pool")
        mixed = sem("a_mixed")
        inverted = sem("a_inverted")
        normed = sem("a_normed")
        out_full = sem("a_out_full")
        out_kept = sem("a_out_kept")
        z_stored = [sem(f"a_z_stored{s}") for s in range(FH)]
        QK_LOADS = 6
        HI_ACT, LO_DVE, LO_POOL = 3, 1, 3

        SPLIT = STEPS
        EXP = STEPS + 7
        MIX = EXP + 2 * QT + 1
        NORM = MIX + QT
        TAIL = NORM + (HEADS - 1) * QT + 3
        BODY = UNITS * STEPS
        assert TAIL + 2 * 2 * FH + 2 < BODY

        def pipeline(engine, ops):
            at = [[f for p, f in ops if p == t] for t in range(2 * BODY)]
            for t in range(BODY):
                for f in at[t]:
                    f(0)
            with engine.Fori(0, ITERATIONS - 1) as i:
                for t in range(BODY):
                    for f in at[BODY + t]:
                        f(i)
                    for f in at[t]:
                        f(i + 1)
            for t in range(BODY, 2 * BODY):
                for f in at[t]:
                    f(ITERATIONS - 1)

        def steps(first, emit, kinds=range(QT)):
            return [(STEPS * u + first + t, lambda i, u=u, t=t: emit(i, u, t // QT, t % QT))
                    for u in range(UNITS) for t in range(STEPS) if t % QT in kinds]

        def heads(first, emit):
            return [(STEPS * u + first + QT * h, lambda i, u=u, h=h: emit(i, u, h)) for u in range(UNITS) for h in range(HEADS)]

        def units(first, emit):
            return [(STEPS * u + first, lambda i, u=u: emit(i, u)) for u in range(UNITS)]

        def tails(first, emit, kinds=range(2 * FH)):
            return [(STEPS * u + first + 2 * j, lambda i, u=u, j=j: emit(i, u, j)) for u in range(UNITS) for j in kinds]

        block = ctx.enter_context(nc.Block())

        @block.sync
        def _(sp):
            sp.dma_start(ident[:], T["ident"]).then_inc(const_in, 16)

            def load(i):
                for u in range(UNITS):
                    s, c, unit = u % B, CHANNELS * i + u // B, UNITS * i + u
                    if used(unit - UNITS + 1):
                        sp.wait_ge(col_full, STEPS * (unit - UNITS + 1))
                    src = QK[s, bass.ds(c, 1), :, :, :, 0:W].rearrange("a p k (h d) w -> p k (a d) h w", d=DH)
                    for r, (qpart, kpart) in enumerate(((0, 0), (0, 1), (1, 0))):
                        sp.dma_start(q[u][r * DH:(r + 1) * DH], src[qpart, 0]).then_inc(qk_in[u], 16)
                        sp.dma_start(k[u][r * DH:(r + 1) * DH], src[kpart, 1]).then_inc(qk_in[u], 16)
                    if used(unit - 1):
                        sp.wait_ge(v_lo, unit - 1)
                    sp.dma_start(v[u % 2][:], V[s, bass.ds(c, 1), 0:W].rearrange("a (t p) f -> p (a t) f", p=P)).then_inc(v_in[u % 2], 16)
                    if s == B - 1:
                        if used(unit - UNITS + 1):
                            sp.wait_ge(out_kept, 2 * FH * (unit - UNITS + 1))
                        sp.dma_start(wo[u // B][:], T["w_o"][bass.ds(c, 1)].rearrange("a (h p) f -> p (a h) f", p=P)).then_inc(wo_in[u // B], 16)
                        sp.dma_start(bo[u // B][:], T["b_o"][bass.ds(c, 1)].rearrange("a p h -> p (a h)")).then_inc(wo_in[u // B], 16)

            load(0)
            sp.wait_ge(wzero, 1)
            for r in range(KR):
                sp.dma_start(wmix[r * C:(r + 1) * C, r * C:(r + 1) * C], T["w_mix"]).then_inc(mixing_in, 16)
            sp.dma_start(bmix[:], T["b_mix"].rearrange("(a c) n -> a c n", a=1).broadcast_to([KR, C, 1])).then_inc(mixing_in, 16)
            sp.dma_start(group[:], T["same_group"]).then_inc(mixing_in, 16)
            sp.dma_start(slot[:], T["slot"]).then_inc(mixing_in, 16)
            for kx in range(3):
                for ky in range(3):
                    to = w_centre if kx == 1 else w_side
                    p0 = (ky if kx == 1 else kx // 2 * 3 + ky) * KR
                    sp.dma_start(to[p0:p0 + KR], T["w_sphere"][kx, ky:ky + 1].broadcast_to([KR, C, C])).then_inc(mixing_in, 16)
            sp.dma_start(side[:], T["side"]).then_inc(mixing_in, 16)
            sp.dma_start(centre[:], T["centre"]).then_inc(mixing_in, 16)
            with sp.Fori(1, ITERATIONS) as i:
                load(i)
            sp.wait_ge(mixing_in, 16 * (KR + 2 + 3 + 9))

        @block.tensor
        def _(pe):
            pe.wait_ge(const_in, 16)
            pe.wait_ge(ident16_set, 1)
            pe.wait_ge(ones_set, UNITS)

            def row_scores(i, u, h, qt):
                step = BODY * i + STEPS * u + QT * h + qt
                if h == 0 and qt == 0:
                    pe.wait_ge(qk_in[u], 16 * QK_LOADS * (i + 1))
                if used(step - 1):
                    pe.wait_ge(max_done, step - 1)
                nc.tensor.matmul(row[qt % 2][:], q[u][0:KROWS, h, qt * P:(qt + 1) * P], k[u][0:KROWS, h, :],
                                 start=True, stop=True).then_inc(row_full, 1)

            def turn_max(i, u):
                unit = UNITS * i + u
                pe.wait_ge(max_split, unit + 1)
                if used(unit):
                    pe.wait_ge(max_kept, unit)
                for qt in range(QT):
                    last = nc.tensor.matmul(turned[:, qt * P:(qt + 1) * P], maxparts[u][:, :, qt], ident16[:], start=True, stop=True)
                last.then_inc(max_turned, 1)

            def col_scores(i, u, h, kt):
                step = BODY * i + STEPS * u + QT * h + kt
                if h == 0 and kt == 0:
                    pe.wait_ge(max_in[u], 16 * (i + 1))
                if used(step - 1):
                    pe.wait_ge(exp_done, step - 1)
                nc.tensor.matmul(col[kt % 2][:], k[u][:, h, kt * P:(kt + 1) * P], q[u][:, h, :],
                                 start=True, stop=True).then_inc(col_full, 1)

            def mix_step(i, u, h, qt):
                head = HEADS * (UNITS * i + u) + h
                if qt == 0:
                    if h == 0:
                        pe.wait_ge(v_lo, UNITS * i + u + 1)
                    pe.wait_ge(lo_dve, LO_DVE * (head + 1))
                    pe.wait_ge(lo_pool, LO_POOL * (head + 1))
                    if used(head - 1):
                        pe.wait_ge(normed, head - 1)
                at = slice(qt * P, (qt + 1) * P)
                for kt in range(QT):
                    vpart = vp[u % 2][:, kt * HEADS + h, :]
                    nc.tensor.matmul(mix[h % 2][:, qt, :], ph[h % PARTS][:, kt, at], vpart[:, 0:DV], start=kt == 0, stop=False)
                    nc.tensor.matmul(mix[h % 2][:, qt, 0:DH], ph[h % PARTS][:, kt, at], vpart[:, DV:], start=False, stop=False)
                    last = nc.tensor.matmul(mix[h % 2][:, qt, :], pl[h % PARTS][:, kt, at], vpart[:, 0:DV],
                                            start=False, stop=kt == QT - 1)
                last.then_inc(mixed, 1)

            def tail(i, u, j):
                unit = UNITS * i + u
                if j == 0:
                    pe.wait_ge(normed, HEADS * (unit + 1))
                if used(2 * FH * unit + j):
                    pe.wait_ge(out_kept, 2 * FH * unit + j)
                if j < FH:
                    for qt in range(QT):
                        last = nc.tensor.transpose(out[:, qt * P:(qt + 1) * P], o[u % 2][:, qt, j * P:(j + 1) * P], ident[:])
                else:
                    fo = j - FH
                    if fo == 0:
                        pe.wait_ge(wo_in[u // B], 32 * (i + 1))
                    for fh in range(FH):
                        last = nc.tensor.matmul(out[:], wo[u // B][:, fh, fo * P:(fo + 1) * P], oT[:, fh, :],
                                                start=fh == 0, stop=fh == FH - 1)
                last.then_inc(out_full, 1)

            pipeline(pe, units(SPLIT + 1, turn_max) + steps(EXP, col_scores) + steps(0, row_scores) + steps(MIX, mix_step)
                     + tails(TAIL, tail))

        @block.vector
        def _(ve):
            ve.wait_ge(const_in, 16)
            nc.vector.tensor_copy(ident16[:], ident[:]).then_inc(ident16_set, 1)
            for u in range(UNITS):
                nc.vector.memset(k[u][KROWS:SHIFTED], 1.0).then_inc(ones_set, 1)
            for s in range(2):
                nc.vector.memset(vp[s][:, :, DH:DV], 1.0).then_inc(ones_set, 1)

            def row_max(i, u, h, qt):
                step = BODY * i + STEPS * u + QT * h + qt
                ve.wait_ge(row_full, step + 1)
                nc.vector.reduce_max(negmax[u][:, QT * h + qt:QT * h + qt + 1], row[qt % 2][:], AX.X, negate=True).then_inc(max_done, 1)

            def split_max(i, u):
                unit = UNITS * i + u
                high, low = (maxparts[u][:, n * HEADS:(n + 1) * HEADS, :].rearrange("p h t -> p (h t)") for n in range(2))
                ve.wait_ge(max_done, STEPS * (unit + 1))
                nc.vector.tensor_copy(high, negmax[u][:]).then_inc(max_hi, 1)
                ve.wait_ge(max_hi, unit + 1)
                nc.vector.tensor_tensor(low, negmax[u][:], high, ALU.subtract).then_inc(max_split, 1)

            def high_part(i, u, h, kt):
                head = HEADS * (UNITS * i + u) + h
                ve.wait_ge(exp_done, QT * head + kt + 1)
                nc.vector.tensor_copy(ph[h % PARTS][:, kt, :], prob[h % PROBS][:, kt, :]).then_inc(hi_dve, 1)

            def low_part(i, u, h, kt):
                head = HEADS * (UNITS * i + u) + h
                ve.wait_ge(hi_act, HI_ACT * head + kt + 1)
                nc.vector.tensor_tensor(pl[h % PARTS][:, kt, :], prob[h % PROBS][:, kt, :], ph[h % PARTS][:, kt, :],
                                        ALU.subtract).then_inc(lo_dve, 1)

            def invert(i, u, h):
                ve.wait_ge(mixed, QT * (HEADS * (UNITS * i + u) + h + 1))
                nc.vector.reciprocal(inverse[h % 2][:].unsqueeze(2), mix[h % 2][:, :, DH:DV]).then_inc(inverted, 1)

            def norm(i, u, h):
                unit, head = UNITS * i + u, HEADS * (UNITS * i + u) + h
                if h == 0 and used(unit - 1):
                    ve.wait_ge(out_full, 2 * FH * (unit - 2) + FH)
                ve.wait_ge(inverted, head + 1)
                nc.vector.tensor_tensor(o[u % 2][:, :, h * DH:(h + 1) * DH], mix[h % 2][:, :, 0:DH],
                                        inverse[h % 2][:].unsqueeze(2).broadcast_to([P, QT, DH]), ALU.mult).then_inc(normed, 1)

            pipeline(ve, steps(0, row_max) + units(SPLIT, split_max) + steps(EXP + 1, high_part, kinds=(3,))
                     + steps(EXP + 2, low_part, kinds=(0,)) + heads(NORM, invert) + heads(NORM + 1, norm))

        @block.scalar
        def _(act):
            act.wait_ge(ones_set, UNITS + 2)

            def v_high(i, u):
                unit = UNITS * i + u
                act.wait_ge(v_in[u % 2], 16 * (UNITS // 2 * i + u // 2 + 1))
                if used(unit - 1):
                    act.wait_ge(mixed, STEPS * (unit - 1))
                nc.scalar.activation(vp[u % 2][:, :, 0:DH], v[u % 2][:].rearrange("p t (h d) -> p (t h) d", d=DH), ACT.Copy).then_inc(v_hi, 1)

            def keep_max(i, u):
                unit = UNITS * i + u
                act.wait_ge(max_turned, unit + 1)
                nc.scalar.activation(maxrows[u][:], turned[:], ACT.Copy).then_inc(max_kept, 1)

            def load_max(i, u):
                act.wait_ge(max_kept, UNITS * i + u + 1)
                act.dma_start(q[u][KROWS:SHIFTED], maxrows[u][:]).then_inc(max_in[u], 16)

            def exp(i, u, h, kt):
                head = HEADS * (UNITS * i + u) + h
                if kt == 0:
                    if used(head - PROBS + 1):
                        act.wait_ge(lo_dve, LO_DVE * (head - PROBS + 1))
                        act.wait_ge(lo_pool, LO_POOL * (head - PROBS + 1))
                    if used(head - PARTS + 1):
                        act.wait_ge(mixed, QT * (head - PARTS + 1))
                act.wait_ge(col_full, QT * head + kt + 1)
                nc.scalar.activation(prob[h % PROBS][:, kt, :], col[kt % 2][:], ACT.Exp).then_inc(exp_done, 1)

            def high_part(i, u, h, kt):
                head = HEADS * (UNITS * i + u) + h
                act.wait_ge(exp_done, QT * head + kt + 1)
                nc.scalar.activation(ph[h % PARTS][:, kt, :], prob[h % PROBS][:, kt, :], ACT.Copy).then_inc(hi_act, 1)

            def keep_out(i, u, j):
                unit = UNITS * i + u
                act.wait_ge(out_full, 2 * FH * unit + j + 1)
                if j < FH:
                    nc.scalar.activation(oT[:, j, :], out[:], ACT.Copy).then_inc(out_kept, 1)
                else:
                    if used(unit):
                        act.wait_ge(z_stored[j - FH], 16 * unit)
                    nc.scalar.activation(z[j - FH][:], out[:], ACT.Identity, bias=bo[u // B][:, j - FH:j - FH + 1]).then_inc(out_kept, 1)

            def store_z(i, u, j):
                unit, fo = UNITS * i + u, j - FH
                act.wait_ge(out_kept, 2 * FH * unit + j + 1)
                act.dma_start(Z[u % B, fo * P:(fo + 1) * P, bass.ds(CHANNELS * i + u // B, 1)].rearrange("f a w -> f (a w)"),
                              z[fo][:]).then_inc(z_stored[fo], 16)

            pipeline(act, units(SPLIT + 2, keep_max) + units(SPLIT + 3, load_max) + units(EXP - 2, v_high) + steps(EXP, exp)
                     + steps(EXP + 1, high_part, kinds=(0, 1, 2))
                     + tails(TAIL + 1, keep_out) + tails(TAIL + 2, store_z, kinds=range(FH, 2 * FH)))
            for fo in range(FH):
                act.wait_ge(z_stored[fo], 16 * B * C)

        @block.gpsimd
        def _(pool):
            nc.gpsimd.memset(wmix[:], 0.0).then_inc(wzero, 1)

            def v_low(i, u):
                pool.wait_ge(v_hi, UNITS * i + u + 1)
                nc.gpsimd.tensor_tensor(vp[u % 2][:, :, DV:], v[u % 2][:].rearrange("p t (h d) -> p (t h) d", d=DH),
                                        vp[u % 2][:, :, 0:DH], ALU.subtract).then_inc(v_lo, 1)

            def low_part(i, u, h, kt):
                head = HEADS * (UNITS * i + u) + h
                if kt < HI_ACT:
                    pool.wait_ge(hi_act, HI_ACT * head + kt + 1)
                else:
                    pool.wait_ge(hi_dve, head + 1)
                nc.gpsimd.tensor_tensor(pl[h % PARTS][:, kt, :], prob[h % PROBS][:, kt, :], ph[h % PARTS][:, kt, :],
                                        ALU.subtract).then_inc(lo_pool, 1)

            pipeline(pool, units(EXP - 1, v_low) + steps(EXP + 2, low_part, kinds=(1, 2, 3)))


def residual(nc, T, Z, X1, S, mixing, mat_h, mat_l):
    with ExitStack() as ctx:
        sb, ps, sem = allocators(nc, ctx)
        wmix, bmix, group, slot, side, centre, w_side, w_centre = mixing
        NB = F // KR
        U = 4
        TURNS = NB // 2 // U
        START = 2 * U
        z = [sb(f"r_z{s}", [P, 2, W]) for s in range(U)]
        x = [sb(f"r_x{s}", [P, 2, W]) for s in range(U)]
        x1 = [sb(f"r_x1{s}", [P, 2, NEAR + W + NEAR]) for s in range(U)]
        stats = sb("r_stats", [P, B, NB, 6])
        mv = sb("r_mv", [P, B, 2])
        small = sb("r_small", [P, 8, B])
        out = sb("r_out", [P, B, 2])
        l_side = sb("r_l_side", [P, C, P])
        l_centre = sb("r_l_centre", [P, C, P])
        acc = [ps(f"r_acc{s}", [P, W]) for s in range(4)]
        made = [ps(f"r_made{s}", [P, CHUNK * OR]) for s in range(2)]
        sums = ps("r_sums", [P, 2, B])
        KS = 2 * 3 * KR
        KC = 3 * KR

        z_in = [sem(f"r_z_in{s}") for s in range(U)]
        x_in = [sem(f"r_x_in{s}") for s in range(U)]
        acc_full = sem("r_acc_full")
        x1_ready = sem("r_x1_ready")
        wrapped = sem("r_wrapped")
        stats_done = sem("r_stats_done")
        x1_stored = [sem(f"r_x1_stored{s}") for s in range(U)]
        l_ready = sem("r_l_ready")
        made_full = sem("r_made_full")
        mat_hi = sem("r_mat_hi")
        mat_lo = sem("r_mat_lo")
        aggregated = sem("r_aggregated")
        summed = sem("r_summed")
        dve = sem("r_dve")
        std_ready = sem("r_std_ready")
        s_stored = sem("r_s_stored")
        block = ctx.enter_context(nc.Block())

        def pairs(engine):
            for b in range(B):
                with engine.Fori(0, TURNS) as i:
                    for s in range(U):
                        yield b, i, s, (b * TURNS + i) * U + s

        def matrices(b, i, s, n, emit):
            for e in range(2):
                emit(e, 2 * s + e, b * TURNS + i, 2 * n + e)

        def of_channel(mat, o, chunk):
            return mat[:, bass.ds(chunk * CHUNK, CHUNK), o::C].rearrange("p e h -> p (e h)")

        assert CHUNKS == B * TURNS and 2 * U == C

        @block.sync
        def _(sp):
            for b, i, s, n in pairs(sp):
                rows = bass.ds((i * U + s) * 2 * KR, 2 * KR)
                sp.wait_ge(acc_full, START + 2 * (n - U) + 2)
                sp.dma_start(z[s][:], Z[b, rows].rearrange("(t h) c w -> (h c) t w", t=2)).then_inc(z_in[s], 16)
                sp.wait_ge(x1_ready, START + 2 * (n - U) + 2)
                for t in range(2):
                    sp.dma_start(x[s][:, t, :], T["x"][b, :, bass.ds(((i * U + s) * 2 + t) * KR, KR)].rearrange("c h w -> h c w")).then_inc(x_in[s], 16)

        @block.tensor
        def _(pe):
            primed(pe, [acc_full], START)
            pe.wait_ge(l_ready, 2 * C)

            def make(e, o, chunk, k):
                pe.wait_ge(mat_lo, START + k - 1)
                cols = bass.ds(chunk * (CHUNK * OR), CHUNK * OR)
                nc.tensor.matmul(made[e][:], l_side[0:KS, o, :], side[0:KS, cols],
                                 start=True, stop=False)
                nc.tensor.matmul(made[e][:], l_centre[0:KC, o, :], centre[0:KC, cols],
                                 start=False, stop=True).then_inc(made_full, 1)

            for b, i, s, n in pairs(pe):
                pe.wait_ge(z_in[s], 16 * (b * TURNS + i + 1))
                pe.wait_ge(x1_ready, START + 2 * (n - 2) + 2)
                for t in range(2):
                    nc.tensor.matmul(acc[s % 2 * 2 + t][:], wmix[:], z[s][:, t, :], start=True, stop=True).then_inc(acc_full, 1)
                matrices(b, i, s, n, make)
            pe.wait_ge(aggregated, B)
            nc.tensor.matmul(sums[:, 0, :], group[:], mv[:, :, 0], start=True, stop=True)
            nc.tensor.matmul(sums[:, 1, :], group[:], mv[:, :, 1], start=True, stop=False).then_inc(summed, 1)
            pe.wait_ge(dve, 3)
            nc.tensor.matmul(sums[:, 1, :], group[:], small[:, 2, :], start=False, stop=True).then_inc(summed, 1)

        @block.vector
        def _(v):
            primed(v, [x1_ready, mat_lo], START)
            for o in range(C):
                for k, w_, l_ in ((KS, w_side, l_side), (KC, w_centre, l_centre)):
                    nc.vector.tensor_tensor(l_[0:k, o, :].rearrange("p (s c) -> p s c", c=C),
                                            w_[0:k, o, :].unsqueeze(1).broadcast_to([k, KR, C]),
                                            slot[0:k].unsqueeze(2).broadcast_to([k, KR, C]), ALU.mult).then_inc(l_ready, 1)

            def low(e, o, chunk, k):
                v.wait_ge(mat_hi, k + 1)
                nc.vector.tensor_tensor(of_channel(mat_l, o, chunk), made[e][:],
                                        of_channel(mat_h, o, chunk), ALU.subtract).then_inc(mat_lo, 1)

            for b, i, s, n in pairs(v):
                v.wait_ge(x_in[s], 32 * (b * TURNS + i + 1))
                v.wait_ge(x1_stored[s], START + 16 * (b * TURNS + i))
                for t in range(2):
                    v.wait_ge(acc_full, START + 2 * n + t + 1)
                    nc.vector.scalar_tensor_tensor(x1[s][:, t, NEAR:NEAR + W], acc[s % 2 * 2 + t][:], bmix[:], x[s][:, t, :],
                                                   ALU.add, ALU.add).then_inc(x1_ready, 1)
                for t in range(2):
                    v.wait_ge(x1_ready, START + 2 * n + t + 1)
                    nc.vector.bn_stats(stats[:, b, bass.ds((i * U + s) * 2 + t, 1), :].rearrange("p a n -> p (a n)"),
                                       x1[s][:, t, NEAR:NEAR + W]).then_inc(stats_done, 1)
                matrices(b, i, s, n, low)
            v.wait_ge(stats_done, B * NB)
            for b in range(B):
                nc.vector.bn_aggr(mv[:, b, :], stats[:, b].rearrange("p n s -> p (n s)")).then_inc(aggregated, 1)
            v.wait_ge(summed, 1)
            nc.vector.tensor_copy(small[:, 0, :], sums[:, 0, :]).then_inc(dve, 1)
            nc.vector.tensor_tensor(small[:, 1, :], mv[:, :, 0], sums[:, 0, :], ALU.subtract).then_inc(dve, 1)
            v.wait_ge(dve, 2)
            nc.vector.tensor_tensor(small[:, 2, :], small[:, 1, :], small[:, 1, :], ALU.mult).then_inc(dve, 1)
            v.wait_ge(summed, 2)
            nc.vector.tensor_scalar(small[:, 4, :], sums[:, 1, :], 1e-5, None, ALU.add).then_inc(dve, 1)
            v.wait_ge(std_ready, 1)
            nc.vector.reciprocal(out[:, :, 0], small[:, 5, :]).then_inc(dve, 1)
            v.wait_ge(dve, 5)
            nc.vector.scalar_tensor_tensor(out[:, :, 1], small[:, 0, :], -1.0, out[:, :, 0], ALU.mult, ALU.mult).then_inc(dve, 1)

        @block.scalar
        def _(act):
            primed(act, x1_stored, START)

            def high(e, o, chunk, k):
                act.wait_ge(made_full, k + 1)
                nc.scalar.activation(of_channel(mat_h, o, chunk), made[e][:], ACT.Copy).then_inc(mat_hi, 1)

            for b, i, s, n in pairs(act):
                act.wait_ge(x1_ready, START + 2 * n + 2)
                nc.scalar.activation(x1[s][:, :, 0:NEAR], x1[s][:, :, W:W + NEAR], ACT.Copy).then_inc(wrapped, 1)
                nc.scalar.activation(x1[s][:, :, NEAR + W:], x1[s][:, :, NEAR:2 * NEAR], ACT.Copy).then_inc(wrapped, 1)
                act.wait_ge(wrapped, 2 * n + 2)
                act.dma_start(X1[b, bass.ds((i * U + s) * 2 * KR, 2 * KR)].rearrange("(t h) c w -> (h c) t w", t=2),
                              x1[s][:]).then_inc(x1_stored[s], 16)
                matrices(b, i, s, n, high)
            act.wait_ge(dve, 4)
            nc.scalar.activation(small[:, 5, :], small[:, 4, :], ACT.Sqrt).then_inc(std_ready, 1)
            act.wait_ge(dve, 6)
            act.dma_start(S, out[:]).then_inc(s_stored, 16)
            act.wait_ge(s_stored, 16)
            for s in range(U):
                act.wait_ge(x1_stored[s], START + 16 * B * TURNS)


def sphere(nc, T, X1, XP, S, mat_h, mat_l, out):
    with ExitStack() as ctx:
        sb, ps, sem = allocators(nc, ctx)
        M = OR * C
        WSPAN = W + max(max(blk[3]) - min(blk[3]) for blk in SPHERE_WINDOWS)
        bias = sb("s_bias", [M, 1])
        norm = sb("s_norm", [P, B, 2])
        polar = sb("s_polar", [P, sum(len(blk[2]) for blk in SPHERE_POLAR), B, W + 1])
        raw = [sb(f"s_raw{s}", [P, WSPAN]) for s in range(B)]
        xn = [sb(f"s_xn{s}", [P, WSPAN]) for s in range(B)]
        xh = [sb(f"s_xh{s}", [P, WSPAN], BF16) for s in range(B)]
        xl = [sb(f"s_xl{s}", [P, WSPAN], BF16) for s in range(B)]
        res = [sb(f"s_res{s}", [M, W]) for s in range(B)]
        y = [sb(f"s_y{s}", [P, W]) for s in range(B)]
        acc = [ps(f"s_acc{s}", [P, W]) for s in range(B)]

        consts_in = sem("s_consts_in")
        raw_in = [sem(f"s_raw_in{s}") for s in range(B)]
        polar_in = sem("s_polar_in")
        res_in = [sem(f"s_res_in{s}") for s in range(B)]
        xn_done = [sem(f"s_xn_done{s}") for s in range(B)]
        xh_done = [sem(f"s_xh_done{s}") for s in range(B)]
        xl_done = [sem(f"s_xl_done{s}") for s in range(B)]
        acc_full = [sem(f"s_acc_full{s}") for s in range(B)]
        y_ready = [sem(f"s_y_ready{s}") for s in range(B)]
        y_stored = [sem(f"s_y_stored{s}") for s in range(B)]
        widened = sem("s_widened")
        NCONST = 2
        block = ctx.enter_context(nc.Block())

        def windows(engine):
            for first, count in SPHERE_RUNS:
                h0, n, r0, shifts, e0 = SPHERE_WINDOWS[first]
                if count == 1:
                    yield first, h0, n, r0, shifts, e0
                else:
                    with engine.Fori(0, count) as i:
                        yield i + first, i * OR + h0, n, i * OR + r0, shifts, i * len(shifts) + e0

        def polar_blocks():
            before = 0
            for m, (h0, n, tiles, e0) in enumerate(SPHERE_POLAR):
                yield len(SPHERE_WINDOWS) + m, h0, n, len(tiles), before, e0
                before += len(tiles)

        def polar_loads():
            t = 0
            for h0, n, tiles, e0 in SPHERE_POLAR:
                for slots in tiles:
                    slots = slots + [(0, h0)] * (KR - len(slots))
                    m = 0
                    while m < KR:
                        k = m + 1
                        while k < KR and slots[k] == (slots[m][0], slots[k - 1][1] + 1):
                            k += 1
                        yield t, m, k - m, slots[m][0], slots[m][1]
                        m = k
                    t += 1

        NW = len(SPHERE_WINDOWS)

        def span(shifts):
            a = min(shifts)
            return NEAR + a, W + max(shifts) - a

        @block.sync
        def _(sp):
            sp.dma_start(bias[:], T["b_sphere"].rearrange("(a c) n -> a c n", a=1).broadcast_to([OR, C, 1])).then_inc(consts_in, 16)
            sp.dma_start(norm[:], S).then_inc(consts_in, 16)

            def load_window(at, b, r0, shifts):
                c0, cols = span(shifts)
                sp.wait_ge(xn_done[b], at)
                sp.dma_start(raw[b][:, 0:cols], X1[b, bass.ds(r0, KR), :, c0:c0 + cols].rearrange("h c w -> (h c) w")
                             ).then_inc(raw_in[b], 16)

            def load_residual(at, b, h0, n):
                sp.wait_ge(y_ready[b], at)
                sp.dma_start(res[b][0:n * C], X1[b, bass.ds(h0, n), :, NEAR:NEAR + W].rearrange("h c w -> (h c) w")
                             ).then_inc(res_in[b], 16)

            for at, h0, n, r0, shifts, e0 in windows(sp):
                load_window(at, 0, r0, shifts)
                if used(at):
                    load_residual(at - 1, 1, h0 - OR, OR)
                load_window(at, 1, r0, shifts)
                load_residual(at, 0, h0, n)
            last = (NW - 1, SPHERE_WINDOWS[-1][0], OR)
            for at, h0, n, tiles, before, e0 in polar_blocks():
                load_residual(last[0], 1, *last[1:])
                load_residual(at, 0, h0, n)
                last = (at, h0, n)
            load_residual(last[0], 1, *last[1:])

        @block.gpsimd
        def _(pool):
            pieces = ((0, NEAR + W - PAD_L, PAD_L), (PAD_L, NEAR, W), (PAD_L + W, NEAR, PAD_R))
            for to_row, row, rows in ((0, 0, TOP), (TOP, F - BOTTOM, BOTTOM)):
                for to, frm, cols in pieces:
                    pool.dma_start(XP[:, to_row:to_row + rows, :, to:to + cols].rearrange("b h c w -> b (h c) w"),
                                 X1[:, row:row + rows, :, frm:frm + cols].rearrange("b h c w -> b (h c) w")).then_inc(widened, 16)
            pool.wait_ge(widened, 16 * 6)
            for t, m, k, s, r in polar_loads():
                r = r if r < TOP else r - (F - BOTTOM) + TOP
                pool.dma_start(polar[m * C:(m + k) * C, t], XP[:, r:r + k, :, PAD_L + s:PAD_L + s + W + 1].rearrange("b h c w -> (h c) b w")
                             ).then_inc(polar_in, 16)

        @block.scalar
        def _(act):
            act.wait_ge(consts_in, 16 * NCONST)
            def normalise(step, b, source, cols):
                act.wait_ge(xl_done[b], step)
                nc.scalar.activation(xn[b][:, 0:cols], source, ACT.Identity, bias=norm[:, b, 1:2],
                                     scale=norm[:, b, 0:1]).then_inc(xn_done[b], 1)
                act.wait_ge(xn_done[b], step + 1)
                act.wait_ge(acc_full[b], step)
                nc.scalar.activation(xh[b][:, 0:cols], xn[b][:, 0:cols], ACT.Copy).then_inc(xh_done[b], 1)

            def store(at, b, h0, n):
                act.wait_ge(y_ready[b], at + 1)
                act.dma_start(out[b, :, bass.ds(h0, n)].rearrange("c h w -> h c w"), y[b][0:n * C]).then_inc(y_stored[b], 16)

            for at, h0, n, r0, shifts, e0 in windows(act):
                cols = span(shifts)[1]
                for b in range(B):
                    act.wait_ge(raw_in[b], 16 * (at + 1))
                    normalise(at, b, raw[b][:, 0:cols], cols)
                    if used(at):
                        store(at - 1, b, h0 - OR, OR)
            last = (NW - 1, SPHERE_WINDOWS[-1][0], OR)
            act.wait_ge(polar_in, 16 * len(list(polar_loads())))
            for at, h0, n, tiles, before, e0 in polar_blocks():
                for t in range(before, before + tiles):
                    for b in range(B):
                        normalise(NW + t, b, polar[:, t, b, :], W + 1)
                        if t == before:
                            store(last[0], b, *last[1:])
                last = (at, h0, n)
            for b in range(B):
                store(last[0], b, *last[1:])
            for b in range(B):
                act.wait_ge(y_stored[b], 16 * BLOCKS)

        @block.vector
        def _(v):
            v.wait_ge(consts_in, 16 * NCONST)
            def low(step, b, cols):
                v.wait_ge(xh_done[b], step + 1)
                nc.vector.tensor_tensor(xl[b][:, 0:cols], xn[b][:, 0:cols], xh[b][:, 0:cols], ALU.subtract).then_inc(xl_done[b], 1)

            def finish(at, steps, b, n):
                v.wait_ge(acc_full[b], steps)
                v.wait_ge(res_in[b], 16 * (at + 1))
                v.wait_ge(y_stored[b], 16 * at)
                nc.vector.scalar_tensor_tensor(y[b][0:n * C], acc[b][0:n * C, :], bias[0:n * C], res[b][0:n * C],
                                               ALU.add, ALU.add).then_inc(y_ready[b], 1)

            for at, h0, n, r0, shifts, e0 in windows(v):
                low(at, 0, span(shifts)[1])
                if used(at):
                    finish(at - 1, at, 1, OR)
                low(at, 1, span(shifts)[1])
                finish(at, at + 1, 0, n)
            last = (NW - 1, NW, OR)
            for at, h0, n, tiles, before, e0 in polar_blocks():
                for t in range(before, before + tiles):
                    low(NW + t, 0, W + 1)
                    if t == before:
                        finish(last[0], last[1], 1, last[2])
                    low(NW + t, 1, W + 1)
                last = (at, NW + before + tiles, n)
                finish(at, last[1], 0, n)
            finish(last[0], last[1], 1, last[2])

        @block.tensor
        def _(pe):
            def products(b, e, columns, start, stop):
                hi = mat_h[:, bass.ds(e, 1), :].rearrange("p a m -> p (a m)")
                lo = mat_l[:, bass.ds(e, 1), :].rearrange("p a m -> p (a m)")
                nc.tensor.matmul(acc[b][0:M, :], hi, xh[b][:, columns:columns + W], start=start, stop=False)
                nc.tensor.matmul(acc[b][0:M, :], hi, xl[b][:, columns:columns + W], start=False, stop=False)
                return nc.tensor.matmul(acc[b][0:M, :], lo, xh[b][:, columns:columns + W], start=False, stop=stop)

            for at, h0, n, r0, shifts, e0 in windows(pe):
                for b in range(B):
                    pe.wait_ge(xl_done[b], at + 1)
                    pe.wait_ge(y_ready[b], at)
                    for j, s in enumerate(shifts):
                        last = products(b, e0 + j, s - min(shifts), j == 0, j == len(shifts) - 1)
                    last.then_inc(acc_full[b], 1)
            for at, h0, n, tiles, before, e0 in polar_blocks():
                for t in range(tiles):
                    for b in range(B):
                        pe.wait_ge(xl_done[b], NW + before + t + 1)
                        if t == 0:
                            pe.wait_ge(y_ready[b], at)
                        for d in range(2):
                            last = products(b, e0 + 2 * t + d, d, t == d == 0, t == tiles - 1 and d == 1)
                        last.then_inc(acc_full[b], 1)


def program(nc, T, out):
    def dram(name, shape, dt=FP32):
        return nc.dram_tensor(name, shape, dt).ap()

    Y = dram("Y", (B, YROWS, C, QKV))
    QK = dram("QK", (B, C, 2, 2, F, WPAD), BF16)
    V = dram("V", (B, C, WPAD, F))
    Z = dram("Z", (B, F, C, W))
    X1 = dram("X1", (B, F, C, NEAR + W + NEAR))
    XP = dram("XP", (B, TOP + BOTTOM, C, PAD_L + W + PAD_R))
    S = dram("S", (P, B, 2))
    with ExitStack() as ctx:
        sb, _, _ = allocators(nc, ctx)
        band = sb("band", [P, 3, C * OW])
        qk_bias = sb("qk_bias", [P, 2 * FH, C])
        v_bias = sb("v_bias", [C * OW, 1])
        project(nc, T, Y, band, qk_bias, v_bias)
        convolve(nc, T, Y, QK, V, band, qk_bias, v_bias)
    with ExitStack() as ctx:
        sb, _, _ = allocators(nc, ctx)
        wmix = sb("wmix", [P, P])
        bmix = sb("bmix", [P, 1])
        group = sb("group", [P, P])
        slot = sb("slot", [P, KR])
        side = sb("side", [P, CHUNKS * CHUNK * OR])
        centre = sb("centre", [P, CHUNKS * CHUNK * OR])
        w_side = sb("w_side", [P, C, C])
        w_centre = sb("w_centre", [P, C, C])
        mixing = wmix, bmix, group, slot, side, centre, w_side, w_centre
        attend(nc, T, QK, V, Z, mixing)
        mat_h, mat_l = (sb(f"sphere_mat_{part}", [P, CHUNKS * CHUNK, OR * C], BF16) for part in ("h", "l"))
        residual(nc, T, Z, X1, S, mixing, mat_h, mat_l)
        sphere(nc, T, X1, XP, S, mat_h, mat_l, out)


def kernel(**inputs):
    import concourse.bacc as bacc
    from concourse.bass_utils import run_bass_kernel_spmd as run

    a = {name: np.asarray(v) for name, v in inputs.items()}
    layer = lambda name: a["L0_conv_" + name]
    taps = np.stack([layer(n + "_conv_w")[:, :, 0, :] for n in "qkv"])
    taps = np.ascontiguousarray(taps.transpose(2, 0, 1, 3)[..., ::-1]).reshape(C, 3 * C, TAPS)
    arrays = {
        "x": a["x"],
        "w_qkv": np.concatenate([layer("W" + n).transpose(0, 2, 1) for n in "qkv"], 2),
        "b_qkv": np.concatenate([layer("b" + n) for n in "qkv"], 1),
        "taps": np.pad(taps, ((0, 0), (0, 0), (KW - TAPS, OW - 1))),
        "qkv_conv_b": np.stack([layer(n + "_conv_b") for n in "qkv"]),
        "w_o": layer("Wo").transpose(0, 2, 1),
        "b_o": layer("bo").reshape(C, FH, P).transpose(0, 2, 1),
        "w_mix": layer("o_conv_w")[:, :, 0, 0].T,
        "b_mix": layer("o_conv_b").reshape(C, 1),
        "w_sphere": a["L1_conv_weight"].transpose(3, 2, 0, 1),
        "b_sphere": a["L1_conv_bias"].reshape(C, 1),
        **constants(),
    }
    nc = bacc.Bacc("TRN2", target_bir_lowering=False, num_devices=1)
    T, ins = {}, {}
    for name, v in arrays.items():
        v = np.ascontiguousarray(v)
        ins["in_" + name] = v
        T[name] = nc.dram_tensor("in_" + name, v.shape, mybir.dt.from_np(v.dtype), kind="ExternalInput").ap()
    out = nc.dram_tensor("out", a["x"].shape, mybir.dt.from_np(a["x"].dtype), kind="ExternalOutput").ap()
    program(nc, T, out)
    return run(nc, [ins], core_ids=[0]).results[0]["out"]
```
